# Optimizing a Trainium2 kernel written in Bass

```python
import numpy as np
import jax
import jax.numpy as jnp

def _softmax(x, axis=-1):
    return jax.nn.softmax(x, axis=axis)

def _gelu(x):
    return jax.nn.gelu(x, approximate=True)

def _silu(x):
    return jax.nn.silu(x)

def _sigmoid(x):
    return jax.nn.sigmoid(x)

def _layernorm(x, axis=-1, eps=1e-05):
    m = jnp.mean(x, axis=axis, keepdims=True)
    v = jnp.var(x, axis=axis, keepdims=True)
    return (x - m) / jnp.sqrt(v + eps)

def _scatter_add(tgt, idx, src, axis=0):
    return tgt.at[idx].add(src)

def _segment_sum(src, seg, n):
    return jax.ops.segment_sum(src, seg, n)
kernel_name = 'mk_xattn_ffn_d4_seqx_r8_22310f'

def setup_inputs(seed: int=0):
    np.random.seed(seed)
    _w = jnp.asarray

    def _rec_inputs():
        import jax
        import jax.numpy as jnp
        _rk = jax.random.key(seed)
        x = 7.22e-05 + 1 * jax.random.normal(jax.random.fold_in(_rk, 1), (4, 512, 128), jnp.float32)
        _lenS = 512 - jax.random.randint(jax.random.fold_in(_rk, 7), (4,), 0, max(1, 512 // 4) + 1, jnp.int32)
        _lenS2 = 77 - jax.random.randint(jax.random.fold_in(_rk, 8), (4,), 0, max(1, 77 // 4) + 1, jnp.int32)
        _ctx_1024P = jax.random.normal(jax.random.fold_in(_rk, 11), (4, 16, 128), jnp.float32)
        _ctx_1024c = jax.random.dirichlet(jax.random.fold_in(_rk, 511), 0.3 * jnp.ones((16,), jnp.float32), (4, 77))
        _ctx_1024t = jnp.einsum('bsk,bkd->bsd', _ctx_1024c, _ctx_1024P)
        _ctx_1024t = _ctx_1024t * jax.lax.rsqrt(jnp.mean(jnp.square(_ctx_1024t)) + 1e-12) * 0.953939
        ctx_1024 = 4.13588e-05 + 0.999923 * (_ctx_1024t + 0.3 * jax.random.normal(jax.random.fold_in(_rk, 611), (4, 77, 128), jnp.float32))
        itok_BxS_0_255 = jax.random.randint(jax.random.fold_in(_rk, 15), (4, 512), 0, 32, jnp.int32)
        _validS = jnp.arange(512)[None, :] < _lenS[:, None]
        _validS2 = jnp.arange(77)[None, :] < _lenS2[:, None]
        _causal = jnp.tril(jnp.ones((512, 512), dtype=bool))
        mask_BxSxS2_if1 = jnp.where(jnp.ones((4, 512, 77), dtype=bool), 1, 0).astype(jnp.int32)
        mask_BxS2_bk0 = jnp.logical_not(jnp.broadcast_to(_validS2[:, :], (4, 77)))
        mask_SxS2_bk1 = jnp.broadcast_to(_validS2[0:1, :], (512, 77))
        return (x, ctx_1024, itok_BxS_0_255, mask_BxSxS2_if1, mask_BxS2_bk0, mask_SxS2_bk1)
    x, ctx_1024, itok_BxS_0_255, mask_BxSxS2_if1, mask_BxS2_bk0, mask_SxS2_bk1 = _rec_inputs()

    def _L0_xattn_setup():
        import jax, jax.numpy as jnp
        import numpy as np
        B, S, D, H = (4, 256, 128, 16)
        DK = D // H

        def _split_heads(x):
            b, s, _ = x.shape
            return x.reshape(b, s, H, DK).transpose(0, 2, 1, 3)
        key = jax.random.key(seed)
        ks = jax.random.split(key, 9)
        scale = 1.0 / np.sqrt(D)
        inp = {'query': jax.random.normal(ks[0], (B, S, D), jnp.float32), 'key': jax.random.normal(ks[1], (B, S, D), jnp.float32), 'value': jax.random.normal(ks[2], (B, S, D), jnp.float32), 'mask': jnp.ones((B, S, S), jnp.int32), 'Wq': jax.random.normal(ks[3], (D, D), jnp.float32) * scale, 'bq': jnp.zeros((D,), jnp.float32), 'Wk': jax.random.normal(ks[4], (D, D), jnp.float32) * scale, 'bk': jnp.zeros((D,), jnp.float32), 'Wv': jax.random.normal(ks[5], (D, D), jnp.float32) * scale, 'bv': jnp.zeros((D,), jnp.float32)}
        return inp
    _L0_xattn_all = _L0_xattn_setup()
    _L0_xattn_in = {k: v for k, v in _L0_xattn_all.items() if k in ('Wq', 'bq', 'Wk', 'bk', 'Wv', 'bv')}
    del _L0_xattn_all

    def _L0_ffn_setup():
        import jax, jax.numpy as jnp
        import numpy as np
        MICRO_BATCHES = 2
        TOP_K = 2
        LN_EPS = 1e-05
        B, S, D = (4, 512, 128)
        E = 8
        DFF = 4 * D

        def _layernorm(x, g, b):
            mu = jnp.mean(x, axis=-1, keepdims=True)
            var = jnp.mean(jnp.square(x - mu), axis=-1, keepdims=True)
            return (x - mu) * jax.lax.rsqrt(var + LN_EPS) * g + b
        key = jax.random.key(seed)
        ks = jax.random.split(key, 12)
        sd = 1.0 / np.sqrt(D)
        sf = 1.0 / np.sqrt(DFF)
        return {'x': jax.random.normal(ks[0], (B, S, D), dtype=jnp.float32), 'ln_g': jnp.ones((D,), jnp.float32), 'ln_b': jnp.zeros((D,), jnp.float32), 'attn_w': jax.random.normal(ks[1], (D, D), jnp.float32) * sd, 'attn_b': jnp.zeros((D,), jnp.float32), 'gate_w': jax.random.normal(ks[2], (D, E), jnp.float32) * sd, 'w1': jax.random.normal(ks[3], (E, D, DFF), jnp.float32) * sd, 'b1': jnp.zeros((E, DFF), jnp.float32), 'w2': jax.random.normal(ks[4], (E, DFF, D), jnp.float32) * sf, 'b2': jnp.zeros((E, D), jnp.float32), 'next_w': jax.random.normal(ks[5], (D, D), jnp.float32) * sd, 'next_b': jnp.zeros((D,), jnp.float32)}
    _L0_ffn_all = _L0_ffn_setup()
    _L0_ffn_in = {k: v for k, v in _L0_ffn_all.items() if k in ('ln_g', 'ln_b', 'attn_w', 'attn_b', 'gate_w', 'w1', 'b1', 'w2', 'b2', 'next_w', 'next_b')}
    del _L0_ffn_all

    def _L1_xattn_setup():
        import jax, jax.numpy as jnp
        import numpy as np
        B, T, D, H = (2, 256, 128, 32)
        NEG = -1000000000.0
        key = jax.random.key(seed)
        ks = jax.random.split(key, 8)
        q = jax.random.normal(ks[0], (B, T, D), jnp.float32)
        k = jax.random.normal(ks[1], (B, T, D), jnp.float32)
        v = jax.random.normal(ks[2], (B, T, D), jnp.float32)
        Wqkv = jax.random.normal(ks[3], (D, 3 * D), jnp.float32) * 0.02
        bqkv = jax.random.normal(ks[4], (3 * D,), jnp.float32) * 0.02
        Wo = jax.random.normal(ks[5], (D, D), jnp.float32) * 0.02
        bo = jax.random.normal(ks[6], (D,), jnp.float32) * 0.02
        key_padding_mask = jnp.zeros((B, T), bool).at[1, T - 128:].set(True)
        attn_mask = jnp.triu(jnp.ones((T, T), bool), k=1)
        return {'q': q, 'k': k, 'v': v, 'Wqkv': Wqkv, 'bqkv': bqkv, 'Wo': Wo, 'bo': bo, 'key_padding_mask': key_padding_mask, 'attn_mask': attn_mask, 'n_heads': H}
    _L1_xattn_all = _L1_xattn_setup()
    _L1_xattn_in = {k: v for k, v in _L1_xattn_all.items() if k in ('Wqkv', 'bqkv', 'Wo', 'bo')}
    del _L1_xattn_all

    def _L1_ffn_setup():
        import jax, jax.numpy as jnp
        import numpy as np
        NUM_EXPERTS = 8
        TOP_K = 2
        CAPACITY_FACTOR = 1.25
        key = jax.random.key(seed)
        ks = jax.random.split(key, 5)
        B, S, D, H, E = (4, 256, 128, 256, NUM_EXPERTS)
        scale = 0.02
        return {'x': jax.random.normal(ks[0], (B, S, D), dtype=jnp.float32), 'gate_w': jax.random.normal(ks[1], (E, D), dtype=jnp.float32) * scale, 'gate_proj_w': jax.random.normal(ks[2], (E, H, D), dtype=jnp.float32) * scale, 'up_proj_w': jax.random.normal(ks[3], (E, H, D), dtype=jnp.float32) * scale, 'down_proj_w': jax.random.normal(ks[4], (E, D, H), dtype=jnp.float32) * scale}
    _L1_ffn_all = _L1_ffn_setup()
    _L1_ffn_in = {k: v for k, v in _L1_ffn_all.items() if k in ('gate_w', 'gate_proj_w', 'up_proj_w', 'down_proj_w')}
    del _L1_ffn_all

    def _L2_xattn_setup():
        import math
        import jax, jax.numpy as jnp
        import numpy as np
        D_MODEL = 128
        N_HEADS = 16
        D_K = D_MODEL // N_HEADS

        def _alibi_slopes(n_heads):
            power = 2 ** math.ceil(math.log2(n_heads))
            slopes = np.array([2.0 ** (-8 + i) for i in range(power)], dtype=np.float32)
            if n_heads != power:
                ratio = power // n_heads
                slopes = slopes[np.arange(0, power, ratio)][:n_heads]
            return jnp.asarray(slopes)
        key = jax.random.key(seed)
        ks = jax.random.split(key, 11)
        B, S, D = (2, 256, D_MODEL)
        w = 0.02
        return {'query': jax.random.normal(ks[0], (B, S, D), jnp.float32), 'key': jax.random.normal(ks[1], (B, S, D), jnp.float32), 'value': jax.random.normal(ks[2], (B, S, D), jnp.float32), 'Wq': jax.random.normal(ks[3], (D, D), jnp.float32) * w, 'bq': jax.random.normal(ks[4], (D,), jnp.float32) * w, 'Wk': jax.random.normal(ks[5], (D, D), jnp.float32) * w, 'bk': jax.random.normal(ks[6], (D,), jnp.float32) * w, 'Wv': jax.random.normal(ks[7], (D, D), jnp.float32) * w, 'bv': jax.random.normal(ks[8], (D,), jnp.float32) * w, 'Wo': jax.random.normal(ks[9], (D, D), jnp.float32) * w, 'bo': jax.random.normal(ks[10], (D,), jnp.float32) * w}
    _L2_xattn_all = _L2_xattn_setup()
    _L2_xattn_in = {k: v for k, v in _L2_xattn_all.items() if k in ('Wq', 'bq', 'Wk', 'bk', 'Wv', 'bv', 'Wo', 'bo')}
    del _L2_xattn_all

    def _L2_ffn_setup():
        import jax, jax.numpy as jnp
        import numpy as np
        B, S, IN, OUT = (4, 1024, 128, 128)
        EPS = 1e-06

        def _xla_quantized_matmul(x2d, weight_q, weight_scale):
            amax = jnp.max(jnp.abs(x2d), axis=-1, keepdims=True)
            x_scale = jnp.maximum(amax, EPS) / 127.0
            x_q = jnp.clip(jnp.round(x2d / x_scale), -128, 127).astype(jnp.int8)
            acc = jax.lax.dot_general(x_q, weight_q, (((1,), (1,)), ((), ())), preferred_element_type=jnp.int32)
            return acc.astype(jnp.float32) * x_scale * weight_scale[None, :]
        key = jax.random.key(seed)
        k1, k2, k3, k4 = jax.random.split(key, 4)
        x = jax.random.normal(k1, (B, S, IN), dtype=jnp.float32)
        weight_q = jax.random.randint(k2, (OUT, IN), -128, 128, dtype=jnp.int32).astype(jnp.int8)
        weight_scale = jax.random.uniform(k3, (OUT,), dtype=jnp.float32, minval=0.001, maxval=0.01)
        bias = jax.random.normal(k4, (OUT,), dtype=jnp.float32) * 0.01
        return {'x': x, 'weight_q': weight_q, 'weight_scale': weight_scale, 'bias': bias}
    _L2_ffn_all = _L2_ffn_setup()
    _L2_ffn_in = {k: v for k, v in _L2_ffn_all.items() if k in ('weight_q', 'weight_scale', 'bias')}
    del _L2_ffn_all

    def _L3_xattn_setup():
        import jax, jax.numpy as jnp
        import numpy as np
        N_LAYERS = 4
        H = 16
        LOOKBACK = 128
        EPS = 1e-06
        ROPE_BASE = 10000.0
        NEG = jnp.float32(-1e+30)

        def rmsnorm(x, w):
            return x * jax.lax.rsqrt(jnp.mean(x * x, axis=-1, keepdims=True) + EPS) * w

        def rope_cache(L, hd):
            inv = 1.0 / ROPE_BASE ** (jnp.arange(0, hd, 2, dtype=jnp.float32) / hd)
            t = jnp.arange(L, dtype=jnp.float32)
            f = t[:, None] * inv[None, :]
            emb = jnp.concatenate([f, f], axis=-1)
            return (jnp.cos(emb), jnp.sin(emb))

        def apply_rope(x, cos, sin):
            d = x.shape[-1]
            x1, x2 = (x[..., :d // 2], x[..., d // 2:])
            rot = jnp.concatenate([-x2, x1], axis=-1)
            return x * cos + rot * sin

        def split_heads(x, n_heads):
            B, L, D = x.shape
            return x.reshape(B, L, n_heads, D // n_heads).transpose(0, 2, 1, 3)

        def merge_heads(x):
            B, h, L, d = x.shape
            return x.transpose(0, 2, 1, 3).reshape(B, L, h * d)

        def sdpa(q, k, v, bias):
            scale = q.shape[-1] ** (-0.5)
            s = jnp.einsum('bhqd,bhkd->bhqk', q, k) * scale + bias
            p = jax.nn.softmax(s, axis=-1)
            return jnp.einsum('bhqk,bhkd->bhqd', p, v)

        def forward(x, memory, seg_ids, Wqkv, bqkv, Wo, bo, Wq_c, Wkv_c, Wo_c, Wg, Wu, Wd, n1, n2, n3, nf):
            B, L, D = x.shape
            S = memory.shape[1]
            hd = D // H
            cos, sin = rope_cache(L, hd)
            i = jnp.arange(L)
            causal_bias = jnp.where(i[None, :] <= i[:, None], 0.0, NEG)[None, None]
            j = jnp.arange(S)
            allowed = (j[None, None, :] <= seg_ids[:, :, None]) & (j[None, None, :] > seg_ids[:, :, None] - LOOKBACK)
            cross_bias = jnp.where(allowed, 0.0, NEG)[:, None]
            for l in range(N_LAYERS):
                h = rmsnorm(x, n1[l])
                qkv = h @ Wqkv[l].T + bqkv[l]
                q, k, v = jnp.split(qkv, 3, axis=-1)
                q = apply_rope(split_heads(q, H), cos, sin)
                k = apply_rope(split_heads(k, H), cos, sin)
                v = split_heads(v, H)
                o = merge_heads(sdpa(q, k, v, causal_bias)) @ Wo[l].T + bo[l]
                x = x + o
                h2 = rmsnorm(x, n2[l])
                qc = split_heads(h2 @ Wq_c[l].T, H)
                kv = memory @ Wkv_c[l].T
                kc, vc = jnp.split(kv, 2, axis=-1)
                kc, vc = (split_heads(kc, H), split_heads(vc, H))
                oc = merge_heads(sdpa(qc, kc, vc, cross_bias)) @ Wo_c[l].T
                x = x + oc
                h3 = rmsnorm(x, n3[l])
                x = x + jax.nn.silu(h3 @ Wg[l].T) * (h3 @ Wu[l].T) @ Wd[l].T
            return rmsnorm(x, nf)
        key = jax.random.key(seed)
        ks = jax.random.split(key, 16)
        B, L, S, D, F = (2, 256, 32, 128, 512)
        w = 0.02
        inp = {'x': jax.random.normal(ks[0], (B, L, D), jnp.float32), 'memory': jax.random.normal(ks[1], (B, S, D), jnp.float32), 'seg_ids': jnp.sort(jax.random.randint(ks[2], (B, L), 0, S), axis=-1), 'Wqkv': jax.random.normal(ks[3], (N_LAYERS, 3 * D, D), jnp.float32) * w, 'bqkv': jnp.zeros((N_LAYERS, 3 * D), jnp.float32), 'Wo': jax.random.normal(ks[4], (N_LAYERS, D, D), jnp.float32) * w, 'bo': jnp.zeros((N_LAYERS, D), jnp.float32), 'Wq_c': jax.random.normal(ks[5], (N_LAYERS, D, D), jnp.float32) * w, 'Wkv_c': jax.random.normal(ks[6], (N_LAYERS, 2 * D, D), jnp.float32) * w, 'Wo_c': jax.random.normal(ks[7], (N_LAYERS, D, D), jnp.float32) * w, 'Wg': jax.random.normal(ks[8], (N_LAYERS, F, D), jnp.float32) * w, 'Wu': jax.random.normal(ks[9], (N_LAYERS, F, D), jnp.float32) * w, 'Wd': jax.random.normal(ks[10], (N_LAYERS, D, F), jnp.float32) * w, 'n1': jnp.ones((N_LAYERS, D), jnp.float32), 'n2': jnp.ones((N_LAYERS, D), jnp.float32), 'n3': jnp.ones((N_LAYERS, D), jnp.float32), 'nf': jnp.ones((D,), jnp.float32)}
        return inp
    _L3_xattn_all = _L3_xattn_setup()
    _L3_xattn_in = {k: v for k, v in _L3_xattn_all.items() if k in ('Wqkv', 'bqkv', 'Wo', 'bo', 'Wq_c', 'Wkv_c', 'Wo_c', 'Wg', 'Wu', 'Wd', 'n1', 'n2', 'n3', 'nf')}
    del _L3_xattn_all

    def _L3_ffn_setup():
        import jax, jax.numpy as jnp
        import numpy as np
        B, S, H, E = (4, 256, 128, 8)
        key = jax.random.key(seed)
        k1, k2, k3 = jax.random.split(key, 3)
        scale_w = 1.0 / np.sqrt(H)
        return {'x': jax.random.normal(k1, (B, S, H), dtype=jnp.float32), 'router_w': jax.random.normal(k2, (H, E), dtype=jnp.float32) * scale_w, 'router_b': jnp.zeros((E,), dtype=jnp.float32), 'expert_w': jax.random.normal(k3, (E, H, H), dtype=jnp.float32) * scale_w, 'expert_b': jnp.zeros((E, H), dtype=jnp.float32)}
    _L3_ffn_all = _L3_ffn_setup()
    _L3_ffn_in = {k: v for k, v in _L3_ffn_all.items() if k in ('router_w', 'router_b', 'expert_w', 'expert_b')}
    del _L3_ffn_all
    return {'x': x, 'ctx_1024': ctx_1024, 'itok_BxS_0_255': itok_BxS_0_255, 'mask_BxSxS2_if1': mask_BxSxS2_if1, 'mask_BxS2_bk0': mask_BxS2_bk0, 'mask_SxS2_bk1': mask_SxS2_bk1, 'L0_xattn_Wq': _L0_xattn_in['Wq'], 'L0_xattn_bq': _L0_xattn_in['bq'], 'L0_xattn_Wk': _L0_xattn_in['Wk'], 'L0_xattn_bk': _L0_xattn_in['bk'], 'L0_xattn_Wv': _L0_xattn_in['Wv'], 'L0_xattn_bv': _L0_xattn_in['bv'], 'L0_ffn_ln_g': _L0_ffn_in['ln_g'], 'L0_ffn_ln_b': _L0_ffn_in['ln_b'], 'L0_ffn_attn_w': _L0_ffn_in['attn_w'], 'L0_ffn_attn_b': _L0_ffn_in['attn_b'], 'L0_ffn_gate_w': _L0_ffn_in['gate_w'], 'L0_ffn_w1': _L0_ffn_in['w1'], 'L0_ffn_b1': _L0_ffn_in['b1'], 'L0_ffn_w2': _L0_ffn_in['w2'], 'L0_ffn_b2': _L0_ffn_in['b2'], 'L0_ffn_next_w': _L0_ffn_in['next_w'], 'L0_ffn_next_b': _L0_ffn_in['next_b'], 'L1_xattn_Wqkv': _L1_xattn_in['Wqkv'], 'L1_xattn_bqkv': _L1_xattn_in['bqkv'], 'L1_xattn_Wo': _L1_xattn_in['Wo'], 'L1_xattn_bo': _L1_xattn_in['bo'], 'L1_ffn_gate_w': _L1_ffn_in['gate_w'], 'L1_ffn_gate_proj_w': _L1_ffn_in['gate_proj_w'], 'L1_ffn_up_proj_w': _L1_ffn_in['up_proj_w'], 'L1_ffn_down_proj_w': _L1_ffn_in['down_proj_w'], 'L2_xattn_Wq': _L2_xattn_in['Wq'], 'L2_xattn_bq': _L2_xattn_in['bq'], 'L2_xattn_Wk': _L2_xattn_in['Wk'], 'L2_xattn_bk': _L2_xattn_in['bk'], 'L2_xattn_Wv': _L2_xattn_in['Wv'], 'L2_xattn_bv': _L2_xattn_in['bv'], 'L2_xattn_Wo': _L2_xattn_in['Wo'], 'L2_xattn_bo': _L2_xattn_in['bo'], 'L2_ffn_weight_q': _L2_ffn_in['weight_q'], 'L2_ffn_weight_scale': _L2_ffn_in['weight_scale'], 'L2_ffn_bias': _L2_ffn_in['bias'], 'L3_xattn_Wqkv': _L3_xattn_in['Wqkv'], 'L3_xattn_bqkv': _L3_xattn_in['bqkv'], 'L3_xattn_Wo': _L3_xattn_in['Wo'], 'L3_xattn_bo': _L3_xattn_in['bo'], 'L3_xattn_Wq_c': _L3_xattn_in['Wq_c'], 'L3_xattn_Wkv_c': _L3_xattn_in['Wkv_c'], 'L3_xattn_Wo_c': _L3_xattn_in['Wo_c'], 'L3_xattn_Wg': _L3_xattn_in['Wg'], 'L3_xattn_Wu': _L3_xattn_in['Wu'], 'L3_xattn_Wd': _L3_xattn_in['Wd'], 'L3_xattn_n1': _L3_xattn_in['n1'], 'L3_xattn_n2': _L3_xattn_in['n2'], 'L3_xattn_n3': _L3_xattn_in['n3'], 'L3_xattn_nf': _L3_xattn_in['nf'], 'L3_ffn_router_w': _L3_ffn_in['router_w'], 'L3_ffn_router_b': _L3_ffn_in['router_b'], 'L3_ffn_expert_w': _L3_ffn_in['expert_w'], 'L3_ffn_expert_b': _L3_ffn_in['expert_b']}

def reference(x, ctx_1024, itok_BxS_0_255, mask_BxSxS2_if1, mask_BxS2_bk0, mask_SxS2_bk1, L0_xattn_Wq, L0_xattn_bq, L0_xattn_Wk, L0_xattn_bk, L0_xattn_Wv, L0_xattn_bv, L0_ffn_ln_g, L0_ffn_ln_b, L0_ffn_attn_w, L0_ffn_attn_b, L0_ffn_gate_w, L0_ffn_w1, L0_ffn_b1, L0_ffn_w2, L0_ffn_b2, L0_ffn_next_w, L0_ffn_next_b, L1_xattn_Wqkv, L1_xattn_bqkv, L1_xattn_Wo, L1_xattn_bo, L1_ffn_gate_w, L1_ffn_gate_proj_w, L1_ffn_up_proj_w, L1_ffn_down_proj_w, L2_xattn_Wq, L2_xattn_bq, L2_xattn_Wk, L2_xattn_bk, L2_xattn_Wv, L2_xattn_bv, L2_xattn_Wo, L2_xattn_bo, L2_ffn_weight_q, L2_ffn_weight_scale, L2_ffn_bias, L3_xattn_Wqkv, L3_xattn_bqkv, L3_xattn_Wo, L3_xattn_bo, L3_xattn_Wq_c, L3_xattn_Wkv_c, L3_xattn_Wo_c, L3_xattn_Wg, L3_xattn_Wu, L3_xattn_Wd, L3_xattn_n1, L3_xattn_n2, L3_xattn_n3, L3_xattn_nf, L3_ffn_router_w, L3_ffn_router_b, L3_ffn_expert_w, L3_ffn_expert_b):
    import jax
    import jax.numpy as jnp

    def _L0_xattn_ref(query, key, value, mask, Wq, bq, Wk, bk, Wv, bv):
        import jax, jax.numpy as jnp
        import numpy as np
        B, S, D, H = (4, 256, 128, 16)
        DK = D // H

        def _split_heads(x):
            b, s, _ = x.shape
            return x.reshape(b, s, H, DK).transpose(0, 2, 1, 3)
        q = _split_heads(query @ Wq.T + bq)
        k = _split_heads(key @ Wk.T + bk)
        v = _split_heads(value @ Wv.T + bv)
        scores = jnp.einsum('bhqd,bhkd->bhqk', q, k) / np.sqrt(DK).astype(jnp.float32)
        scores = jnp.where(mask[:, None, :, :] == 0, jnp.float32(-1000000000.0), scores)
        p_attn = jax.nn.softmax(scores, axis=-1)
        x = jnp.einsum('bhqk,bhkd->bhqd', p_attn, v)
        return x.transpose(0, 2, 1, 3).reshape(query.shape[0], -1, H * DK)

    def _L0_ffn_ref(x, ln_g, ln_b, attn_w, attn_b, gate_w, w1, b1, w2, b2, next_w, next_b):
        import jax, jax.numpy as jnp
        import numpy as np
        MICRO_BATCHES = 2
        TOP_K = 2
        LN_EPS = 1e-05
        B, S, D = (4, 512, 128)
        E = 8
        DFF = 4 * D

        def _layernorm(x, g, b):
            mu = jnp.mean(x, axis=-1, keepdims=True)
            var = jnp.mean(jnp.square(x - mu), axis=-1, keepdims=True)
            return (x - mu) * jax.lax.rsqrt(var + LN_EPS) * g + b
        Bx, Sx, Dx = x.shape
        N = Bx * Sx
        x_flat = x.reshape(N, Dx)
        x_attn = _layernorm(x_flat, ln_g, ln_b) @ attn_w + attn_b + x_flat
        logits = x_attn @ gate_w
        _ = jax.lax.top_k(logits, TOP_K)
        tpe = N // (MICRO_BATCHES * E)
        g = x_attn.reshape(MICRO_BATCHES, E, tpe, Dx)
        h = jax.nn.gelu(jnp.einsum('metd,edf->metf', g, w1) + b1[None, :, None, :], approximate=False)
        y = jnp.einsum('metf,efd->metd', h, w2) + b2[None, :, None, :]
        out = jax.nn.gelu(y @ next_w + next_b, approximate=False)
        return out.reshape(Bx, Sx, Dx)

    def _L1_xattn_ref(q, k, v, Wqkv, bqkv, Wo, bo, key_padding_mask, attn_mask, n_heads):
        import jax, jax.numpy as jnp
        import numpy as np
        B, T, D, H = (2, 256, 128, 32)
        NEG = -1000000000.0
        Bq, T1, Dm = q.shape
        T2 = k.shape[1]
        dh = Dm // n_heads
        x = jnp.concatenate([q, k, v], axis=1)
        proj = x @ Wqkv + bqkv
        proj = proj.reshape(Bq, -1, 3, n_heads, dh)
        qp = proj[:, :T1, 0]
        kp = proj[:, T1:T1 + T2, 1]
        vp = proj[:, T1 + T2:, 2]
        scores = jnp.einsum('bqhd,bkhd->bhqk', qp, kp) / np.sqrt(dh).astype(qp.dtype)
        mask = key_padding_mask[:, None, None, :] | attn_mask[None, None, :, :]
        scores = jnp.where(mask, NEG, scores)
        attn = jax.nn.softmax(scores, axis=-1)
        y = jnp.einsum('bhqk,bkhd->bqhd', attn, vp)
        y = y.reshape(Bq, T1, Dm)
        return y @ Wo + bo

    def _L1_ffn_ref(x, gate_w, gate_proj_w, up_proj_w, down_proj_w):
        import jax, jax.numpy as jnp
        import numpy as np
        NUM_EXPERTS = 8
        TOP_K = 2
        CAPACITY_FACTOR = 1.25
        B, S, D = x.shape
        E, K = (NUM_EXPERTS, TOP_K)
        T = B * S
        xf = x.reshape(T, D)
        logits = xf @ gate_w.T
        probs = jax.nn.softmax(logits, axis=-1)
        top_p, top_i = jax.lax.top_k(probs, K)
        w = top_p / (jnp.sum(top_p, axis=-1, keepdims=True) + 1e-09)
        capacity = int(CAPACITY_FACTOR * T / E)
        oh = jax.nn.one_hot(top_i, E, dtype=jnp.int32)
        rank = jnp.cumsum(oh, axis=0) - 1
        my_rank = jnp.sum(rank * oh, axis=-1)
        keep = (my_rank < capacity).astype(w.dtype)
        comb = jnp.einsum('tk,tke->te', w * keep, oh.astype(w.dtype))
        out = jnp.zeros_like(xf)
        for e in range(E):
            g = jax.nn.silu(xf @ gate_proj_w[e].T)
            u = xf @ up_proj_w[e].T
            y = g * u @ down_proj_w[e].T
            out = out + comb[:, e:e + 1] * y
        return out.reshape(B, S, D)

    def _L2_xattn_ref(query, key, value, Wq, bq, Wk, bk, Wv, bv, Wo, bo):
        import math
        import jax, jax.numpy as jnp
        import numpy as np
        D_MODEL = 128
        N_HEADS = 16
        D_K = D_MODEL // N_HEADS

        def _alibi_slopes(n_heads):
            power = 2 ** math.ceil(math.log2(n_heads))
            slopes = np.array([2.0 ** (-8 + i) for i in range(power)], dtype=np.float32)
            if n_heads != power:
                ratio = power // n_heads
                slopes = slopes[np.arange(0, power, ratio)][:n_heads]
            return jnp.asarray(slopes)
        B, Sq, D = query.shape
        Sk = key.shape[1]
        H, dk = (N_HEADS, D_K)
        q = (query @ Wq.T + bq).reshape(B, Sq, H, dk).transpose(0, 2, 1, 3)
        k = (key @ Wk.T + bk).reshape(B, Sk, H, dk).transpose(0, 2, 1, 3)
        v = (value @ Wv.T + bv).reshape(B, Sk, H, dk).transpose(0, 2, 1, 3)
        scores = jnp.einsum('bhqd,bhkd->bhqk', q, k) / jnp.sqrt(jnp.float32(dk))
        dist = (jnp.arange(Sq)[:, None] - jnp.arange(Sk)[None, :]).astype(scores.dtype)
        slopes = _alibi_slopes(H)
        scores = scores + slopes[None, :, None, None] * dist[None, None, :, :]
        attn = jax.nn.softmax(scores, axis=-1)
        out = jnp.einsum('bhqk,bhkd->bhqd', attn, v)
        out = out.transpose(0, 2, 1, 3).reshape(B, Sq, D)
        return out @ Wo.T + bo

    def _L2_ffn_ref(x, weight_q, weight_scale, bias):
        import jax, jax.numpy as jnp
        import numpy as np
        B, S, IN, OUT = (4, 1024, 128, 128)
        EPS = 1e-06

        def _xla_quantized_matmul(x2d, weight_q, weight_scale):
            amax = jnp.max(jnp.abs(x2d), axis=-1, keepdims=True)
            x_scale = jnp.maximum(amax, EPS) / 127.0
            x_q = jnp.clip(jnp.round(x2d / x_scale), -128, 127).astype(jnp.int8)
            acc = jax.lax.dot_general(x_q, weight_q, (((1,), (1,)), ((), ())), preferred_element_type=jnp.int32)
            return acc.astype(jnp.float32) * x_scale * weight_scale[None, :]
        orig_shape = x.shape
        x2d = x.reshape(-1, orig_shape[-1])
        out = _xla_quantized_matmul(x2d, weight_q, weight_scale)
        out = out.reshape(*orig_shape[:-1], out.shape[-1])
        out = out + bias
        return out

    def _L3_xattn_ref(x, memory, seg_ids, Wqkv, bqkv, Wo, bo, Wq_c, Wkv_c, Wo_c, Wg, Wu, Wd, n1, n2, n3, nf):
        import jax, jax.numpy as jnp
        import numpy as np
        N_LAYERS = 4
        H = 16
        LOOKBACK = 128
        EPS = 1e-06
        ROPE_BASE = 10000.0
        NEG = jnp.float32(-1e+30)

        def rmsnorm(x, w):
            return x * jax.lax.rsqrt(jnp.mean(x * x, axis=-1, keepdims=True) + EPS) * w

        def rope_cache(L, hd):
            inv = 1.0 / ROPE_BASE ** (jnp.arange(0, hd, 2, dtype=jnp.float32) / hd)
            t = jnp.arange(L, dtype=jnp.float32)
            f = t[:, None] * inv[None, :]
            emb = jnp.concatenate([f, f], axis=-1)
            return (jnp.cos(emb), jnp.sin(emb))

        def apply_rope(x, cos, sin):
            d = x.shape[-1]
            x1, x2 = (x[..., :d // 2], x[..., d // 2:])
            rot = jnp.concatenate([-x2, x1], axis=-1)
            return x * cos + rot * sin

        def split_heads(x, n_heads):
            B, L, D = x.shape
            return x.reshape(B, L, n_heads, D // n_heads).transpose(0, 2, 1, 3)

        def merge_heads(x):
            B, h, L, d = x.shape
            return x.transpose(0, 2, 1, 3).reshape(B, L, h * d)

        def sdpa(q, k, v, bias):
            scale = q.shape[-1] ** (-0.5)
            s = jnp.einsum('bhqd,bhkd->bhqk', q, k) * scale + bias
            p = jax.nn.softmax(s, axis=-1)
            return jnp.einsum('bhqk,bhkd->bhqd', p, v)

        def forward(x, memory, seg_ids, Wqkv, bqkv, Wo, bo, Wq_c, Wkv_c, Wo_c, Wg, Wu, Wd, n1, n2, n3, nf):
            B, L, D = x.shape
            S = memory.shape[1]
            hd = D // H
            cos, sin = rope_cache(L, hd)
            i = jnp.arange(L)
            causal_bias = jnp.where(i[None, :] <= i[:, None], 0.0, NEG)[None, None]
            j = jnp.arange(S)
            allowed = (j[None, None, :] <= seg_ids[:, :, None]) & (j[None, None, :] > seg_ids[:, :, None] - LOOKBACK)
            cross_bias = jnp.where(allowed, 0.0, NEG)[:, None]
            for l in range(N_LAYERS):
                h = rmsnorm(x, n1[l])
                qkv = h @ Wqkv[l].T + bqkv[l]
                q, k, v = jnp.split(qkv, 3, axis=-1)
                q = apply_rope(split_heads(q, H), cos, sin)
                k = apply_rope(split_heads(k, H), cos, sin)
                v = split_heads(v, H)
                o = merge_heads(sdpa(q, k, v, causal_bias)) @ Wo[l].T + bo[l]
                x = x + o
                h2 = rmsnorm(x, n2[l])
                qc = split_heads(h2 @ Wq_c[l].T, H)
                kv = memory @ Wkv_c[l].T
                kc, vc = jnp.split(kv, 2, axis=-1)
                kc, vc = (split_heads(kc, H), split_heads(vc, H))
                oc = merge_heads(sdpa(qc, kc, vc, cross_bias)) @ Wo_c[l].T
                x = x + oc
                h3 = rmsnorm(x, n3[l])
                x = x + jax.nn.silu(h3 @ Wg[l].T) * (h3 @ Wu[l].T) @ Wd[l].T
            return rmsnorm(x, nf)
        return forward(x, memory, seg_ids, Wqkv, bqkv, Wo, bo, Wq_c, Wkv_c, Wo_c, Wg, Wu, Wd, n1, n2, n3, nf)

    def _L3_ffn_ref(x, router_w, router_b, expert_w, expert_b):
        import jax, jax.numpy as jnp
        import numpy as np
        B, S, H, E = (4, 256, 128, 8)
        b, s, h = x.shape
        xt = x.reshape(b * s, h)
        logits = xt @ router_w + router_b
        probs = jax.nn.softmax(logits, axis=-1)
        gate = jnp.max(probs, axis=-1)
        idx = jnp.argmax(probs, axis=-1)
        out_all = jnp.einsum('th,ehd->ted', xt, expert_w) + expert_b[None, :, :]
        e_out = jnp.take_along_axis(out_all, idx[:, None, None], axis=1)[:, 0, :]
        y = gate[:, None] * e_out
        return y.reshape(b, s, h)
    x = x + _L0_xattn_ref(_layernorm(x, axis=-1), ctx_1024, ctx_1024, mask_BxSxS2_if1, L0_xattn_Wq, L0_xattn_bq, L0_xattn_Wk, L0_xattn_bk, L0_xattn_Wv, L0_xattn_bv)
    x = x + _L0_ffn_ref(_layernorm(x, axis=-1), L0_ffn_ln_g, L0_ffn_ln_b, L0_ffn_attn_w, L0_ffn_attn_b, L0_ffn_gate_w, L0_ffn_w1, L0_ffn_b1, L0_ffn_w2, L0_ffn_b2, L0_ffn_next_w, L0_ffn_next_b)
    x = x + _L1_xattn_ref(_layernorm(x, axis=-1), ctx_1024, ctx_1024, L1_xattn_Wqkv, L1_xattn_bqkv, L1_xattn_Wo, L1_xattn_bo, mask_BxS2_bk0, mask_SxS2_bk1, 32)
    x = x + _L1_ffn_ref(_layernorm(x, axis=-1), L1_ffn_gate_w, L1_ffn_gate_proj_w, L1_ffn_up_proj_w, L1_ffn_down_proj_w)
    x = x + _L2_xattn_ref(_layernorm(x, axis=-1), ctx_1024, ctx_1024, L2_xattn_Wq, L2_xattn_bq, L2_xattn_Wk, L2_xattn_bk, L2_xattn_Wv, L2_xattn_bv, L2_xattn_Wo, L2_xattn_bo)
    x = x + _L2_ffn_ref(_layernorm(x, axis=-1), L2_ffn_weight_q, L2_ffn_weight_scale, L2_ffn_bias)
    x = x + _L3_xattn_ref(_layernorm(x, axis=-1), ctx_1024, itok_BxS_0_255, L3_xattn_Wqkv, L3_xattn_bqkv, L3_xattn_Wo, L3_xattn_bo, L3_xattn_Wq_c, L3_xattn_Wkv_c, L3_xattn_Wo_c, L3_xattn_Wg, L3_xattn_Wu, L3_xattn_Wd, L3_xattn_n1, L3_xattn_n2, L3_xattn_n3, L3_xattn_nf)
    x = x + _L3_ffn_ref(_layernorm(x, axis=-1), L3_ffn_router_w, L3_ffn_router_b, L3_ffn_expert_w, L3_ffn_expert_b)
    return x

_drawn_inputs = setup_inputs


def setup_inputs(seed=0):
    import zlib

    import numpy as np

    out = dict(_drawn_inputs(seed))
    spreads = {'L0_xattn_bq': (0.0, 0.286),
     'L0_xattn_bk': (0.0, 2.0),
     'L0_xattn_bv': (0.0, 0.1),
     'L0_ffn_ln_g': (1.0, 0.2),
     'L0_ffn_ln_b': (0.0, 0.1),
     'L0_ffn_attn_b': (0.0, 0.1),
     'L0_ffn_b1': (0.0, 0.1),
     'L0_ffn_b2': (0.0, 0.1),
     'L0_ffn_next_b': (0.0, 0.1),
     'L3_xattn_bqkv': (0.0, 0.8),
     'L3_xattn_bo': (0.0, 0.274),
     'L3_xattn_n1': (1.0, 0.6),
     'L3_xattn_n2': (1.0, 0.6),
     'L3_xattn_n3': (1.0, 0.6),
     'L3_xattn_nf': (1.0, 0.2),
     'L3_ffn_router_b': (0.0, 0.488),
     'L3_ffn_expert_b': (0.0, 0.8)}
    factors = {'L1_xattn_bqkv': 7.822,
     'L1_xattn_bo': 3.03,
     'L1_ffn_gate_w': 7.642,
     'L1_ffn_gate_proj_w': 7.136,
     'L1_ffn_up_proj_w': 7.107,
     'L1_ffn_down_proj_w': 7.239,
     'L2_xattn_Wq': 27.773,
     'L2_xattn_bq': 200.0,
     'L2_xattn_Wk': 27.177,
     'L2_xattn_bk': 200.0,
     'L2_xattn_bv': 21.829,
     'L2_xattn_bo': 2.886,
     'L2_ffn_bias': 23.529,
     'L3_xattn_Wqkv': 6.557,
     'L3_xattn_Wo': 5.043,
     'L3_xattn_Wq_c': 8.0,
     'L3_xattn_Wkv_c': 5.726,
     'L3_xattn_Wo_c': 5.821,
     'L3_xattn_Wg': 8.0,
     'L3_xattn_Wu': 8.0,
     'L3_xattn_Wd': 8.0}
    for name, (base, spread) in spreads.items():
        noise = np.random.default_rng([zlib.crc32(name.encode()), seed]).standard_normal(out[name].shape)
        drawn = base * np.exp(spread * noise) if base else spread * noise
        out[name] = jnp.asarray(drawn.astype(out[name].dtype))
    for name, factor in factors.items():
        out[name] = (out[name] * factor).astype(out[name].dtype)
    return out
```

```python
import numpy as np
import concourse.bass as bass
from concourse import mybir
from contextlib import ExitStack
from itertools import zip_longest

P = 128
B, S, D = 4, 512, 128
NI = S // P
NT = B * NI
SC = 77
MASK_W = (SC + 3) // 4
G, HG, HR = 4, 4, 32
MROW, KROW, QROW = 8, 9, 10
NEG = -float(2 ** 100)
E8 = 8
F0 = 512
F1 = 256
CAP = int(1.25 * B * S / E8)
NL = 4
LOOKBACK = 128
MAGIC = 1.5 * 2 ** 23

CONST_COLS = {}
_at = 0
for _n, _w in (("ident", P), ("causal", P), ("causal_t", P), ("cumul", P), ("cos", NI * 8), ("sin", NI * 8),
               ("kscale8", 1), ("kscale4", 1), ("iota", SC), ("rev", E8), ("minus_half", NI)):
    CONST_COLS[_n] = (_at, _w)
    _at += _w
CONST_W = _at
V_N1, V_N2, V_N3, V_LNG, V_LNB, V_ATTB, V_B1, V_B2 = 0, 4, 8, 12, 13, 14, 15, 47
VEC_W = 55
R_NEXTB, R_WS, R_QB, R_NF, R_RB = 0, P, 2 * P, 3 * P, 4 * P
ROW_W = 4 * P + E8
U_WQ, U_WK, U_WV, U_WO, U_BV, U_BO, U_W = 0, 512, 1024, 1152, 1280, 1408, 1536
L_QKV, L_WO, L_WG, L_WU, L_WD, L_BQKV, L_BO, L_W = 0, 384, 512, 1024, 1536, 2048, 2432, 2560
M_ATT, M_NEXT, M_GATE, M_ROUT, MAT_W = 0, 128, 256, 264, 272


class Line:

    def __init__(self, prog, name, chained):
        self.prog, self.name, self.chained = prog, name, chained
        self.todo, self.waited = [], {}
        self.part("start")

    def part(self, stage):
        self.sem = self.prog.semaphore(f"{self.name}_{stage}")
        self.count = 0
        self.last = None

    def wait(self, *marks):
        for m in marks:
            if m is None:
                continue
            if isinstance(m, list):
                self.wait(*m)
            elif self.waited.get(m[1], 0) < m[2]:
                self.waited[m[1]] = m[2]
                self.todo.append(("wait", m[0], m[2]))

    def do(self, what, *after, signal=True):
        self.wait(*after)
        if self.chained:
            self.wait(self.last)
        if not signal:
            self.todo.append(("do", what, None))
            return None
        self.count += 1
        self.todo.append(("do", what, self.sem))
        self.last = (self.sem, id(self.sem), self.count)
        return self.last

    def play(self, eng):
        for kind, a, n in self.todo:
            if kind == "wait":
                eng.wait_ge(a, n)
            elif n is None:
                a(eng)
            else:
                a(eng).then_inc(n, 1)


class Ring:

    def __init__(self, bufs):
        self.bufs, self.free, self.n = bufs, [[] for _ in bufs], -1

    def take(self):
        self.n += 1
        i = self.n % len(self.bufs)
        return Slot(self, i, self.bufs[i], self.free[i])


class Slot:
    def __init__(self, ring, i, buf, busy):
        self.ring, self.i, self.buf, self.busy = ring, i, buf, busy

    def read_by(self, *marks):
        self.ring.free[self.i] = list(marks)


class Prog:
    def __init__(self, nc, ctx):
        self.nc, self.ctx, self.nsem = nc, ctx, 0

    def semaphore(self, name):
        self.nsem += 1
        return self.ctx.enter_context(self.nc.semaphore(name))

    def sbuf(self, name, shape, dt=mybir.dt.float32):
        return self.ctx.enter_context(self.nc.sbuf_tensor(name, shape, dt))

    def psum(self, name, shape, dt=mybir.dt.float32):
        return self.ctx.enter_context(self.nc.psum_tensor(name, shape, dt))


def pipeline(items):
    before = None
    for item in list(items) + [None]:
        first = item[0]() if item else iter(())
        second = before[1]() if before else iter(())
        for _ in zip_longest(second, first):
            pass
        before = item


def build(nc, io):
    F32, BF, I32 = mybir.dt.float32, mybir.dt.bfloat16, mybir.dt.int32
    U8, I8 = mybir.dt.uint8, mybir.dt.int8
    ALU, ACT, AX = mybir.AluOpType, mybir.ActivationFunctionType, mybir.AxisListType
    with ExitStack() as ctx:
        pr = Prog(nc, ctx)
        sb = pr.sbuf
        pe, dve, act, pool = (Line(pr, n, c) for n, c in (("pe", False), ("dve", True), ("act", True), ("pool", True)))
        sync = Line(pr, "sync", False)
        lines = (pe, dve, act, pool)

        def stage(name):
            for line in lines:
                line.part(name)

        A = sb("A", [P, 10240])
        w1 = A[:, 0:4096].rearrange("p (e f) -> p e f", e=E8)
        w2 = A[:, 4096:8192].rearrange("p (e c d) -> p e c d", e=E8, c=4)
        gate1 = A[:, 0:2048].rearrange("p (e h) -> p e h", e=E8)
        up1 = A[:, 2048:4096].rearrange("p (e h) -> p e h", e=E8)
        down1 = A[:, 4096:6144].rearrange("p (e c d) -> p e c d", e=E8, c=2)
        qk_tok = A[:, 0:4096].rearrange("p (t k h r) -> p t k h r", t=NI, k=2, h=16)
        v_self = A[:, 4096:6144].rearrange("p (t h r) -> p t h r", t=NI, h=16)
        k_self = Ring([A[:, 6144 + 2048 * n:8192 + 2048 * n].rearrange("p (i s) -> p i s", i=HG) for n in range(2)])
        expert = sb("expert", [P, E8 * D])
        unit_w = Ring([sb(f"unit_w{n}", [P, U_W]) for n in range(2)])
        layer_w = Ring([sb(f"layer_w{n}", [P, L_W]) for n in range(2)])
        x = sb("x", [P, NT, D])
        y = sb("y", [P, NT, D])
        hT = sb("hT", [P, B, S])
        hn = Ring([sb(f"hn{n}", [P, NI, D]) for n in range(2)])
        kx = sb("kx", [P, 16, B * SC])
        vx = sb("vx", [P, B, 16, HR])
        q_g = Ring([sb(f"q_g{n}", [P, S]) for n in range(4)])
        prob = Ring([sb(f"prob{n}", [P, 2 * S]) for n in range(3)])
        mneg = Ring([sb(f"mneg{n}", [P, NI, HG, HR]) for n in range(2)])
        oT = Ring([sb(f"oT{n}", [P, S]) for n in range(2)])
        o_tok = Ring([sb(f"o_tok{n}", [P, NI, D]) for n in range(2)])
        hid = Ring([sb(f"hid{n}", [P, 4, S]) for n in range(2)])
        bias_q_raw = sb("bias_q", [P, NT * SC // 2])
        bias_k_raw = sb("bias_k", [P, B * S // 2])
        bias_q = bias_q_raw[:, :].bitcast(BF).rearrange("p (t k) -> p t k", t=NT)
        bias_k = bias_k_raw[:, :].bitcast(BF).rearrange("p (b s) -> p b s", b=B)
        k_extra = bias_q_raw[:, 0:G * SC].rearrange("p (g k) -> p g k", g=G)
        q_extra = bias_k_raw[:, 0:S]
        qkv = sb("qkv", [P, NI, 3 * D])
        rope_b = sb("rope_b", [P, NI * 2 * D])
        cst = sb("cst", [P, CONST_W])
        ident_b = sb("ident_b", [P, P], BF)
        causal_b = sb("causal_b", [P, 2 * P], BF)
        cumul_b = sb("cumul_b", [P, 2 * P], BF)
        vec = sb("vec", [P, VEC_W])
        rows = sb("rows", [P, ROW_W])
        mats = sb("mats", [P, MAT_W])
        ub = sb("ub", [P, 8, 2 * G])
        ubs = sb("ubs", [P, 8, G])
        ctxT = sb("ctxT", [P, B, SC])
        expert_b = sb("expert_b", [E8, D])
        wq8_words = sb("wq8", [P, D // 4], I32)
        wq8 = wq8_words[:, :].bitcast(I8)
        wqb = sb("wqb", [P, D], BF)
        stats = sb("stats", [P, NI, 6])
        mv = sb("mv", [P, NI, 2])
        ve = sb("ve", [P, NI])
        rstd = Ring([sb(f"rstd{n}", [P, NI]) for n in range(2)])
        recip = sb("recip", [P, NI * HG])
        comb = sb("comb", [P, NT, E8])
        small = sb("small", [P, 16])

        def const(name):
            a, w = CONST_COLS[name]
            return cst[:, a:a + w]

        ident = const("ident")
        wide = Ring([pr.psum(f"wide{n}", [P, 2 * S]) for n in range(3)])
        acc = Ring([pr.psum(f"acc{n}", [P, S]) for n in range(2)])

        def mm(out, lhsT, rhs, *after, start=True, stop=True, signal=False, turn=False):
            return pe.do(lambda e: e.matmul(out, lhsT, rhs, start=start, stop=stop, is_transpose=turn),
                         *after, signal=signal)

        def v_tt(out, a, b, op, *after, line=dve):
            return line.do(lambda e: e.tensor_tensor(out, a, b, op), *after)

        def v_ts(out, a, s1, s2, op0, op1=None, *after, line=dve):
            if op1 is None:
                return line.do(lambda e: e.tensor_scalar(out, a, s1, None, op0), *after)
            return line.do(lambda e: e.tensor_scalar(out, a, s1, s2, op0, op1), *after)

        def v_stt(out, a, s, b, op0, op1, *after):
            return dve.do(lambda e: e.scalar_tensor_tensor(out=out, in0=a, scalar=s, in1=b, op0=op0, op1=op1), *after)

        def v_red(out, a, op, *after, negate=False, mag=False):
            return dve.do(lambda e: e.tensor_reduce(out, a, AX.X, op, negate=negate, apply_absolute_value=mag), *after)

        def v_copy(out, a, *after, line=dve):
            return line.do(lambda e: e.tensor_copy(out, a), *after)

        def a_act(out, a, func, *after, bias=0.0, scale=1.0):
            return act.do(lambda e: e.activation(out, a, func, bias=bias, scale=scale), *after)

        def a_copy(out, a, *after, scale=1.0):
            return a_act(out, a, ACT.Copy, *after, scale=scale)

        def zero(ap, *after, value=0.0, line=pool):
            return line.do(lambda e: e.memset(ap, value), *after)

        def load(name, pairs, *after):
            sem = pr.semaphore(f"load_{name}")
            sync.wait(*after)
            for dst, src in pairs:
                sync.todo.append(("do16", dst, src, sem))
            return (sem, id(sem), 16 * len(pairs))

        def spread(src, n, parts=P):
            return src.partition_broadcast(parts) if n else src

        ld_const = load("const", [(cst[:, :], io["consts"])])
        ld_small = load("small", [(ctxT[:, :, :], io["ctxT"]), (ub[:, :, :], io["unit_b"]),
                                  (vec[:, :], io["vecs"]), (mats[:, :], io["mats"]),
                                  (rows[:, :], spread(io["rows"], 1)), (expert_b[:, :], io["expert_b"]),
                                  (wq8_words[:, :], io["wq8"])])

        def load_unit(n, *after):
            s = unit_w.take()
            s.mark = load(f"unit{n}", [(s.buf[:, 0:U_BV], io["unit_w"][n]),
                                       (s.buf[:, U_BV:U_W], spread(io["unit_rows"][n], 1))], s.busy, *after)
            return s

        def load_layer(n):
            s = layer_w.take()
            s.mark = load(f"layer{n}", [(s.buf[:, 0:L_BQKV], io["layer_w"][n]),
                                        (s.buf[:, L_BQKV:L_W], spread(io["layer_rows"][n], 1))], s.busy)
            return s

        m_in = hid.bufs[0][:, :, :].rearrange("p c s -> p (c s)")
        mask_raw = m_in[:, 0:NT * SC].bitcast(I32).rearrange("p (t k) -> p t k", t=NT)
        units = {0: load_unit(0)}
        ld_mask = load("mask", [(mask_raw, io["mask"].rearrange("b (i p) k -> p (b i) k", p=P))])
        ld_x = [load(f"x{b}", [(x[:, NI * b:NI * b + NI, :], io["x"][b].rearrange("(i p) d -> p i d", p=P))])
                for b in range(B)]
        units[1] = load_unit(1)
        ld_w0 = load("experts0", [(w1, io["w1"]), (w2, io["w2"])])
        ld_experts3 = load("experts3", [(expert[:, :], io["expert_w"])])
        layers = {0: load_layer(0), 1: load_layer(1)}

        made = [zero(kx[:, :, :]), zero(vx[:, :, :, :])]
        made = [zero(vx[:, :, :, MROW:MROW + 1], value=1.0)]
        for r in (mneg, o_tok):
            for buf in r.bufs:
                made.append(zero(buf[:, :, :, :] if r is mneg else buf[:, :, :]))
        made_pool = made[-1]
        v_copy(ident_b[:, :], ident, ld_const)
        v_copy(causal_b[:, 0:P], const("causal"))
        v_copy(causal_b[:, P:2 * P], const("causal_t"))
        v_copy(cumul_b[:, 0:P], const("cumul"))
        zero(cumul_b[:, P:2 * P], value=1.0, line=dve)
        v_copy(wqb[:, :], wq8, ld_small)
        for n in range(8):
            made_dve = v_ts(ubs[:, n, :], ub[:, n, G:2 * G], const("kscale4" if n in (1, 2) else "kscale8"), None,
                            ALU.mult, None)
        for line in (pe, act, pool, dve):
            line.wait(ld_const, ld_small, made_pool, made_dve)
        x_at = {b: [ld_x[b]] for b in range(B)}
        y_at = {b: [] for b in range(B)}
        hT_free = {b: [] for b in range(B)}

        def tiles(buf, b):
            return buf[:, NI * b:NI * b + NI, :]

        def normalise(src, dst, eps, rms, *after):
            for i in range(NI):
                dve.do(lambda e, i=i: e.bn_stats(stats[:, i, :], src[:, i, :]), *after)
            for i in range(NI):
                dve.do(lambda e, i=i: e.bn_aggr(mv[:, i, :], stats[:, i, :]))
            mean, var = mv[:, :, 0], mv[:, :, 1]
            if rms:
                v_tt(ve[:, :], mean, mean, ALU.mult)
                v_stt(ve[:, :], ve[:, :], eps, var, ALU.add, ALU.add)
            else:
                v_ts(ve[:, :], var, eps, None, ALU.add)
            r = rstd.take()
            ready = v_tt(r.buf[:, :], ve[:, :], const("minus_half"), ALU.pow, dve.last, r.busy, line=pool)
            for i in range(NI):
                if rms:
                    done = v_ts(dst[:, i, :], src[:, i, :], r.buf[:, i:i + 1], None, ALU.mult, None, ready)
                else:
                    done = v_ts(dst[:, i, :], src[:, i, :], mv[:, i, 0:1], r.buf[:, i:i + 1],
                                ALU.subtract, ALU.mult, ready)
            r.read_by(done)
            return done

        def turn_batch(src, b, *after, scale=None, shift=None, dst=None, busy=None):
            s = wide.take()
            for i in range(NI):
                m = mm(s.buf[:, P * i:P * i + P], src[:, i, :], ident, *after, s.busy, signal=i == NI - 1, turn=True)
            out = hT[:, b, :] if dst is None else dst
            wait = [m] + (hT_free[b] if busy is None else busy)
            if scale is None:
                done = a_copy(out, s.buf[:, 0:S], wait)
            elif shift is None:
                done = a_copy(out, s.buf[:, 0:S], wait, scale=scale)
            else:
                done = a_act(out, s.buf[:, 0:S], ACT.Identity, wait, bias=shift, scale=scale)
            s.read_by(done)
            return m, done

        mask_free = [[]]

        def turn_masks(*after):
            for b in range(B):
                s = wide.take()
                for i in range(NI):
                    m = mm(s.buf[0:SC, P * i:P * i + P], bias_q[:, NI * b + i, :], ident_b[:, :], *after, s.busy,
                           signal=i == NI - 1)
                done = a_copy(bias_k[0:SC, b, :], s.buf[0:SC, 0:S], m, mask_free[0])
                s.read_by(done)
            return [m, done]

        def project_out(ot, ready, w, bias, stream, at, b):
            s = oT.take()
            m, done = turn_batch(ot.buf, b, *ready, dst=s.buf[:, :], busy=s.busy)
            ot.read_by(m)
            yield
            a = acc.take()
            for i in range(NI):
                m = mm(a.buf[:, P * i:P * i + P], s.buf[:, P * i:P * i + P], w, done, a.busy, signal=i == NI - 1)
            s.read_by(m)
            dst = tiles(stream, b)
            done = v_tt(dst, a.buf[:, :].rearrange("p (i d) -> p i d", i=NI), dst, ALU.add, m, *at[b])
            a.read_by(done)
            if bias is not None:
                done = v_tt(dst, dst, bias.unsqueeze(1).broadcast_to([P, NI, D]), ALU.add, done, line=pool)
            at[b] = [done]
            yield

        def normalise_heads(ta, dh, ot, h0):
            v = ta.buf[:, 0:S].rearrange("p (t i r) -> p t i r", t=NI, i=HG)
            rc = recip[:, :].rearrange("p (t i) -> p t i", t=NI)
            dve.do(lambda e: e.reciprocal(rc, v[:, :, :, MROW]), ta.mark)
            out = ot.buf[:, :, h0 * dh:(h0 + HG) * dh].rearrange("p t (i r) -> p t i r", i=HG)
            done = v_tt(out, v[:, :, :, 0:dh], rc.unsqueeze(3).broadcast_to([P, NI, HG, dh]), ALU.mult, ot.busy)
            ta.read_by(done)
            return done

        def group_out(a, m, dh, ot, h0):
            s = oT.take()
            done = a_copy(s.buf[:, :], a.buf[:, :], m, s.busy)
            a.read_by(done)
            yield
            t = wide.take()
            for i in range(NI):
                t.mark = mm(t.buf[:, P * i:P * i + P], s.buf[:, P * i:P * i + P], ident, done, t.busy,
                            signal=i == NI - 1, turn=True)
            s.read_by(t.mark)
            yield
            ot.done = normalise_heads(t, dh, ot, h0)

        def add_maxima(mx, q, ready):
            t = wide.take()
            for i in range(NI):
                m = mm(t.buf[:, P * i:P * i + P], mx.buf[:, i, :, :].rearrange("p h r -> p (h r)"), ident,
                       ready, t.busy, signal=i == NI - 1, turn=True)
            mx.read_by(m)
            q.full = v_tt(q.buf[:, :], t.buf[:, 0:S], q.buf[:, :], ALU.add, m)
            t.read_by(q.full)

        kx_free, vx_free = [[]], [[]]

        def cross_unit(n, dh, src, at, masked, alibi, proj, bias_o, eps, scale_of, first_unit=True, rms=False):
            w = units[n]
            state = {"reads": []}

            def keys_values():
                for g in range(G):
                    s = wide.take()
                    m = mm(s.buf[:, 0:B * SC], w.buf[:, U_WK + P * g:U_WK + P * g + P],
                           ctxT[:, :, :].rearrange("p b k -> p (b k)"), w.mark, s.busy, signal=True)
                    done = []
                    for i in range(HG):
                        r = slice(HR * i, HR * i + HR)
                        out, inp = kx[r, HG * g + i, :], s.buf[r, 0:B * SC]
                        ks = const("kscale4" if dh == 4 else "kscale8")[r, :]
                        if alibi:
                            a_act(out, inp, ACT.Identity, m, kx_free[0], bias=ubs[r, n, g:g + 1], scale=ks)
                            o3 = out.rearrange("p (b k) -> p b k", b=B)
                            done.append(v_tt(o3, o3, k_extra[r, g:g + 1, :].broadcast_to([HR, B, SC]), ALU.add,
                                             act.last, *state["extra"]))
                        elif i % 2:
                            done.append(a_act(out, inp, ACT.Identity, m, kx_free[0], bias=ubs[r, n, g:g + 1],
                                              scale=ks))
                        else:
                            done.append(v_ts(out, inp, ks, ubs[r, n, g:g + 1], ALU.mult, ALU.add, m, kx_free[0]))
                    s.read_by(act.last, dve.last)
                    yield
                s = wide.take()
                for b in range(B):
                    m = mm(s.buf[0:SC, P * b:P * b + P], ctxT[:, b, :], w.buf[:, U_WV:U_WV + P], w.mark, s.busy,
                           signal=b == B - 1)
                pv = s.buf[0:SC, 0:S].rearrange("p (b h r) -> p b h r", b=B, h=D // dh)[:, :, 0:16, :]
                bv = w.buf[0:SC, U_BV:U_BV + 16 * dh].rearrange("p (h r) -> p h r", h=16)
                for b in range(B):
                    state["v"] = v_tt(vx[0:SC, b, :, 0:dh], pv[:, b, :, :], bv, ALU.add, m, vx_free[0])
                s.read_by(state["v"])
                state["k"] = [act.last, dve.last]
                yield

            def prep(b):
                h = hn.take()
                done = normalise(tiles(src, b), h.buf, eps, rms, *at[b], h.busy)
                m, state["h", b] = turn_batch(h.buf, b, done, scale=scale_of)
                h.read_by(m)
                yield

            def scores(b, g):
                if b == 0 and g == 0:
                    yield from keys_values()
                if g == 0 and first_unit:
                    yield from prep(b)
                if g == 0 and not first_unit:
                    state["h", b] = prepared[b]
                prepared[b] = state["h", b]
                s = wide.take()
                m = mm(s.buf[:, 0:S], w.buf[:, U_WQ + P * g:U_WQ + P * g + P], hT[:, b, :], w.mark,
                       state["h", b], s.busy, signal=True)
                hT_free[b] = [m]
                q = state["q", b, g] = q_g.take()
                if alibi:
                    done = v_stt(q.buf[:, :], s.buf[:, 0:S], ub[:, n, g:g + 1], q_extra[:, :], ALU.add, ALU.add,
                                 m, q.busy, *state["extra"])
                else:
                    done = v_ts(q.buf[:, :], s.buf[:, 0:S], ub[:, n, g:g + 1], None, ALU.add, None, m, q.busy)
                s.read_by(done)
                yield
                mx = mneg.take()
                for half in range(2):
                    s = wide.take()
                    for tt in range(2):
                        t = 2 * half + tt
                        bank = s.buf[:, S * tt:S * tt + HG * SC]
                        if masked:
                            mm(bank.rearrange("p (i k) -> p i k", i=HG), ident_b[:, :],
                               bias_q[:, NI * b + t:NI * b + t + 1, :].broadcast_to([P, HG, SC]), *masked, s.busy,
                               stop=False)
                        for i in range(HG):
                            m = mm(bank[:, SC * i:SC * i + SC], q.buf[:, P * t:P * t + P],
                                   kx[:, HG * g + i, SC * b:SC * b + SC], done, s.busy, *state["k"],
                                   start=not masked, stop=not masked or i == HG - 1, signal=(tt, i) == (1, HG - 1))
                    v = s.buf[:, :].rearrange("p (t c) -> p t c", t=2)[:, :, 0:HG * SC]\
                        .rearrange("p t (i k) -> p t i k", i=HG)
                    top = v_red(mx.buf[:, 2 * half:2 * half + 2, :, MROW], v, ALU.max, m, mx.busy, negate=True)
                    s.read_by(top)
                    yield
                add_maxima(mx, q, top)
                yield

            def attend(b, g):
                q = state["q", b, g]
                a = acc.take()
                if g == 0:
                    state["o", b] = o_tok.take()
                ot = state["o", b]
                pend = None
                for hp in range(HG // 2 + 1):
                    nxt = None
                    if hp < HG // 2:
                        s = wide.take()
                        for ii in range(2):
                            i = 2 * hp + ii
                            bank = s.buf[0:SC, S * ii:S * ii + S]
                            if masked:
                                mm(bank, ident_b[0:SC, 0:SC], bias_k[0:SC, b, :], *masked, s.busy, stop=False)
                            m = mm(bank, kx[:, HG * g + i, SC * b:SC * b + SC], q.buf[:, :], q.full, s.busy,
                                   start=not masked, stop=True, signal=ii == 1)
                        q.read_by(m)
                        pb = prob.take()
                        e = a_act(pb.buf[0:SC, :], s.buf[0:SC, :], ACT.Exp, m, pb.busy)
                        s.read_by(e)
                        nxt = (hp, pb, e)
                        yield
                    if pend:
                        php, pb, e = pend
                        for ii in range(2):
                            i = 2 * php + ii
                            m = mm(a.buf[HR * i:HR * i + HR, :], vx[0:SC, b, HG * g + i, :],
                                   pb.buf[0:SC, S * ii:S * ii + S], e, a.busy, state["v"], signal=ii == 1)
                        pb.read_by(m)
                        yield
                    pend = nxt
                yield from group_out(a, m, dh, ot, HG * g)
                if (b, g) == (B - 1, G - 1):
                    kx_free[0] = vx_free[0] = [m]
                    if masked or alibi:
                        mask_free[0] = [m, q.full]
                if g == G - 1:
                    if proj:
                        yield from project_out(ot, [ot.done], w.buf[:, U_WO:U_WO + P],
                                               w.buf[:, U_BO:U_BO + P] if bias_o else None, src if rms else x,
                                               at if rms else x_at, b)
                        if b == B - 1:
                            w.read_by(pe.last, pool.last)
                    else:
                        dst = tiles(x, b)
                        done = v_tt(dst, dst, ot.buf[:, :, :], ALU.add, ot.done, *x_at[b], line=pool)
                        ot.read_by(done)
                        x_at[b] = [done]
                        if b == B - 1:
                            w.read_by(pe.last)
                    if b == B - 1:
                        w.free = True

            prepared = cross_unit.prepared
            if alibi:
                state["extra"] = cross_unit.extra
            return [((lambda b=b, g=g: scores(b, g)), (lambda b=b, g=g: attend(b, g)))
                    for b in range(B) for g in range(G)]

        cross_unit.prepared = {}

        stage("l0_attn")
        done = v_ts(bias_q[:, :, :], mask_raw, 0.0, NEG, ALU.is_equal, ALU.mult, ld_mask)
        hid.free[0] = [done]
        masks = turn_masks(done)
        pipeline(cross_unit(0, 8, x, x_at, masks, False, False, False, 1e-5, None))
        units[2] = load_unit(2)

        stage("l0_ffn")

        def ffn0_first(b, st):
            h1, h2 = hn.take(), hn.take()
            done1 = normalise(tiles(x, b), h1.buf, 1e-5, False, *x_at[b], h1.busy)
            yield
            st["x1T"] = q_g.take()
            m, st["x1"] = turn_batch(h1.buf, b, done1, dst=st["x1T"].buf[:, :], busy=st["x1T"].busy)
            done2 = normalise(h1.buf, h2.buf, 1e-5, False, done1, h2.busy)
            h1.read_by(m, done2)
            yield
            st["ln"] = q_g.take()
            m, ln = turn_batch(h2.buf, b, done2, scale=vec[:, V_LNG:V_LNG + 1], shift=vec[:, V_LNB:V_LNB + 1],
                               dst=st["ln"].buf[:, :], busy=st["ln"].busy)
            h2.read_by(m)
            a = wide.take()
            m = mm(a.buf[:, 0:S], mats[:, M_ATT:M_ATT + P], st["ln"].buf[:, :], ln, a.busy, signal=True)
            st["ln"].read_by(m)
            st["xa"] = v_stt(hT[:, b, :], a.buf[:, 0:S], vec[:, V_ATTB:V_ATTB + 1], st["x1T"].buf[:, :], ALU.add,
                             ALU.add, m, st["x1"], *hT_free[b])
            a.read_by(st["xa"])
            st["x1T"].read_by(st["xa"])
            yield

        def ffn0_second(b, st):
            out = acc.take()
            y2 = q_g.take()
            for i in range(NI):
                e = (NI * b + i) % E8
                s = wide.take()
                for c in range(4):
                    m = mm(s.buf[:, P * c:P * c + P], w1[:, e, P * c:P * c + P], hT[:, b, P * i:P * i + P],
                           ld_w0, st["xa"], s.busy, signal=c == 3)
                h = hid.take()
                for c in range(4):
                    k = V_B1 + 4 * e + c
                    g = a_act(h.buf[:, c, 0:P], s.buf[:, P * c:P * c + P], ACT.Gelu, m, h.busy, bias=vec[:, k:k + 1])
                s.read_by(g)
                yield
                s = wide.take()
                for c in range(4):
                    m = mm(s.buf[:, 0:P], w2[:, e, c, :], h.buf[:, c, 0:P], g, s.busy, start=c == 0, stop=c == 3,
                           signal=c == 3)
                h.read_by(m)
                ydone = v_ts(y2.buf[:, P * i:P * i + P], s.buf[:, 0:P], vec[:, V_B2 + e:V_B2 + e + 1], None, ALU.add,
                             None, m, y2.busy)
                s.read_by(ydone)
                m = mm(out.buf[:, P * i:P * i + P], y2.buf[:, P * i:P * i + P], mats[:, M_NEXT:M_NEXT + P], ydone,
                       out.busy, signal=True)
                yield
            hT_free[b] = [m]
            y2.read_by(m)
            st["w_read"] = m
            h = hid.take()
            hv = h.buf[:, 0, :].rearrange("p (i d) -> p i d", i=NI)
            nb = rows[:, R_NEXTB:R_NEXTB + P].unsqueeze(1).broadcast_to([P, NI, D])
            done = v_tt(hv, out.buf[:, :].rearrange("p (i d) -> p i d", i=NI), nb, ALU.add, m, h.busy)
            out.read_by(done)
            g = a_act(h.buf[:, 1, :], h.buf[:, 0, :], ACT.Gelu, done)
            dst = tiles(x, b)
            done = v_tt(dst, dst, h.buf[:, 1, :].rearrange("p (i d) -> p i d", i=NI), ALU.add, g, *x_at[b],
                        line=pool)
            h.read_by(done)
            x_at[b] = [done]
            yield

        sts = [{} for _ in range(B)]
        pipeline([((lambda b=b: ffn0_first(b, sts[b])), (lambda b=b: ffn0_second(b, sts[b]))) for b in range(B)])
        w0_read = sts[B - 1]["w_read"]

        stage("l1_attn")
        raw = hid.take()
        words = raw.buf[:, 0, :].bitcast(I32)
        am_w = words[:, 0:NI * MASK_W].rearrange("p (i w) -> p i w", i=NI)
        pm_w = words[:, NI * MASK_W:(NI + B) * MASK_W].rearrange("p (b w) -> p b w", b=B)
        am = raw.buf[:, 0, 0:NI * MASK_W].bitcast(U8).rearrange("p (i k) -> p i k", i=NI)[:, :, 0:SC]
        pm = raw.buf[:, 0, NI * MASK_W:(NI + B) * MASK_W].bitcast(U8)\
            .rearrange("p (b k) -> p b k", b=B)[:, :, 0:SC]
        mm_f = raw.buf[:, 1:4, :].rearrange("p c s -> p (c s)")[:, 0:NT * SC].rearrange("p (b i k) -> p b i k", b=B, i=NI)
        ld_m1 = load("masks1", [(am_w, io["attn_mask"].rearrange("(i p) k -> p i k", p=P)),
                                (pm_w, spread(io["pad_mask"], 1))], raw.busy)
        for b in range(B):
            done = v_tt(mm_f[:, b, :, :], am, pm[:, b:b + 1, :].broadcast_to([P, NI, SC]), ALU.max, ld_m1)
        done = v_ts(bias_q[:, :, :], mm_f.rearrange("p b i k -> p (b i) k"), 0.0, NEG, ALU.is_gt, ALU.mult,
                    mask_free[0])
        raw.read_by(done)
        masks = turn_masks(done)
        ld_w1 = load("experts1", [(gate1, io["gate1"]), (up1, io["up1"]), (down1, io["down1"])], w0_read)
        pipeline(cross_unit(1, 4, x, dict(x_at), masks, False, True, False, 1e-5, None)
                 + [None] + cross_unit(2, 4, x, x_at, masks, False, True, True, 1e-5, None, first_unit=False))
        units[3], units[4] = load_unit(3), load_unit(4)

        stage("l1_ffn")
        logits = acc.take()
        for b in range(B):
            h = hn.take()
            done = normalise(tiles(x, b), h.buf, 1e-5, False, *x_at[b], h.busy)
            m, done = turn_batch(h.buf, b, done)
            h.read_by(m)
            sts[b]["h"] = done
            for i in range(NI):
                t = NI * b + i
                m = mm(logits.buf[:, E8 * t:E8 * t + E8], hT[:, b, P * i:P * i + P], mats[:, M_GATE:M_GATE + E8],
                       done, logits.busy, signal=(b, i) == (B - 1, NI - 1))

        work = hid.take()
        wk = work.buf[:, :, :].rearrange("p c s -> p (c s)")
        taken = [0]

        def piece(n, dt=F32):
            a = taken[0]
            taken[0] += n
            return wk[:, a:a + n]

        def softmax8(lg, n, prob_out, mx, *after):
            v_red(mx, lg, ALU.max, *after)
            v_tt(prob_out, lg, mx.unsqueeze(2).broadcast_to([P, n, E8]), ALU.subtract)
            a_act(prob_out, prob_out, ACT.Exp, dve.last)
            v_red(mx, prob_out, ALU.add, act.last)
            dve.do(lambda e: e.reciprocal(mx, mx))
            return v_tt(prob_out, prob_out, mx.unsqueeze(2).broadcast_to([P, n, E8]), ALU.mult)

        def first_max(pv, n, mx, c, hot):
            v_red(mx, pv, ALU.max)
            v_tt(c, pv, mx.unsqueeze(2).broadcast_to([P, n, E8]), ALU.is_equal)
            v_tt(c, c, const("rev").unsqueeze(1).broadcast_to([P, n, E8]), ALU.mult)
            v_red(small[:, 0:n], c, ALU.max)
            return v_tt(hot, c, small[:, 0:n].unsqueeze(2).broadcast_to([P, n, E8]), ALU.is_equal)

        W8 = NT * E8
        lv = logits.buf[:, 0:W8].rearrange("p (t e) -> p t e", e=E8)
        probs = piece(W8).rearrange("p (t e) -> p t e", e=E8)
        cand = piece(W8).rearrange("p (t e) -> p t e", e=E8)
        hot = piece(2 * W8).rearrange("p (k t e) -> p k t e", k=2, e=E8)
        tops = piece(2 * NT).rearrange("p (k t) -> p k t", k=2)
        rank = piece(2 * W8)
        before = piece(2 * W8)
        tot = piece(2 * W8)
        hot_b = piece(W8).bitcast(BF)
        dve.wait(work.busy)
        act.wait(work.busy)
        softmax8(lv, NT, probs, tops[:, 0, :], m)
        logits.read_by(dve.last)
        first_max(probs, NT, tops[:, 0, :], cand, hot[:, 0])
        v_tt(cand, hot[:, 0], probs, ALU.mult)
        v_tt(probs, probs, cand, ALU.subtract)
        v_tt(probs, probs, hot[:, 0], ALU.subtract)
        first_max(probs, NT, tops[:, 1, :], cand, hot[:, 1])
        v_tt(small[:, 0:NT], tops[:, 0, :], tops[:, 1, :], ALU.add)
        v_ts(small[:, 0:NT], small[:, 0:NT], 1e-9, None, ALU.add)
        dve.do(lambda e: e.reciprocal(small[:, 0:NT], small[:, 0:NT]))
        v_tt(tops, tops, small[:, 0:NT].unsqueeze(1).broadcast_to([P, 2, NT]), ALU.mult)
        hf = hot.rearrange("p k t e -> p (k t e)")
        hb = v_copy(hot_b, hf)
        s = wide.take()
        mm(s.buf[:, 0:2 * W8], cumul_b[:, 0:P], hot_b, hb, s.busy)
        m = mm(s.buf[:, S:S + 2 * W8], cumul_b[:, P:2 * P], hot_b, signal=True)
        v_copy(rank, s.buf[:, 0:2 * W8], m)
        v_copy(tot, s.buf[:, S:S + 2 * W8])
        s.read_by(dve.last)
        r4, b4, t4 = (v.rearrange("p (k t e) -> p k t e", k=2, e=E8) for v in (rank, before, tot))
        zero(b4[:, :, 0, :], line=dve)
        for t in range(1, NT):
            v_tt(b4[:, :, t, :], b4[:, :, t - 1, :], t4[:, :, t - 1, :], ALU.add)
        v_tt(rank, rank, before, ALU.add)
        v_ts(rank, rank, float(CAP) + 0.5, None, ALU.is_lt)
        v_tt(rank, rank, hf, ALU.mult)
        for k in range(2):
            v_tt(r4[:, k], r4[:, k], tops[:, k, :].unsqueeze(2).broadcast_to([P, NT, E8]), ALU.mult)
        combined = v_tt(comb[:, :, :], r4[:, 0], r4[:, 1], ALU.add)
        work.read_by(combined)

        def ffn1_step(b, e):
            def first():
                h = hid.take()
                sts[b]["hid"] = h
                for c in range(2):
                    s = wide.take()
                    mm(s.buf[:, 0:S], gate1[:, e, P * c:P * c + P], hT[:, b, :], ld_w1, sts[b]["h"], s.busy)
                    m = mm(s.buf[:, S:2 * S], up1[:, e, P * c:P * c + P], hT[:, b, :], signal=True)
                    g = a_act(h.buf[:, c, :], s.buf[:, 0:S], ACT.Silu, m, h.busy)
                    done = v_tt(h.buf[:, c, :], s.buf[:, S:2 * S], h.buf[:, c, :], ALU.mult, g)
                    s.read_by(done)
                    yield
                h.done = done
                hT_free[b] = [m]
                st_h[b, e] = h

            def second():
                h = st_h[b, e]
                a = acc.take()
                for i in range(NI):
                    for c in range(2):
                        m = mm(a.buf[:, P * i:P * i + P], h.buf[:, c, P * i:P * i + P], down1[:, e, c, :], h.done,
                               a.busy, start=c == 0, stop=c == 1, signal=(i, c) == (NI - 1, 1))
                    if i == 1:
                        yield
                h.read_by(m)
                for i in range(NI):
                    t = NI * b + i
                    done = v_stt(x[:, t, :], a.buf[:, P * i:P * i + P], comb[:, t, e:e + 1], x[:, t, :], ALU.mult,
                                 ALU.add, m, *x_at[b])
                x_at[b] = [done]
                a.read_by(done)
                st_h["w_read"] = m
                yield
            return first, second

        st_h = {}
        pipeline([ffn1_step(b, e) for b in range(B) for e in range(E8)])
        cleared = zero(A[:, :], st_h["w_read"])
        zero(qk_tok[:, :, 1, :, MROW:MROW + 1], value=1.0)
        cleared = zero(v_self[:, :, :, MROW:MROW + 1], value=1.0)

        stage("l2_attn")
        cross_unit.extra = [load("extras", [(k_extra, io["k_extra"]), (q_extra, io["q_extra"])], mask_free[0])]
        pipeline(cross_unit(3, 8, x, x_at, None, True, True, True, 1e-5, None))

        stage("l2_ffn")

        def quant_first(b, st):
            h = hn.take()
            normalise(tiles(x, b), h.buf, 1e-5, False, *x_at[b], h.busy)
            xs = q_g.take()
            st["xs"] = xs
            sc, inv = xs.buf[:, 0:NI], xs.buf[:, NI:2 * NI]
            v_red(sc, h.buf[:, :, :], ALU.max, xs.busy, mag=True)
            v_ts(sc, sc, 1e-6, 1.0 / 127.0, ALU.max, ALU.mult)
            dve.do(lambda e: e.reciprocal(inv, sc))
            for i in range(NI):
                v_ts(h.buf[:, i, :], h.buf[:, i, :], inv[:, i:i + 1], MAGIC, ALU.mult, ALU.add)
            v_ts(h.buf[:, :, :], h.buf[:, :, :], -MAGIC, -128.0, ALU.add, ALU.max)
            done = v_ts(h.buf[:, :, :], h.buf[:, :, :], 127.0, None, ALU.min)
            yield
            q = st["q"] = q_g.take()
            m, st["qd"] = turn_batch(h.buf, b, done, dst=q.buf[:, 0:S // 2].bitcast(BF), busy=q.busy)
            h.read_by(m)
            yield

        def quant_second(b, st):
            a = acc.take()
            qb = st["q"].buf[:, 0:S // 2].bitcast(BF)
            for i in range(NI):
                m = mm(a.buf[:, P * i:P * i + P], qb[:, P * i:P * i + P], wqb[:, :], st["qd"], a.busy,
                       signal=i == NI - 1)
            st["q"].read_by(m)
            h = hid.take()
            hv = h.buf[:, 0, :].rearrange("p (i d) -> p i d", i=NI)
            for i in range(NI):
                v_stt(hv[:, i, :], a.buf[:, P * i:P * i + P], st["xs"].buf[:, i:i + 1], rows[:, R_WS:R_WS + P],
                      ALU.mult, ALU.mult, m, h.busy)
            a.read_by(dve.last)
            st["xs"].read_by(dve.last)
            done = v_tt(hv, hv, rows[:, R_QB:R_QB + P].unsqueeze(1).broadcast_to([P, NI, D]), ALU.add)
            dst = tiles(x, b)
            done = v_tt(dst, dst, hv, ALU.add, done, *x_at[b], line=pool)
            h.read_by(done)
            x_at[b] = [done]
            yield

        pipeline([((lambda b=b: quant_first(b, sts[b])), (lambda b=b: quant_second(b, sts[b]))) for b in range(B)])

        stage("l3")
        raw = hid.take()
        seg_i = raw.buf[:, 3, 0:NT].bitcast(I32)
        seg = raw.buf[:, 3, NT:2 * NT]
        seg_lo = raw.buf[:, 3, 2 * NT:3 * NT]
        flat = raw.buf[:, 0:3, :].rearrange("p c s -> p (c s)")
        ld_seg = load("segments", [(seg_i, io["seg"])], raw.busy)
        late = flat[:, 0:NT * SC].rearrange("p (t k) -> p t k", t=NT)
        iota = const("iota").unsqueeze(1).broadcast_to([P, NT, SC])
        v_copy(seg, seg_i, ld_seg)
        v_ts(seg_lo, seg, -float(LOOKBACK), None, ALU.add)
        v_tt(late, iota, seg.unsqueeze(2).broadcast_to([P, NT, SC]), ALU.is_gt)
        v_tt(bias_q[:, :, :], iota, seg_lo.unsqueeze(2).broadcast_to([P, NT, SC]), ALU.is_le, mask_free[0])
        v_tt(late, late, bias_q[:, :, :], ALU.max)
        done = v_ts(bias_q[:, :, :], late, NEG, None, ALU.mult)
        raw.read_by(done)
        masks = turn_masks(done)
        for b in range(B):
            done = normalise(tiles(x, b), tiles(y, b), 1e-5, False, *x_at[b])
            y_at[b] = [done]

        tok_free = [[cleared]]
        v_free = [[cleared]]
        k_self.free = [[cleared], [cleared]]
        rope_free = [[]]

        def self_items(l):
            w = layers[l]
            st = {}

            def prep(b):
                h = hn.take()
                done = normalise(tiles(y, b), h.buf, 1e-6, True, *y_at[b], h.busy)
                m, hd = turn_batch(h.buf, b, done, scale=vec[:, V_N1 + l:V_N1 + l + 1])
                h.read_by(m)
                yield
                for half in range(2):
                    s = wide.take()
                    for tt in range(2):
                        i = 2 * half + tt
                        m = mm(s.buf[:, S * tt:S * tt + 3 * D], hT[:, b, P * i:P * i + P],
                               w.buf[:, L_QKV:L_QKV + 3 * D], w.mark, hd, s.busy, signal=tt == 1)
                    v = s.buf[:, :].rearrange("p (t c) -> p t c", t=2)
                    bias = w.buf[:, L_BQKV:L_BQKV + 3 * D].unsqueeze(1).broadcast_to([P, 2, 3 * D])
                    v_tt(qkv[:, 2 * half:2 * half + 2, 0:2 * D], v[:, :, 0:2 * D], bias[:, :, 0:2 * D], ALU.add, m,
                         rope_free[0])
                    for tt in range(2):
                        i = 2 * half + tt
                        st["v"] = v_tt(v_self[:, i, :, 0:8], v[:, tt, 2 * D:3 * D].rearrange("p (h r) -> p h r", h=16),
                                       w.buf[:, L_BQKV + 2 * D:L_BQKV + 3 * D].rearrange("p (h r) -> p h r", h=16),
                                       ALU.add, v_free[0])
                    s.read_by(dve.last)
                    yield
                hT_free[b] = [m]
                qk = qkv[:, :, 0:2 * D].rearrange("p t (h r) -> p t h r", r=8)
                rot = rope_b[:, :].rearrange("p (t h r) -> p t h r", t=NI, r=8)
                cs = const("cos").rearrange("p (t r) -> p t r", t=NI)
                sn = const("sin").rearrange("p (t r) -> p t r", t=NI)
                shape = [P, NI, 32, 4]
                v_tt(rot[:, :, :, 0:4], qk[:, :, :, 4:8], sn[:, :, 0:4].unsqueeze(2).broadcast_to(shape), ALU.mult,
                     rope_free[0])
                v_tt(rot[:, :, :, 4:8], qk[:, :, :, 0:4], sn[:, :, 4:8].unsqueeze(2).broadcast_to(shape), ALU.mult)
                v_tt(qk, qk, cs.unsqueeze(2).broadcast_to([P, NI, 32, 8]), ALU.mult)
                st["qk"] = v_tt(qk_tok[:, :, :, :, 0:8].rearrange("p t k h r -> p t (k h) r"), qk, rot, ALU.add,
                                tok_free[0])
                rope_free[0] = [st["qk"]]
                yield

            def scores(b, g):
                if g == 0:
                    yield from prep(b)
                    st["free"] = []
                s = wide.take()
                for k in range(2):
                    for i in range(NI):
                        m = mm(s.buf[:, S * k + P * i:S * k + P * i + P],
                               qk_tok[:, i, k, HG * g:HG * g + HG, :].rearrange("p h r -> p (h r)"), ident,
                               st["qk"], s.busy, signal=(k, i) == (1, NI - 1), turn=True)
                if g == G - 1:
                    tok_free[0] = [m]
                q, kk = q_g.take(), k_self.take()
                st[b, g] = (q, kk)
                done = [a_copy(q.buf[:, :], s.buf[:, 0:S], m, q.busy)]
                for i in range(HG):
                    r = slice(HR * i, HR * i + HR)
                    if i % 2:
                        done.append(a_copy(kk.buf[r, i, :], s.buf[r, S:2 * S], m, kk.busy))
                    else:
                        done.append(v_copy(kk.buf[r, i, :], s.buf[r, S:2 * S], m, kk.busy))
                s.read_by(*done)
                yield
                mx = mneg.take()
                for t in range(NI):
                    n = P * (t + 1)
                    per = HG if t < 2 else 2
                    for h0 in range(0, HG, per):
                        s = wide.take()
                        pitch = n if t < 2 else S
                        for i in range(h0, h0 + per):
                            at0 = pitch * (i - h0)
                            mm(s.buf[:, at0:at0 + n], q.buf[:, P * t:P * t + P], kk.buf[:, i, 0:n], *done, s.busy,
                               stop=False)
                            m = mm(s.buf[:, at0 + n - P:at0 + n], ident_b[:, :], causal_b[:, 0:P], start=False,
                                   signal=i == h0 + per - 1)
                        v = s.buf[:, 0:pitch * per].rearrange("p (i k) -> p i k", i=per)[:, :, 0:n]
                        top = v_red(mx.buf[:, t, h0:h0 + per, MROW], v, ALU.max, m, mx.busy, negate=True)
                        s.read_by(top)
                        yield
                add_maxima(mx, q, top)
                yield

            def attend(b, g):
                q, kk = st[b, g]
                a = acc.take()
                if g == 0:
                    st["o", b] = o_tok.take()
                ot = st["o", b]
                steps = [(j, h0, HG if j > 1 else 2) for j in range(NI) for h0 in range(0, HG, HG if j > 1 else 2)]
                pend = None
                for step in steps + [None]:
                    nxt = None
                    if step:
                        j, h0, per = step
                        n = S - P * j
                        pitch = n if j > 1 else S
                        s = wide.take()
                        for i in range(h0, h0 + per):
                            at0 = pitch * (i - h0)
                            mm(s.buf[:, at0:at0 + n], kk.buf[:, i, P * j:P * j + P], q.buf[:, P * j:S], q.full,
                               s.busy, stop=False)
                            m = mm(s.buf[:, at0:at0 + P], ident_b[:, :], causal_b[:, P:2 * P], start=False,
                                   signal=i == h0 + per - 1)
                        pb = prob.take()
                        sv = s.buf[:, 0:pitch * per].rearrange("p (i k) -> p i k", i=per)[:, :, 0:n]
                        pv = pb.buf[:, 0:n * per].rearrange("p (i k) -> p i k", i=per)
                        e = a_act(pv, sv, ACT.Exp, m, pb.busy, scale=8 ** -0.5)
                        s.read_by(e)
                        nxt = (j, h0, per, n, pb, pv, e)
                        if step == steps[-1]:
                            q.read_by(m)
                            kk.read_by(m)
                        yield
                    if pend:
                        j, h0, per, n, pb, pv, e = pend
                        for i in range(h0, h0 + per):
                            m = mm(a.buf[HR * i:HR * i + HR, P * j:S], v_self[:, j, HG * g + i, :],
                                   pv[:, i - h0, :], e, a.busy, start=j == 0, stop=j == NI - 1,
                                   signal=i == h0 + per - 1)
                        pb.read_by(m)
                    pend = nxt
                if g == G - 1:
                    v_free[0] = [m]
                yield from group_out(a, m, 8, ot, HG * g)
                if g == G - 1:
                    yield from project_out(ot, [ot.done], w.buf[:, L_WO:L_WO + P], w.buf[:, L_BO:L_BO + P], y, y_at, b)

            items = []
            for b in range(B):
                if b:
                    items.append(None)
                items += [((lambda b=b, g=g: scores(b, g)), (lambda b=b, g=g: attend(b, g))) for g in range(G)]
            return items

        def ffn3(l, b):
            w = layers[l]
            st = {}

            def first():
                h = hn.take()
                done = normalise(tiles(y, b), h.buf, 1e-6, True, *y_at[b], h.busy)
                m, st["h"] = turn_batch(h.buf, b, done, scale=vec[:, V_N3 + l:V_N3 + l + 1])
                h.read_by(m)
                yield

            def second():
                h = hid.take()
                for c in range(4):
                    s = wide.take()
                    mm(s.buf[:, 0:S], w.buf[:, L_WG + P * c:L_WG + P * c + P], hT[:, b, :], st["h"], s.busy)
                    m = mm(s.buf[:, S:2 * S], w.buf[:, L_WU + P * c:L_WU + P * c + P], hT[:, b, :], signal=True)
                    g = a_act(h.buf[:, c, :], s.buf[:, 0:S], ACT.Silu, m, h.busy)
                    done = v_tt(h.buf[:, c, :], s.buf[:, S:2 * S], h.buf[:, c, :], ALU.mult, g)
                    s.read_by(done)
                    yield
                hT_free[b] = [m]
                a = acc.take()
                for i in range(NI):
                    for c in range(4):
                        m = mm(a.buf[:, P * i:P * i + P], h.buf[:, c, P * i:P * i + P],
                               w.buf[:, L_WD + P * c:L_WD + P * c + P], done, a.busy, start=c == 0, stop=c == 3,
                               signal=(i, c) == (NI - 1, 3))
                    yield
                h.read_by(m)
                dst = tiles(y, b)
                done = v_tt(dst, a.buf[:, :].rearrange("p (i d) -> p i d", i=NI), dst, ALU.add, m, *y_at[b])
                a.read_by(done)
                y_at[b] = [done]
                if b == B - 1:
                    w.read_by(m)
                yield
            return first, second

        for l in range(NL):
            stage(f"l3_self{l}")
            pipeline(self_items(l))
            stage(f"l3_cross{l}")
            pipeline(cross_unit(4 + l, 8, y, y_at, masks, False, True, False, 1e-6,
                                vec[:, V_N2 + l:V_N2 + l + 1], rms=True))
            if l + 1 < NL:
                units[5 + l] = load_unit(5 + l)
            stage(f"l3_ffn{l}")
            pipeline([ffn3(l, b) for b in range(B)])
            if l + 2 < NL:
                layers[l + 2] = load_layer(l + 2)

        stage("l3_moe")

        def moe_first(b, st):
            h = hn.take()
            done = normalise(tiles(y, b), h.buf, 1e-6, True, *y_at[b], h.busy)
            v_tt(h.buf[:, :, :], h.buf[:, :, :], rows[:, R_NF:R_NF + P].unsqueeze(1).broadcast_to([P, NI, D]),
                 ALU.mult, done)
            dst = tiles(x, b)
            xd = v_tt(dst, dst, h.buf[:, :, :], ALU.add, *x_at[b])
            x_at[b] = [xd]
            done = normalise(dst, h.buf, 1e-5, False, xd)
            m, st["h"] = turn_batch(h.buf, b, done)
            h.read_by(m)
            yield
            s = wide.take()
            for i in range(NI):
                m = mm(s.buf[:, E8 * i:E8 * i + E8], hT[:, b, P * i:P * i + P], mats[:, M_ROUT:M_ROUT + E8], st["h"],
                       s.busy, signal=i == NI - 1)
            k = st["k"] = q_g.take()
            W = NI * E8
            lg, pv, cand, hot, cf = (k.buf[:, W * n:W * n + W].rearrange("p (i e) -> p i e", e=E8) for n in range(5))
            mx = k.buf[:, 5 * W:5 * W + NI]
            v_tt(lg, s.buf[:, 0:W].rearrange("p (i e) -> p i e", e=E8),
                 rows[:, R_RB:R_RB + E8].unsqueeze(1).broadcast_to([P, NI, E8]), ALU.add, m, k.busy)
            s.read_by(dve.last)
            softmax8(lg, NI, pv, mx)
            first_max(pv, NI, mx, cand, hot)
            st["coef"] = v_tt(cf, hot, mx.unsqueeze(2).broadcast_to([P, NI, E8]), ALU.mult)
            st["cf"] = cf
            yield

        def moe_second(b, st):
            s = wide.take()
            for i in range(NI):
                m = mm(s.buf[0:E8, P * i:P * i + P], st["cf"][:, i, :], ident, st["coef"], s.busy,
                       signal=i == NI - 1, turn=True)
            c = q_g.take()
            done = a_copy(c.buf[0:E8, :], s.buf[0:E8, 0:S], m, c.busy)
            s.read_by(done)
            a = acc.take()
            for i in range(NI):
                m = mm(a.buf[:, P * i:P * i + P], c.buf[0:E8, P * i:P * i + P], expert_b[:, :], done, a.busy,
                       signal=i == NI - 1)
            c.read_by(m)
            dst = tiles(x, b)
            done = v_tt(dst, a.buf[:, :].rearrange("p (i d) -> p i d", i=NI), dst, ALU.add, m, *x_at[b])
            a.read_by(done)
            yield
            for i in range(NI):
                t = NI * b + i
                s = wide.take()
                mm(s.buf[:, 0:S], hT[:, b, P * i:P * i + P], expert[:, 0:S], ld_experts3, st["h"], s.busy)
                m = mm(s.buf[:, S:2 * S], hT[:, b, P * i:P * i + P], expert[:, S:2 * S], signal=True)
                for e in range(E8):
                    done = v_stt(x[:, t, :], s.buf[:, D * e:D * e + D], st["cf"][:, i, e:e + 1], x[:, t, :],
                                 ALU.mult, ALU.add, m)
                s.read_by(done)
                yield
            st["k"].read_by(done)
            hT_free[b] = [m]
            out_sem = pr.semaphore(f"out{b}")
            sync.wait(done)
            sync.todo.append(("do16", io["out"][b].rearrange("(i p) d -> p i d", p=P), tiles(x, b), out_sem))
            stores.append(out_sem)
            yield

        stores = []
        sts = [{} for _ in range(B)]
        pipeline([((lambda b=b: moe_first(b, sts[b])), (lambda b=b: moe_second(b, sts[b]))) for b in range(B)])
        for sem in stores:
            sync.todo.append(("wait", sem, 16))

        block = ctx.enter_context(nc.Block())

        @block.sync
        def _(e):
            for entry in sync.todo:
                if entry[0] == "wait":
                    e.wait_ge(entry[1], entry[2])
                else:
                    e.dma_start(entry[1], entry[2]).then_inc(entry[3], 16)

        @block.tensor
        def _(e):
            pe.play(e)

        @block.vector
        def _(e):
            dve.play(e)

        @block.scalar
        def _(e):
            act.play(e)

        @block.gpsimd
        def _(e):
            pool.play(e)


def heads(w, dh):
    out = np.zeros((w.shape[0], 16, HR), w.dtype)
    out[:, :, :dh] = w.reshape(w.shape[0], 16, dh)
    return out.reshape(w.shape[0], 16 * HR)


def constants():
    c = np.zeros((P, CONST_W), np.float32)

    def put(name, v):
        a, w = CONST_COLS[name]
        c[:, a:a + w] = np.asarray(v).reshape(P, w) if np.ndim(v) > 1 else v

    r = np.arange(P)
    put("ident", np.eye(P))
    put("causal", np.where(r[None, :] > r[:, None], NEG, 0.0))
    put("causal_t", np.where(r[:, None] > r[None, :], NEG, 0.0))
    put("cumul", (r[:, None] <= r[None, :]).astype(np.float32))
    inv = (1.0 / np.float32(10000.0) ** (np.arange(0, 8, 2, dtype=np.float32) / np.float32(8))).astype(np.float32)
    ang = (np.arange(S, dtype=np.float32)[:, None] * inv[None, :]).astype(np.float32)
    ang = np.concatenate([ang, ang], 1)
    sign = np.array([-1.0] * 4 + [1.0] * 4, np.float32)
    put("cos", np.cos(ang).reshape(NI, P, 8).transpose(1, 0, 2).reshape(P, -1))
    put("sin", (np.sin(ang) * sign).reshape(NI, P, 8).transpose(1, 0, 2).reshape(P, -1))
    real = (r % HR < MROW)
    put("kscale8", np.where(real, 8 ** -0.5, 1.0)[:, None])
    put("kscale4", np.where(real, 4 ** -0.5, 1.0)[:, None])
    put("iota", np.tile(np.arange(SC, dtype=np.float32), (P, 1)))
    put("rev", np.tile(np.arange(E8, 0, -1, dtype=np.float32), (P, 1)))
    put("minus_half", np.full((P, NI), -0.5, np.float32))
    return c


def position_rows():
    slopes = 2.0 ** (-8 + np.arange(16))
    k = np.zeros((HG, HR, G, SC), np.float32)
    q = np.zeros((HG, HR, S), np.float32)
    for g in range(G):
        for i in range(HG):
            k[i, KROW, g] = -slopes[HG * g + i] * np.arange(SC)
            k[i, QROW, g] = slopes[HG * g + i]
    q[:, KROW] = 1.0
    q[:, QROW] = np.arange(S)
    return k.reshape(P, G, SC), q.reshape(P, S)


def mask_words(m):
    out = np.zeros((m.shape[0], 4 * MASK_W), np.uint8)
    out[:, :SC] = m.view(np.uint8)
    return out.view(np.int32)


def layout(i):
    z = np.zeros
    f = np.float32
    unit_w, unit_b, unit_rows = z((8, P, U_BV), f), z((P, 8, 2 * G), f), z((8, U_W - U_BV), f)

    def unit(n, dh, wq, wk, wv, bq, bk, bv, wo, bo):
        unit_w[n, :, U_WQ:U_WQ + 512] = heads(wq, dh)
        unit_w[n, :, U_WK:U_WK + 512] = heads(wk, dh)
        unit_w[n, :, U_WV:U_WV + wv.shape[1]] = wv
        if wo is not None:
            unit_w[n, :wo.shape[0], U_WO:U_WO + P] = wo
        qb, kb = z((G, HG, HR), f), z((G, HG, HR), f)
        if bq is not None:
            qb[:, :, :dh] = bq.reshape(G, HG, dh)
            kb[:, :, :dh] = bk.reshape(G, HG, dh)
            unit_rows[n, 0:bv.size] = bv
        kb[:, :, MROW] = 1.0
        unit_b[:, n, 0:G] = qb.reshape(G, P).T
        unit_b[:, n, G:] = kb.reshape(G, P).T
        if bo is not None:
            unit_rows[n, P:] = bo

    unit(0, 8, i["L0_xattn_Wq"].T, i["L0_xattn_Wk"].T, i["L0_xattn_Wv"].T, i["L0_xattn_bq"], i["L0_xattn_bk"],
         i["L0_xattn_bv"], None, None)
    w, wb = i["L1_xattn_Wqkv"], i["L1_xattn_bqkv"]
    for u in range(2):
        c = slice(64 * u, 64 * u + 64)
        unit(1 + u, 4, w[:, :P][:, c], w[:, P:2 * P][:, c], w[:, 2 * P:][:, c], wb[:P][c], wb[P:2 * P][c],
             wb[2 * P:][c], i["L1_xattn_Wo"][c], i["L1_xattn_bo"])
    unit(3, 8, i["L2_xattn_Wq"].T, i["L2_xattn_Wk"].T, i["L2_xattn_Wv"].T, i["L2_xattn_bq"], i["L2_xattn_bk"],
         i["L2_xattn_bv"], i["L2_xattn_Wo"].T, i["L2_xattn_bo"])
    for l in range(NL):
        kv = i["L3_xattn_Wkv_c"][l]
        unit(4 + l, 8, i["L3_xattn_Wq_c"][l].T, kv[:P].T, kv[P:].T, None, None, None, i["L3_xattn_Wo_c"][l].T, None)

    layer_w, layer_rows = z((NL, P, L_BQKV), f), z((NL, L_W - L_BQKV), f)
    for l in range(NL):
        layer_w[l, :, L_QKV:L_QKV + 384] = i["L3_xattn_Wqkv"][l].T
        layer_w[l, :, L_WO:L_WO + P] = i["L3_xattn_Wo"][l].T
        layer_w[l, :, L_WG:L_WG + F0] = i["L3_xattn_Wg"][l].T
        layer_w[l, :, L_WU:L_WU + F0] = i["L3_xattn_Wu"][l].T
        layer_w[l, :, L_WD:L_WD + F0] = i["L3_xattn_Wd"][l].T.reshape(4, P, D).transpose(1, 0, 2).reshape(P, -1)
        layer_rows[l, 0:384] = i["L3_xattn_bqkv"][l]
        layer_rows[l, 384:] = i["L3_xattn_bo"][l]

    vecs = z((P, VEC_W), f)
    for at, name in ((V_N1, "L3_xattn_n1"), (V_N2, "L3_xattn_n2"), (V_N3, "L3_xattn_n3")):
        vecs[:, at:at + NL] = i[name].T
    for at, name in ((V_LNG, "L0_ffn_ln_g"), (V_LNB, "L0_ffn_ln_b"), (V_ATTB, "L0_ffn_attn_b")):
        vecs[:, at] = i[name]
    vecs[:, V_B1:V_B1 + 4 * E8] = i["L0_ffn_b1"].reshape(E8 * 4, P).T
    vecs[:, V_B2:V_B2 + E8] = i["L0_ffn_b2"].T
    rows = np.concatenate([i["L0_ffn_next_b"], i["L2_ffn_weight_scale"], i["L2_ffn_bias"], i["L3_xattn_nf"],
                           i["L3_ffn_router_b"]])
    mats = np.concatenate([i["L0_ffn_attn_w"], i["L0_ffn_next_w"], i["L1_ffn_gate_w"].T, i["L3_ffn_router_w"]], 1)
    k_extra, q_extra = position_rows()
    return {
        "x": i["x"], "ctxT": i["ctx_1024"].transpose(2, 0, 1), "mask": i["mask_BxSxS2_if1"],
        "attn_mask": mask_words(i["mask_SxS2_bk1"]), "pad_mask": mask_words(i["mask_BxS2_bk0"]),
        "seg": i["itok_BxS_0_255"].reshape(NT, P).T, "unit_w": unit_w, "unit_b": unit_b, "unit_rows": unit_rows,
        "layer_w": layer_w, "layer_rows": layer_rows, "vecs": vecs, "rows": rows, "mats": mats,
        "consts": constants(), "k_extra": k_extra, "q_extra": q_extra,
        "w1": i["L0_ffn_w1"].transpose(1, 0, 2),
        "w2": i["L0_ffn_w2"].reshape(E8, 4, P, D).transpose(2, 0, 1, 3),
        "gate1": i["L1_ffn_gate_proj_w"].transpose(2, 0, 1), "up1": i["L1_ffn_up_proj_w"].transpose(2, 0, 1),
        "down1": i["L1_ffn_down_proj_w"].transpose(2, 0, 1).reshape(2, P, E8, D).transpose(1, 2, 0, 3),
        "wq8": np.ascontiguousarray(i["L2_ffn_weight_q"].T).view(np.int32), "expert_w": i["L3_ffn_expert_w"].transpose(1, 0, 2).reshape(P, E8 * D),
        "expert_b": i["L3_ffn_expert_b"],
    }


def kernel(**inputs):
    import concourse.bacc as bacc
    from concourse.bass_utils import run_bass_kernel_spmd as run

    arrays = {f"in_{k}": np.ascontiguousarray(v)
              for k, v in layout({k: np.asarray(v) for k, v in inputs.items()}).items()}
    nc = bacc.Bacc("TRN2", target_bir_lowering=False, num_devices=1)
    io = {k[3:]: nc.dram_tensor(k, v.shape, mybir.dt.from_np(v.dtype), kind="ExternalInput").ap()
          for k, v in arrays.items()}
    io["out"] = nc.dram_tensor("out", (B, S, D), mybir.dt.float32, kind="ExternalOutput").ap()
    build(nc, io)
    return run(nc, [arrays], core_ids=[0]).results[0]["out"]
```

```python
import numpy as np
import concourse.bass as bass
from concourse import mybir
from contextlib import ExitStack
from itertools import zip_longest

P = 128
B, S, D = 4, 512, 128
NI = S // P
NT = B * NI
SC = 77
SK = SC + SC % 2
MASK_W = (SC + 3) // 4
G, HG, HR = 4, 4, 32
PART = 8
MROW, KROW, QROW = 24, 26, 27
VSUM = 8
HIGH = -(1 << 12)
NEG = -float(2 ** 100)
E8 = 8
F0 = 512
F1 = 256
CAP = int(1.25 * B * S / E8)
NL = 4
LOOKBACK = 128
MAGIC = 1.5 * 2 ** 23

CONST_COLS = {}
_at = 0
for _n, _w in (("ident", P), ("causal", P), ("causal_t", P), ("cumul", P), ("cos", NI * 8), ("sin", NI * 8),
               ("kscale8", 1), ("kscale4", 1), ("pick", 2), ("position", NI), ("iota", SC), ("rev", E8), ("minus_half", NI)):
    CONST_COLS[_n] = (_at, _w)
    _at += _w
CONST_W = _at
V_N1, V_N2, V_N3, V_LNG, V_LNB, V_ATTB, V_B1, V_B2 = 0, 4, 8, 12, 13, 14, 15, 47
VEC_W = 55
R_NEXTB, R_WS, R_QB, R_NF, R_RB = 0, P, 2 * P, 3 * P, 4 * P
ROW_W = 4 * P + E8
U_WK, U_WQ, U_WV, U_WO, U_BQ, U_BV, U_BO, U_W = 0, 512, 640, 768, 896, 1024, 1152, 1280
L_QKV, L_WO, L_WG, L_WU, L_WD, L_BQKV, L_BO, L_W = 0, 384, 512, 1024, 1536, 2048, 2432, 2560
M_ATT, M_NEXT, M_GATE, M_ROUT, MAT_W = 0, 128, 256, 264, 272


class Line:

    def __init__(self, prog, name, chained):
        self.prog, self.name, self.chained = prog, name, chained
        self.todo, self.waited, self.last = [], {}, None
        self.part("start")

    def part(self, stage):
        self.sem, self.key = self.prog.semaphore(f"{self.name}_{stage}"), self.prog.nsem
        self.count = 0

    def wait(self, *marks):
        for m in marks:
            if m is None:
                continue
            if isinstance(m, list):
                self.wait(*m)
            elif self.waited.get(m[1], 0) < m[2]:
                self.waited[m[1]] = m[2]
                self.todo.append(("wait", m[0], m[2]))

    def do(self, what, *after, signal=True):
        self.wait(*after)
        if self.chained:
            self.wait(self.last)
        if not signal:
            self.todo.append(("do", what, None))
            return None
        self.count += 1
        self.todo.append(("do", what, self.sem))
        self.last = (self.sem, self.key, self.count)
        return self.last

    def play(self, eng):
        for kind, a, n in self.todo:
            if kind == "wait":
                eng.wait_ge(a, n)
            elif n is None:
                a(eng)
            else:
                a(eng).then_inc(n, 1)


class Ring:

    def __init__(self, bufs):
        self.bufs, self.free, self.idle = bufs, [[] for _ in bufs], list(range(len(bufs)))

    def take(self):
        i = self.idle.pop(0)
        return Slot(self, i, self.bufs[i], self.free[i])


class Slot:
    def __init__(self, ring, i, buf, busy):
        self.ring, self.i, self.buf, self.busy = ring, i, buf, busy

    def read_by(self, *marks):
        assert self.i not in self.ring.idle
        self.ring.free[self.i] = list(marks)
        self.ring.idle.append(self.i)


class Prog:
    def __init__(self, nc, ctx):
        self.nc, self.ctx, self.nsem = nc, ctx, 0

    def semaphore(self, name):
        self.nsem += 1
        return self.ctx.enter_context(self.nc.semaphore(name))

    def sbuf(self, name, shape, dt=mybir.dt.float32):
        return self.ctx.enter_context(self.nc.sbuf_tensor(name, shape, dt))

    def psum(self, name, shape, dt=mybir.dt.float32):
        return self.ctx.enter_context(self.nc.psum_tensor(name, shape, dt))


def pipeline(items):
    live = []

    def tick():
        for _ in zip_longest(*[phases[n]() for phases, n in reversed(live)]):
            pass
        live[:] = [(phases, n + 1) for phases, n in live if n + 1 < len(phases)]

    for item in list(items) + [None]:
        if item:
            live.append((item, 0))
            tick()
        while item is None and live:
            tick()


def build(nc, io):
    F32, BF, I32, FR = mybir.dt.float32, mybir.dt.bfloat16, mybir.dt.int32, mybir.dt.float32r
    U8, I8 = mybir.dt.uint8, mybir.dt.int8
    ALU, ACT, AX = mybir.AluOpType, mybir.ActivationFunctionType, mybir.AxisListType
    with ExitStack() as ctx:
        pr = Prog(nc, ctx)
        sb = pr.sbuf
        pe, dve, act, pool = (Line(pr, n, c) for n, c in (("pe", False), ("dve", True), ("act", True), ("pool", True)))
        sync = Line(pr, "sync", False)
        lines = (pe, dve, act, pool)

        def stage(name):
            for line in lines:
                line.part(name)

        A = sb("A", [P, 8192])
        w1 = A[:, 0:4096].rearrange("p (e f) -> p e f", e=E8)
        w2 = A[:, 4096:8192].rearrange("p (e c d) -> p e c d", e=E8, c=4)
        gate1 = A[:, 0:2048].rearrange("p (e h) -> p e h", e=E8)
        up1 = A[:, 2048:4096].rearrange("p (e h) -> p e h", e=E8)
        down1 = A[:, 4096:6144].rearrange("p (e c d) -> p e c d", e=E8, c=2)
        k_tok = A[:, 0:2048].rearrange("p (t h r) -> p t h r", t=NI, h=16)
        v_self = Ring([A[:, 2048 * n:2048 * n + 2048].rearrange("p (t h r) -> p t h r", t=NI, h=16) for n in (1, 2)])
        y = A[:, 6144:8192].rearrange("p (t d) -> p t d", t=NT)
        k_self = Ring([sb(f"k_self{n}", [P, HG, S], FR) for n in range(2)])
        unit_w = Ring([sb(f"unit_w{n}", [P, U_W]) for n in range(2)])
        layer_w = Ring([sb(f"layer_w{n}", [P, L_W]) for n in range(2)])
        x = sb("x", [P, NT, D])
        hT = sb("hT", [P, B, S])
        hn = Ring([sb(f"hn{n}", [P, NI, D]) for n in range(2)])
        kx = sb("kx", [P, 16, B * SK], FR)
        vx = sb("vx", [P, B, 16, HR])
        q_g = Ring([sb(f"q_g{n}", [P, 2, S], FR) for n in range(4)])
        prob = Ring([sb(f"prob{n}", [P, 2 * S]) for n in range(3)])
        oT = Ring([sb(f"oT{n}", [P, S]) for n in range(2)])
        o_tok = Ring([sb(f"o_tok{n}", [P, NI, D]) for n in range(2)])
        hid = Ring([sb(f"hid{n}", [P, 4, S]) for n in range(2)])
        bias_q_raw = sb("bias_q", [P, NT * SK // 2])
        bias_k_raw = sb("bias_k", [P, B * S // 2])
        bias_q = bias_q_raw[:, :].bitcast(BF).rearrange("p (t k) -> p t k", t=NT)
        bias_k = bias_k_raw[:, :].bitcast(BF).rearrange("p (b s) -> p b s", b=B)
        k_extra = bias_q_raw[:, 0:G * SK].rearrange("p (g k) -> p g k", g=G)
        qkv = sb("qkv", [P, NI, 3 * D])
        rope_b = sb("rope_b", [P, NI * 2 * D])
        cst = sb("cst", [P, CONST_W])
        ident_b = sb("ident_b", [P, P], BF)
        causal_b = sb("causal_b", [P, 2 * P], BF)
        cumul_b = sb("cumul_b", [P, 2 * P], BF)
        vec = sb("vec", [P, VEC_W])
        rows = sb("rows", [P, ROW_W])
        mats = sb("mats", [P, MAT_W])
        ub = sb("ub", [P, 8, G])
        ubs = sb("ubs", [P, 8, G])
        ctxT = sb("ctxT", [P, B, SK])
        expert_b = sb("expert_b", [E8, D])
        wq8_words = sb("wq8", [P, D // 4], I32)
        wq8 = wq8_words[:, :].bitcast(I8)
        wqb = sb("wqb", [P, D], BF)
        stats = sb("stats", [P, NI, 6])
        mv = sb("mv", [P, NI, 2])
        ve = sb("ve", [P, NI])
        rstd = Ring([sb(f"rstd{n}", [P, NI]) for n in range(2)])
        recip = sb("recip", [P, NI * HG])
        comb = sb("comb", [P, NT, E8])
        small = sb("small", [P, 16])
        maxima = sb("maxima", [P, NI, HG])

        def const(name):
            a, w = CONST_COLS[name]
            return cst[:, a:a + w]

        ident = const("ident")
        wide = Ring([pr.psum(f"wide{n}", [P, 2 * S]) for n in range(3)])
        acc = Ring([pr.psum(f"acc{n}", [P, S]) for n in range(2)])

        def mm(out, lhsT, rhs, *after, start=True, stop=True, signal=False, turn=False):
            return pe.do(lambda e: e.matmul(out, lhsT, rhs, start=start, stop=stop, is_transpose=turn),
                         *after, signal=signal)

        def v_tt(out, a, b, op, *after, line=dve):
            return line.do(lambda e: e.tensor_tensor(out, a, b, op), *after)

        def v_ts(out, a, s1, s2, op0, op1=None, *after, line=dve):
            if op1 is None:
                return line.do(lambda e: e.tensor_scalar(out, a, s1, None, op0), *after)
            return line.do(lambda e: e.tensor_scalar(out, a, s1, s2, op0, op1), *after)

        def v_stt(out, a, s, b, op0, op1, *after):
            return dve.do(lambda e: e.scalar_tensor_tensor(out=out, in0=a, scalar=s, in1=b, op0=op0, op1=op1), *after)

        def v_red(out, a, op, *after, negate=False, mag=False):
            return dve.do(lambda e: e.tensor_reduce(out, a, AX.X, op, negate=negate, apply_absolute_value=mag), *after)

        def v_copy(out, a, *after, line=dve):
            return line.do(lambda e: e.tensor_copy(out, a), *after)

        def a_act(out, a, func, *after, bias=0.0, scale=1.0):
            return act.do(lambda e: e.activation(out, a, func, bias=bias, scale=scale), *after)

        def a_copy(out, a, *after, scale=1.0):
            return a_act(out, a, ACT.Copy, *after, scale=scale)

        def zero(ap, *after, value=0.0, line=pool):
            return line.do(lambda e: e.memset(ap, value), *after)

        def load(name, pairs, *after):
            sem = pr.semaphore(f"load_{name}")
            sync.wait(*after)
            for dst, src in pairs:
                sync.todo.append(("do16", dst, src, sem))
            return (sem, pr.nsem, 16 * len(pairs))

        def spread(src, n, parts=P):
            return src.partition_broadcast(parts) if n else src

        ld_const = load("const", [(cst[:, :], io["consts"])])
        ld_small = load("small", [(ctxT[:, :, :], io["ctxT"]), (ub[:, :, :], io["unit_b"]),
                                  (vec[:, :], io["vecs"]), (mats[:, :], io["mats"]),
                                  (rows[:, :], spread(io["rows"], 1)), (expert_b[:, :], io["expert_b"]),
                                  (wq8_words[:, :], io["wq8"])])

        def load_unit(n, *after):
            s = unit_w.take()
            s.mark = load(f"unit{n}", [(s.buf[:, 0:U_BQ], io["unit_w"][n]),
                                       (s.buf[:, U_BQ:U_W], spread(io["unit_rows"][n], 1))], s.busy, *after)
            return s

        def load_layer(n):
            s = layer_w.take()
            s.mark = load(f"layer{n}", [(s.buf[:, 0:L_BQKV], io["layer_w"][n]),
                                        (s.buf[:, L_BQKV:L_W], spread(io["layer_rows"][n], 1))], s.busy)
            return s

        m_in = hid.bufs[0][:, :, :].rearrange("p c s -> p (c s)")
        mask_raw = m_in[:, 0:NT * SC].bitcast(I32).rearrange("p (t k) -> p t k", t=NT)
        units = {0: load_unit(0)}
        ld_mask = load("mask", [(mask_raw, io["mask"].rearrange("b (i p) k -> p (b i) k", p=P))])
        ld_x = [load(f"x{b}", [(x[:, NI * b:NI * b + NI, :], io["x"][b].rearrange("(i p) d -> p i d", p=P))])
                for b in range(B)]
        units[1] = load_unit(1)
        ld_w0 = load("experts0", [(w1, io["w1"]), (w2, io["w2"])])
        experts3 = {}
        layers = {0: load_layer(0), 1: load_layer(1)}

        zeros = small[:, 0:1]
        blank = zero(zeros)
        made = [zero(vx[:, :, :, :])]
        for h in range(16):
            v_copy(kx[:, h, :], zeros.broadcast_to([P, B * SK]), blank)
        for n in range(2 * HG):
            a_copy(k_self.bufs[n // HG][:, n % HG, :], zeros.broadcast_to([P, S]), blank)
        made_act = act.last
        made = [zero(vx[:, :, :, VSUM:VSUM + 1], value=1.0)]
        for buf in o_tok.bufs:
            made.append(zero(buf[:, :, :]))
        made_pool = made[-1]
        v_copy(ident_b[:, :], ident, ld_const)
        v_copy(causal_b[:, 0:P], const("causal"))
        v_copy(causal_b[:, P:2 * P], const("causal_t"))
        v_copy(cumul_b[:, 0:P], const("cumul"))
        zero(cumul_b[:, P:2 * P], value=1.0, line=dve)
        v_copy(wqb[:, :], wq8, ld_small)
        for n in range(8):
            made_dve = v_ts(ubs[:, n, :], ub[:, n, :], const("kscale4" if n in (1, 2) else "kscale8"), None,
                            ALU.mult, None)
        for line in (pe, act, pool, dve):
            line.wait(made_act, ld_const, ld_small, made_pool, made_dve)
        x_at = {b: [ld_x[b]] for b in range(B)}
        y_at = {b: [] for b in range(B)}
        hT_free = {b: [] for b in range(B)}

        def tiles(buf, b):
            return buf[:, NI * b:NI * b + NI, :]

        def normalise(src, dst, eps, rms, *after):
            for i in range(NI):
                dve.do(lambda e, i=i: e.bn_stats(stats[:, i, :], src[:, i, :]), *after)
            for i in range(NI):
                dve.do(lambda e, i=i: e.bn_aggr(mv[:, i, :], stats[:, i, :]))
            mean, var = mv[:, :, 0], mv[:, :, 1]
            if rms:
                v_tt(ve[:, :], mean, mean, ALU.mult)
                v_stt(ve[:, :], ve[:, :], eps, var, ALU.add, ALU.add)
            else:
                v_ts(ve[:, :], var, eps, None, ALU.add)
            r = rstd.take()
            ready = v_tt(r.buf[:, :], ve[:, :], const("minus_half"), ALU.pow, dve.last, r.busy, line=pool)
            for i in range(NI):
                if rms:
                    done = v_ts(dst[:, i, :], src[:, i, :], r.buf[:, i:i + 1], None, ALU.mult, None, ready)
                else:
                    done = v_ts(dst[:, i, :], src[:, i, :], mv[:, i, 0:1], r.buf[:, i:i + 1],
                                ALU.subtract, ALU.mult, ready)
            r.read_by(done)
            return done

        def turn_batch(src, b, *after, scale=None, shift=None, dst=None, busy=None):
            s = wide.take()
            for i in range(NI):
                m = mm(s.buf[:, P * i:P * i + P], src[:, i, :], ident, *after, s.busy, signal=i == NI - 1, turn=True)
            out = hT[:, b, :] if dst is None else dst
            wait = [m] + (hT_free[b] if busy is None else busy)
            if scale is None:
                done = a_copy(out, s.buf[:, 0:S], wait)
            elif shift is None:
                done = a_copy(out, s.buf[:, 0:S], wait, scale=scale)
            else:
                done = a_act(out, s.buf[:, 0:S], ACT.Identity, wait, bias=shift, scale=scale)
            s.read_by(done)
            return m, done

        mask_free = [[]]

        def turn_masks(*after):
            for b in range(B):
                s = wide.take()
                for i in range(NI):
                    m = mm(s.buf[0:SC, P * i:P * i + P], bias_q[:, NI * b + i, 0:SC], ident_b[:, :], *after, s.busy,
                           signal=i == NI - 1)
                done = a_copy(bias_k[0:SC, b, :], s.buf[0:SC, 0:S], m, mask_free[0])
                s.read_by(done)
            return [m, done]

        def project_out(ot, ready, w, bias, stream, at, b):
            s = oT.take()
            m, done = turn_batch(ot.buf, b, *ready, dst=s.buf[:, :], busy=s.busy)
            ot.read_by(m)
            yield
            a = wide.take()
            for i in range(NI):
                m = mm(a.buf[:, P * i:P * i + P], s.buf[:, P * i:P * i + P], w, done, a.busy, signal=i == NI - 1)
            s.read_by(m)
            dst = tiles(stream, b)
            done = v_tt(dst, a.buf[:, 0:S].rearrange("p (i d) -> p i d", i=NI), dst, ALU.add, m, *at[b])
            a.read_by(done)
            if bias is not None:
                done = v_tt(dst, dst, bias.unsqueeze(1).broadcast_to([P, NI, D]), ALU.add, done, line=pool)
            at[b] = [done]
            yield

        def normalise_heads(ta, dh, ot, h0):
            v = ta.buf[:, 0:S].rearrange("p (t i r) -> p t i r", t=NI, i=HG)
            rc = recip[:, :].rearrange("p (t i) -> p t i", t=NI)
            dve.do(lambda e: e.reciprocal(rc, v[:, :, :, VSUM]), ta.mark)
            out = ot.buf[:, :, h0 * dh:(h0 + HG) * dh].rearrange("p t (i r) -> p t i r", i=HG)
            done = v_tt(out, v[:, :, :, 0:dh], rc.unsqueeze(3).broadcast_to([P, NI, HG, dh]), ALU.mult, ot.busy)
            ta.read_by(done)
            return done

        def group_out(a, m, dh, ot, h0):
            s = oT.take()
            done = a_copy(s.buf[:, :], a.buf[:, :], m, s.busy)
            a.read_by(done)
            yield
            t = wide.take()
            for i in range(NI):
                t.mark = mm(t.buf[:, P * i:P * i + P], s.buf[:, P * i:P * i + P], ident, done, t.busy,
                            signal=i == NI - 1, turn=True)
            s.read_by(t.mark)
            yield
            ot.done = normalise_heads(t, dh, ot, h0)

        def high_part(out, src, *after):
            return dve.do(lambda e: e.tensor_scalar(out.bitcast(I32), src.bitcast(I32), HIGH, None,
                                                    ALU.bitwise_and), *after)

        def queries_in_parts(src, qt, *after):
            high, copy, low = (qt.buf[:, :, :, PART * n:PART * n + src.shape[3]] for n in range(3))
            tail = zero(qt.buf[:, :, :, MROW:HR], qt.busy)
            done = high_part(high, src, *after, qt.busy)
            twin = v_copy(copy, high, done, line=pool)
            return [v_tt(low, src, high, ALU.subtract), twin, tail]

        def token_queries():
            s = hid.take()
            s.buf = s.buf[:, :, :].rearrange("p t (h r) -> p t h r", h=16)
            return s

        def turn_queries(qt, g, n, q, *after):
            s = wide.take()
            for k in range(n):
                h = HG * (g + k)
                for i in range(NI):
                    m = mm(s.buf[:, S * k + P * i:S * k + P * i + P],
                           qt.buf[:, i, h:h + HG, :].rearrange("p h r -> p (h r)"), ident, *after, s.busy,
                           signal=(k, i) == (n - 1, NI - 1), turn=True)
            done = a_copy(q.buf[:, 0:n, :].rearrange("p k s -> p (k s)"), s.buf[:, 0:S * n], m, q.busy)
            s.read_by(done)
            return m, done

        def maxima_to_queries(qt, g):
            h = HG * g
            v = qt.buf[:, :, h:h + HG, :]
            high_part(v[:, :, :, MROW], maxima[:, :, :])
            return v_tt(v[:, :, :, MROW + 1], maxima[:, :, :], v[:, :, :, MROW], ALU.subtract)

        kx_free, vx_free = [[]], [[]]

        rope_free = [[]]
        masks = {}

        def cross_unit(n, dh, src, at, masked, alibi, proj, bias_o, eps, scale_of, first_unit=True, rms=False):
            state = {}
            prepared = cross_unit.prepared

            def keys_values():
                w = state["w"] = units[n]
                for g in range(G):
                    s = wide.take()
                    m = mm(s.buf[:, 0:B * SK], w.buf[:, U_WK + P * g:U_WK + P * g + P],
                           ctxT[:, :, :].rearrange("p b k -> p (b k)"), w.mark, s.busy, signal=True)
                    whole, high = rope_b[:, 0:B * SK], rope_b[:, B * SK:2 * B * SK]
                    v_ts(whole, s.buf[:, 0:B * SK], const("kscale4" if dh == 4 else "kscale8"), ubs[:, n, g:g + 1],
                         ALU.mult, ALU.add, m, rope_free[0])
                    s.read_by(dve.last)
                    if alibi:
                        w3 = whole.rearrange("p (b k) -> p b k", b=B)
                        v_tt(w3, w3, k_extra[:, g:g + 1, :].broadcast_to([P, B, SK]), ALU.add, *state["extra"])
                    high_part(high, whole)
                    v_ts(whole, whole, const("pick")[:, 0:1], None, ALU.mult)
                    for i in range(HG):
                        r = slice(HR * i, HR * i + HR)
                        v_stt(kx[r, HG * g + i, :], high[r, :], const("pick")[r, 1:2], whole[r, :], ALU.mult,
                              ALU.add, kx_free[0])
                    yield
                s = wide.take()
                for b in range(B):
                    m = mm(s.buf[0:SC, P * b:P * b + P], ctxT[:, b, 0:SC], w.buf[:, U_WV:U_WV + P], w.mark, s.busy,
                           signal=b == B - 1)
                pv = s.buf[0:SC, 0:S].rearrange("p (b h r) -> p b h r", b=B, h=D // dh)[:, :, 0:16, :]
                bv = w.buf[0:SC, U_BV:U_BV + 16 * dh].rearrange("p (h r) -> p h r", h=16)
                for b in range(B):
                    state["kv"] = v_tt(vx[0:SC, b, :, 0:dh], pv[:, b, :, :], bv, ALU.add, m, vx_free[0])
                s.read_by(state["kv"])
                rope_free[0] = [state["kv"]]
                yield

            def scores(b):
                if b == 0:
                    if alibi:
                        state["extra"] = cross_unit.extra
                    yield from keys_values()
                w = state["w"]
                if first_unit:
                    h = hn.take()
                    done = normalise(tiles(src, b), h.buf, eps, rms, *at[b], h.busy)
                    yield
                    yield
                    m, prepared[b] = turn_batch(h.buf, b, done, scale=scale_of)
                    h.read_by(m)
                    yield
                s = wide.take()
                for i in range(NI):
                    m = mm(s.buf[:, P * i:P * i + P], hT[:, b, P * i:P * i + P], w.buf[:, U_WQ:U_WQ + P], w.mark,
                           prepared[b], s.busy, signal=i == NI - 1)
                hT_free[b] = [m]
                whole = qkv[:, :, 0:D]
                done = v_tt(whole, s.buf[:, 0:S].rearrange("p (i d) -> p i d", i=NI),
                            w.buf[:, U_BQ:U_BQ + D].unsqueeze(1).broadcast_to([P, NI, D]), ALU.add, m)
                s.read_by(done)
                qt = token_queries()
                ready = queries_in_parts(whole.rearrange("p t (h r) -> p t h r", r=dh)[:, :, 0:16, :], qt)
                if alibi:
                    zero(qt.buf[:, :, :, KROW:KROW + 1], value=1.0)
                    ready = [ready, v_copy(qt.buf[:, :, :, QROW], const("position").unsqueeze(2)
                                           .broadcast_to([P, NI, 16]), line=pool)]
                yield
                pairs = [q_g.take() for _ in range(G // 2)]
                state["q", b] = pairs
                for pair in range(G // 2):
                    _, pairs[pair].turned = turn_queries(qt, 2 * pair, 2, pairs[pair], *ready)
                    yield

                def full(pair):
                    pairs[pair].busy = []
                    return turn_queries(qt, 2 * pair, 2, pairs[pair], state["max", b, 2 * pair + 1])

                for g in range(G):
                    q = pairs[g // 2]
                    for half in range(2):
                        s = wide.take()
                        for tt in range(2):
                            t = 2 * half + tt
                            bank = s.buf[:, S * tt:S * tt + HG * SK]
                            if masked:
                                mm(bank.rearrange("p (i k) -> p i k", i=HG), ident_b[:, :],
                                   bias_q[:, NI * b + t:NI * b + t + 1, :].broadcast_to([P, HG, SK]),
                                   masks[masked], s.busy, stop=False)
                            m = mm(bank.rearrange("p (i k) -> p i k", i=HG),
                                   q.buf[:, g % 2, P * t:P * t + P],
                                   kx[:, HG * g:HG * g + HG, SK * b:SK * b + SK], q.turned, s.busy,
                                   state["kv"], start=not masked, signal=tt == 1)
                        v = s.buf[:, :].rearrange("p (t c) -> p t c", t=2)[:, :, 0:HG * SK]\
                            .rearrange("p t (i k) -> p t i k", i=HG)[:, :, :, 0:SC]
                        top = v_red(maxima[:, 2 * half:2 * half + 2, :], v, ALU.max, m, negate=True)
                        s.read_by(top)
                        if half == 1:
                            state["max", b, g] = maxima_to_queries(qt, g)
                        if (g, half) == (2, 0):
                            _, pairs[0].full = full(0)
                        yield
                m, pairs[1].full = full(1)
                qt.read_by(m, dve.last)
                yield

            def attend(b):
                w = state["w"]
                ot = o_tok.take()
                pairs = state["q", b]
                pend, sums, out = None, None, iter(())
                for step in [(g, hp) for g in range(G) for hp in range(HG // 2)] + [None]:
                    nxt = None
                    if step:
                        g, hp = step
                        q = pairs[g // 2]
                        s = wide.take()
                        for ii in range(2):
                            i = 2 * hp + ii
                            bank = s.buf[0:SC, S * ii:S * ii + S]
                            if masked:
                                mm(bank, ident_b[0:SC, 0:SC], bias_k[0:SC, b, :], masks[masked], s.busy, stop=False)
                            m = mm(bank, kx[:, HG * g + i, SK * b:SK * b + SC],
                                   q.buf[:, g % 2, :], q.full, s.busy, start=not masked, signal=ii == 1)
                        if (g % 2, hp) == (1, HG // 2 - 1):
                            q.read_by(m)
                        pb = prob.take()
                        e = a_act(pb.buf[0:SC, :], s.buf[0:SC, :], ACT.Exp, m, pb.busy)
                        s.read_by(e)
                        nxt = (g, hp, pb, e)
                    next(out, None)
                    if pend:
                        g, hp, pb, e = pend
                        if hp == 0:
                            a = acc.take()
                        for ii in range(2):
                            i = 2 * hp + ii
                            m = mm(a.buf[HR * i:HR * i + HR, :], vx[0:SC, b, HG * g + i, :],
                                   pb.buf[0:SC, S * ii:S * ii + S], e, a.busy, state["kv"], signal=ii == 1)
                        pb.read_by(m)
                        if hp == 1:
                            for _ in out:
                                pass
                            out = group_out(a, m, dh, ot, HG * g)
                    pend = nxt
                    yield
                state["out", b] = (out, ot)
                if b == B - 1:
                    kx_free[0] = vx_free[0] = [m]
                    if masked or alibi:
                        mask_free[0] = [m, pool.last]

            def finish(b):
                w = state["w"]
                out, ot = state["out", b]
                yield from out
                if proj:
                    yield from project_out(ot, [ot.done], w.buf[:, U_WO:U_WO + P],
                                           w.buf[:, U_BO:U_BO + P] if bias_o else None, src if rms else x,
                                           at if rms else x_at, b)
                else:
                    dst = tiles(x, b)
                    done = v_tt(dst, dst, ot.buf[:, :, :], ALU.add, ot.done, *x_at[b], line=pool)
                    ot.read_by(done)
                    x_at[b] = [done]
                if b == B - 1:
                    w.read_by(pe.last, pool.last, dve.last)
                    if n in load_after:
                        for k in load_after[n]:
                            units[k] = load_unit(k)

            return [((lambda b=b: scores(b)), (lambda b=b: attend(b)), (lambda b=b: finish(b)))
                    for b in range(B)]

        load_after = {0: [2], 1: [3], 2: [4], 3: [5], 4: [6], 5: [7]}
        cross_unit.prepared = {}

        stage("l0_attn")
        cleared = zero(bias_q[:, :, :])
        done = v_ts(bias_q[:, :, 0:SC], mask_raw, 0.0, NEG, ALU.is_equal, ALU.mult, ld_mask, cleared)
        hid.free[0] = [done]
        masks["l0"] = turn_masks(done)
        pipeline(cross_unit(0, 8, x, x_at, "l0", False, False, False, 1e-5, None))

        stage("l0_ffn")

        def ffn0_first(b, st):
            h1, h2 = hn.take(), hn.take()
            done1 = normalise(tiles(x, b), h1.buf, 1e-5, False, *x_at[b], h1.busy)
            yield
            st["x1T"] = st["ln"] = prob.take()
            m, st["x1"] = turn_batch(h1.buf, b, done1, dst=st["x1T"].buf[:, 0:S], busy=st["x1T"].busy)
            done2 = normalise(h1.buf, h2.buf, 1e-5, False, done1, h2.busy)
            h1.read_by(m, done2)
            yield
            m, ln = turn_batch(h2.buf, b, done2, scale=vec[:, V_LNG:V_LNG + 1], shift=vec[:, V_LNB:V_LNB + 1],
                               dst=st["ln"].buf[:, S:2 * S], busy=st["ln"].busy)
            h2.read_by(m)
            a = wide.take()
            m = mm(a.buf[:, 0:S], mats[:, M_ATT:M_ATT + P], st["ln"].buf[:, S:2 * S], ln, a.busy, signal=True)
            st["xa"] = v_stt(hT[:, b, :], a.buf[:, 0:S], vec[:, V_ATTB:V_ATTB + 1], st["x1T"].buf[:, 0:S], ALU.add,
                             ALU.add, m, st["x1"], *hT_free[b])
            a.read_by(st["xa"])
            st["x1T"].read_by(m, st["xa"])
            yield

        def ffn0_second(b, st):
            out = acc.take()
            y2 = prob.take()
            for i in range(NI):
                e = (NI * b + i) % E8
                s = wide.take()
                for c in range(4):
                    m = mm(s.buf[:, P * c:P * c + P], w1[:, e, P * c:P * c + P], hT[:, b, P * i:P * i + P],
                           ld_w0, st["xa"], s.busy, signal=c == 3)
                h = hid.take()
                for c in range(4):
                    k = V_B1 + 4 * e + c
                    g = a_act(h.buf[:, c, 0:P], s.buf[:, P * c:P * c + P], ACT.Gelu, m, h.busy, bias=vec[:, k:k + 1])
                s.read_by(g)
                yield
                s = wide.take()
                for c in range(4):
                    m = mm(s.buf[:, 0:P], w2[:, e, c, :], h.buf[:, c, 0:P], g, s.busy, start=c == 0, stop=c == 3,
                           signal=c == 3)
                h.read_by(m)
                ydone = v_ts(y2.buf[:, P * i:P * i + P], s.buf[:, 0:P], vec[:, V_B2 + e:V_B2 + e + 1], None, ALU.add,
                             None, m, y2.busy)
                s.read_by(ydone)
                m = mm(out.buf[:, P * i:P * i + P], y2.buf[:, P * i:P * i + P], mats[:, M_NEXT:M_NEXT + P], ydone,
                       out.busy, signal=True)
                yield
            hT_free[b] = [m]
            y2.read_by(m)
            st["w_read"] = m
            h = hid.take()
            hv = h.buf[:, 0, :].rearrange("p (i d) -> p i d", i=NI)
            nb = rows[:, R_NEXTB:R_NEXTB + P].unsqueeze(1).broadcast_to([P, NI, D])
            done = v_tt(hv, out.buf[:, :].rearrange("p (i d) -> p i d", i=NI), nb, ALU.add, m, h.busy)
            out.read_by(done)
            g = a_act(h.buf[:, 1, :], h.buf[:, 0, :], ACT.Gelu, done)
            dst = tiles(x, b)
            done = v_tt(dst, dst, h.buf[:, 1, :].rearrange("p (i d) -> p i d", i=NI), ALU.add, g, *x_at[b],
                        line=pool)
            h.read_by(done)
            x_at[b] = [done]
            yield

        sts = [{} for _ in range(B)]
        pipeline([((lambda b=b: ffn0_first(b, sts[b])), (lambda b=b: ffn0_second(b, sts[b]))) for b in range(B)])
        w0_read = sts[B - 1]["w_read"]

        stage("l1_attn")
        raw = hid.take()
        words = raw.buf[:, 0, :].bitcast(I32)
        am_w = words[:, 0:NI * MASK_W].rearrange("p (i w) -> p i w", i=NI)
        pm_w = words[:, NI * MASK_W:(NI + B) * MASK_W].rearrange("p (b w) -> p b w", b=B)
        am = raw.buf[:, 0, 0:NI * MASK_W].bitcast(U8).rearrange("p (i k) -> p i k", i=NI)[:, :, 0:SC]
        pm = raw.buf[:, 0, NI * MASK_W:(NI + B) * MASK_W].bitcast(U8)\
            .rearrange("p (b k) -> p b k", b=B)[:, :, 0:SC]
        mm_f = raw.buf[:, 1:4, :].rearrange("p c s -> p (c s)")[:, 0:NT * SC].rearrange("p (b i k) -> p b i k", b=B, i=NI)
        ld_m1 = load("masks1", [(am_w, io["attn_mask"].rearrange("(i p) k -> p i k", p=P)),
                                (pm_w, spread(io["pad_mask"], 1))], raw.busy)
        for b in range(B):
            done = v_tt(mm_f[:, b, :, :], am, pm[:, b:b + 1, :].broadcast_to([P, NI, SC]), ALU.max, ld_m1)
        done = v_ts(bias_q[:, :, 0:SC], mm_f.rearrange("p b i k -> p (b i) k"), 0.0, NEG, ALU.is_gt, ALU.mult,
                    mask_free[0])
        raw.read_by(done)
        masks["l1"] = turn_masks(done)
        ld_w1 = load("experts1", [(gate1, io["gate1"]), (up1, io["up1"]), (down1, io["down1"])], w0_read)
        pipeline(cross_unit(1, 4, x, x_at, "l1", False, True, False, 1e-5, None)
                 + [None] + cross_unit(2, 4, x, x_at, "l1", False, True, True, 1e-5, None, first_unit=False))

        stage("l1_ffn")
        logits = acc.take()
        for b in range(B):
            h = hn.take()
            done = normalise(tiles(x, b), h.buf, 1e-5, False, *x_at[b], h.busy)
            m, done = turn_batch(h.buf, b, done)
            h.read_by(m)
            sts[b]["h"] = done
            for i in range(NI):
                t = NI * b + i
                m = mm(logits.buf[:, E8 * t:E8 * t + E8], hT[:, b, P * i:P * i + P], mats[:, M_GATE:M_GATE + E8],
                       done, logits.busy, signal=(b, i) == (B - 1, NI - 1))

        work = hid.take()
        wk = work.buf[:, :, :].rearrange("p c s -> p (c s)")
        taken = [0]

        def piece(n, dt=F32):
            a = taken[0]
            taken[0] += n
            return wk[:, a:a + n]

        def softmax8(lg, n, prob_out, mx, *after):
            v_red(mx, lg, ALU.max, *after)
            v_tt(prob_out, lg, mx.unsqueeze(2).broadcast_to([P, n, E8]), ALU.subtract)
            a_act(prob_out, prob_out, ACT.Exp, dve.last)
            v_red(mx, prob_out, ALU.add, act.last)
            dve.do(lambda e: e.reciprocal(mx, mx))
            return v_tt(prob_out, prob_out, mx.unsqueeze(2).broadcast_to([P, n, E8]), ALU.mult)

        def first_max(pv, n, mx, c, hot):
            v_red(mx, pv, ALU.max)
            v_tt(c, pv, mx.unsqueeze(2).broadcast_to([P, n, E8]), ALU.is_equal)
            v_tt(c, c, const("rev").unsqueeze(1).broadcast_to([P, n, E8]), ALU.mult)
            v_red(small[:, 0:n], c, ALU.max)
            return v_tt(hot, c, small[:, 0:n].unsqueeze(2).broadcast_to([P, n, E8]), ALU.is_equal)

        W8 = NT * E8
        lv = logits.buf[:, 0:W8].rearrange("p (t e) -> p t e", e=E8)
        probs = piece(W8).rearrange("p (t e) -> p t e", e=E8)
        cand = piece(W8).rearrange("p (t e) -> p t e", e=E8)
        hot = piece(2 * W8).rearrange("p (k t e) -> p k t e", k=2, e=E8)
        tops = piece(2 * NT).rearrange("p (k t) -> p k t", k=2)
        rank = piece(2 * W8)
        before = piece(2 * W8)
        tot = piece(2 * W8)
        hot_b = piece(W8).bitcast(BF)
        dve.wait(work.busy)
        act.wait(work.busy)
        softmax8(lv, NT, probs, tops[:, 0, :], m)
        logits.read_by(dve.last)
        first_max(probs, NT, tops[:, 0, :], cand, hot[:, 0])
        v_tt(cand, hot[:, 0], probs, ALU.mult)
        v_tt(probs, probs, cand, ALU.subtract)
        v_tt(probs, probs, hot[:, 0], ALU.subtract)
        first_max(probs, NT, tops[:, 1, :], cand, hot[:, 1])
        v_tt(small[:, 0:NT], tops[:, 0, :], tops[:, 1, :], ALU.add)
        v_ts(small[:, 0:NT], small[:, 0:NT], 1e-9, None, ALU.add)
        dve.do(lambda e: e.reciprocal(small[:, 0:NT], small[:, 0:NT]))
        v_tt(tops, tops, small[:, 0:NT].unsqueeze(1).broadcast_to([P, 2, NT]), ALU.mult)
        hf = hot.rearrange("p k t e -> p (k t e)")
        hb = v_copy(hot_b, hf)
        s = wide.take()
        mm(s.buf[:, 0:2 * W8], cumul_b[:, 0:P], hot_b, hb, s.busy)
        m = mm(s.buf[:, S:S + 2 * W8], cumul_b[:, P:2 * P], hot_b, signal=True)
        v_copy(rank, s.buf[:, 0:2 * W8], m)
        v_copy(tot, s.buf[:, S:S + 2 * W8])
        s.read_by(dve.last)
        r4, b4, t4 = (v.rearrange("p (k t e) -> p k t e", k=2, e=E8) for v in (rank, before, tot))
        zero(b4[:, :, 0, :], line=dve)
        for t in range(1, NT):
            v_tt(b4[:, :, t, :], b4[:, :, t - 1, :], t4[:, :, t - 1, :], ALU.add)
        v_tt(rank, rank, before, ALU.add)
        v_ts(rank, rank, float(CAP) + 0.5, None, ALU.is_lt)
        v_tt(rank, rank, hf, ALU.mult)
        for k in range(2):
            v_tt(r4[:, k], r4[:, k], tops[:, k, :].unsqueeze(2).broadcast_to([P, NT, E8]), ALU.mult)
        combined = v_tt(comb[:, :, :], r4[:, 0], r4[:, 1], ALU.add)
        work.read_by(combined)

        def ffn1_step(b, e):
            def first():
                h = hid.take()
                sts[b]["hid"] = h
                for c in range(2):
                    s = wide.take()
                    mm(s.buf[:, 0:S], gate1[:, e, P * c:P * c + P], hT[:, b, :], ld_w1, sts[b]["h"], s.busy)
                    m = mm(s.buf[:, S:2 * S], up1[:, e, P * c:P * c + P], hT[:, b, :], signal=True)
                    g = a_act(h.buf[:, c, :], s.buf[:, 0:S], ACT.Silu, m, h.busy)
                    done = v_tt(h.buf[:, c, :], s.buf[:, S:2 * S], h.buf[:, c, :], ALU.mult, g)
                    s.read_by(done)
                    yield
                h.done = done
                hT_free[b] = [m]
                st_h[b, e] = h

            def second():
                h = st_h[b, e]
                a = acc.take()
                for i in range(NI):
                    for c in range(2):
                        m = mm(a.buf[:, P * i:P * i + P], h.buf[:, c, P * i:P * i + P], down1[:, e, c, :], h.done,
                               a.busy, start=c == 0, stop=c == 1, signal=(i, c) == (NI - 1, 1))
                    if i == 1:
                        yield
                h.read_by(m)
                for i in range(NI):
                    t = NI * b + i
                    done = v_stt(x[:, t, :], a.buf[:, P * i:P * i + P], comb[:, t, e:e + 1], x[:, t, :], ALU.mult,
                                 ALU.add, m, *x_at[b])
                x_at[b] = [done]
                a.read_by(done)
                st_h["w_read"] = m
                yield
            return first, second

        st_h = {}
        pipeline([ffn1_step(b, e) for b in range(B) for e in range(E8)])
        zero(A[:, 0:6144], st_h["w_read"])
        zero(k_tok[:, :, :, MROW:MROW + 2], value=1.0)
        for buf in v_self.bufs:
            cleared = zero(buf[:, :, :, VSUM:VSUM + 1], value=1.0)

        stage("l2_attn")
        cross_unit.extra = [load("extras", [(k_extra, io["k_extra"])], mask_free[0])]
        pipeline(cross_unit(3, 8, x, x_at, "", True, True, True, 1e-5, None))

        stage("l2_ffn")

        def quant_first(b, st):
            h = hn.take()
            normalise(tiles(x, b), h.buf, 1e-5, False, *x_at[b], h.busy)
            xs = prob.take()
            st["xs"] = xs
            sc, inv = xs.buf[:, 0:NI], xs.buf[:, NI:2 * NI]
            v_red(sc, h.buf[:, :, :], ALU.max, xs.busy, mag=True)
            v_ts(sc, sc, 1e-6, 1.0 / 127.0, ALU.max, ALU.mult)
            dve.do(lambda e: e.reciprocal(inv, sc))
            for i in range(NI):
                v_ts(h.buf[:, i, :], h.buf[:, i, :], inv[:, i:i + 1], MAGIC, ALU.mult, ALU.add)
            v_ts(h.buf[:, :, :], h.buf[:, :, :], -MAGIC, -128.0, ALU.add, ALU.max)
            done = v_ts(h.buf[:, :, :], h.buf[:, :, :], 127.0, None, ALU.min)
            yield
            m, st["qd"] = turn_batch(h.buf, b, done, dst=xs.buf[:, S:S + S // 2].bitcast(BF), busy=xs.busy)
            h.read_by(m)
            yield

        def quant_second(b, st):
            a = acc.take()
            qb = st["xs"].buf[:, S:S + S // 2].bitcast(BF)
            for i in range(NI):
                m = mm(a.buf[:, P * i:P * i + P], qb[:, P * i:P * i + P], wqb[:, :], st["qd"], a.busy,
                       signal=i == NI - 1)
            h = hid.take()
            hv = h.buf[:, 0, :].rearrange("p (i d) -> p i d", i=NI)
            for i in range(NI):
                v_stt(hv[:, i, :], a.buf[:, P * i:P * i + P], st["xs"].buf[:, i:i + 1], rows[:, R_WS:R_WS + P],
                      ALU.mult, ALU.mult, m, h.busy)
            a.read_by(dve.last)
            st["xs"].read_by(m, dve.last)
            done = v_tt(hv, hv, rows[:, R_QB:R_QB + P].unsqueeze(1).broadcast_to([P, NI, D]), ALU.add)
            dst = tiles(x, b)
            done = v_tt(dst, dst, hv, ALU.add, done, *x_at[b], line=pool)
            h.read_by(done)
            x_at[b] = [done]
            yield

        pipeline([((lambda b=b: quant_first(b, sts[b])), (lambda b=b: quant_second(b, sts[b]))) for b in range(B)])

        stage("l3")
        raw = hid.take()
        seg_i = raw.buf[:, 3, 0:NT].bitcast(I32)
        seg = raw.buf[:, 3, NT:2 * NT]
        seg_lo = raw.buf[:, 3, 2 * NT:3 * NT]
        flat = raw.buf[:, 0:3, :].rearrange("p c s -> p (c s)")
        ld_seg = load("segments", [(seg_i, io["seg"])], raw.busy)
        late = flat[:, 0:NT * SC].rearrange("p (t k) -> p t k", t=NT)
        iota = const("iota").unsqueeze(1).broadcast_to([P, NT, SC])
        v_copy(seg, seg_i, ld_seg)
        v_ts(seg_lo, seg, -float(LOOKBACK), None, ALU.add)
        v_tt(late, iota, seg.unsqueeze(2).broadcast_to([P, NT, SC]), ALU.is_gt)
        empty = zero(bias_q[:, :, :], mask_free[0])
        v_tt(bias_q[:, :, 0:SC], iota, seg_lo.unsqueeze(2).broadcast_to([P, NT, SC]), ALU.is_le, mask_free[0], empty)
        v_tt(late, late, bias_q[:, :, 0:SC], ALU.max)
        done = v_ts(bias_q[:, :, 0:SC], late, NEG, None, ALU.mult)
        raw.read_by(done)
        masks["l3"] = turn_masks(done)
        for b in range(B):
            done = normalise(tiles(x, b), tiles(y, b), 1e-5, False, *x_at[b])
            y_at[b] = [done]

        tok_free = [[cleared]]
        v_self.free = [[cleared], [cleared]]

        def self_items(l):
            st = {}

            def project_in(b):
                w = st["w"] = layers[l]
                h = hn.take()
                done = normalise(tiles(y, b), h.buf, 1e-6, True, *y_at[b], h.busy)
                yield
                yield
                m, hd = turn_batch(h.buf, b, done, scale=vec[:, V_N1 + l:V_N1 + l + 1])
                h.read_by(m)
                yield
                for half in range(2):
                    s = wide.take()
                    for tt in range(2):
                        i = 2 * half + tt
                        m = mm(s.buf[:, S * tt:S * tt + 3 * D], hT[:, b, P * i:P * i + P],
                               w.buf[:, L_QKV:L_QKV + 3 * D], w.mark, hd, s.busy, signal=tt == 1)
                    v = s.buf[:, :].rearrange("p (t c) -> p t c", t=2)
                    bias = w.buf[:, L_BQKV:L_BQKV + 3 * D].unsqueeze(1).broadcast_to([P, 2, 3 * D])
                    v_tt(qkv[:, 2 * half:2 * half + 2, 0:2 * D], v[:, :, 0:2 * D], bias[:, :, 0:2 * D], ALU.add, m)
                    if half == 0:
                        st["v", b] = v_self.take()
                    for tt in range(2):
                        i = 2 * half + tt
                        st["v"] = v_tt(st["v", b].buf[:, i, :, 0:8], v[:, tt, 2 * D:3 * D].rearrange("p (h r) -> p h r", h=16),
                                       w.buf[:, L_BQKV + 2 * D:L_BQKV + 3 * D].rearrange("p (h r) -> p h r", h=16),
                                       ALU.add, st["v", b].busy)
                    s.read_by(dve.last)
                    yield
                st["v", b].mark = st["v"]
                hT_free[b] = [m]
                qk = qkv[:, :, 0:2 * D].rearrange("p t (h r) -> p t h r", r=8)
                rot = rope_b[:, :].rearrange("p (t h r) -> p t h r", t=NI, r=8)
                cs = const("cos").rearrange("p (t r) -> p t r", t=NI)
                sn = const("sin").rearrange("p (t r) -> p t r", t=NI)
                shape = [P, NI, 32, 4]
                v_tt(rot[:, :, :, 0:4], qk[:, :, :, 4:8], sn[:, :, 0:4].unsqueeze(2).broadcast_to(shape), ALU.mult,
                     rope_free[0])
                v_tt(rot[:, :, :, 4:8], qk[:, :, :, 0:4], sn[:, :, 4:8].unsqueeze(2).broadcast_to(shape), ALU.mult)
                yield
                v_tt(qk, qk, cs.unsqueeze(2).broadcast_to([P, NI, 32, 8]), ALU.mult)
                v_tt(rot, rot, qk, ALU.add)
                yield

            def cut_in(b):
                rot = rope_b[:, :].rearrange("p (t h r) -> p t h r", t=NI, r=8)
                q, k = rot[:, :, 0:16, :], rot[:, :, 16:32, :]
                qt = st["qt", b] = token_queries()
                ready = queries_in_parts(q, qt)
                high, low, copy = (k_tok[:, :, :, PART * n:PART * n + PART] for n in range(3))
                done = high_part(high, k, tok_free[0])
                twin = v_copy(copy, high, done, line=pool)
                done = v_tt(low, k, high, ALU.subtract)
                st["qk"] = ready + [twin, done]
                rope_free[0] = [done]
                yield

            def scores(b, g):
                if (b, g) == (0, 0):
                    yield from project_in(b)
                    yield from cut_in(b)
                qt = st["qt", b]
                q, kk = q_g.take(), k_self.take()
                st[b, g] = (q, kk)
                _, turned = turn_queries(qt, g, 1, q, *st["qk"])
                s = wide.take()
                for i in range(NI):
                    m = mm(s.buf[:, P * i:P * i + P],
                           k_tok[:, i, HG * g:HG * g + HG, :].rearrange("p h r -> p (h r)"), ident,
                           st["qk"], s.busy, signal=i == NI - 1, turn=True)
                if g == G - 1:
                    tok_free[0] = [m]
                done = [turned]
                for i in range(HG):
                    r = slice(HR * i, HR * i + HR)
                    if i % 2:
                        done.append(a_copy(kk.buf[r, i, :], s.buf[r, 0:S], m, kk.busy))
                    else:
                        done.append(v_copy(kk.buf[r, i, :], s.buf[r, 0:S], m, kk.busy))
                s.read_by(*done)
                yield
                for t in range(NI):
                    n = P * (t + 1)
                    per = HG if t < 2 else 2
                    for h0 in range(0, HG, per):
                        s = wide.take()
                        pitch = n if t < 2 else S
                        for i in range(h0, h0 + per):
                            at0 = pitch * (i - h0)
                            mm(s.buf[:, at0:at0 + n], q.buf[:, 0, P * t:P * t + P],
                               kk.buf[:, i, 0:n], *done, s.busy, stop=False)
                            m = mm(s.buf[:, at0 + n - P:at0 + n], ident_b[:, :], causal_b[:, 0:P], start=False,
                                   signal=i == h0 + per - 1)
                        v = s.buf[:, 0:pitch * per].rearrange("p (i k) -> p i k", i=per)[:, :, 0:n]
                        top = v_red(maxima[:, t, h0:h0 + per], v, ALU.max, m, negate=True)
                        s.read_by(top)
                        yield
                q.busy = []
                m, q.full = turn_queries(qt, g, 1, q, maxima_to_queries(qt, g))
                if g == G - 1:
                    qt.read_by(m)
                yield

            def attend(b, g):
                w = st["w"]
                q, kk = st[b, g]
                a = acc.take()
                if g == 0:
                    st["o", b] = o_tok.take()
                ot = st["o", b]
                steps = [(j, h0, HG if j > 1 else 2) for j in range(NI) for h0 in range(0, HG, HG if j > 1 else 2)]
                pend = None
                for step in steps + [None]:
                    nxt = None
                    if step:
                        j, h0, per = step
                        n = S - P * j
                        pitch = n if j > 1 else S
                        s = wide.take()
                        for i in range(h0, h0 + per):
                            at0 = pitch * (i - h0)
                            mm(s.buf[:, at0:at0 + n], kk.buf[:, i, P * j:P * j + P],
                               q.buf[:, 0, P * j:S], q.full, s.busy, stop=False)
                            m = mm(s.buf[:, at0:at0 + P], ident_b[:, :], causal_b[:, P:2 * P], start=False,
                                   signal=i == h0 + per - 1)
                        pb = prob.take()
                        sv = s.buf[:, 0:pitch * per].rearrange("p (i k) -> p i k", i=per)[:, :, 0:n]
                        pv = pb.buf[:, 0:n * per].rearrange("p (i k) -> p i k", i=per)
                        e = a_act(pv, sv, ACT.Exp, m, pb.busy, scale=8 ** -0.5)
                        s.read_by(e)
                        nxt = (j, h0, per, n, pb, pv, e)
                        if step == steps[-1]:
                            q.read_by(m)
                            kk.read_by(m)
                        yield
                    if pend:
                        j, h0, per, n, pb, pv, e = pend
                        for i in range(h0, h0 + per):
                            m = mm(a.buf[HR * i:HR * i + HR, P * j:S], st["v", b].buf[:, j, HG * g + i, :],
                                   pv[:, i - h0, :], e, a.busy, st["v", b].mark, start=j == 0, stop=j == NI - 1,
                                   signal=i == h0 + per - 1)
                        pb.read_by(m)
                    pend = nxt
                if g == G - 1:
                    st["v", b].read_by(m)
                st["out", b, g] = (a, m, ot)

            def finish(b, g):
                a, m, ot = st["out", b, g]
                w = st["w"]
                yield from group_out(a, m, 8, ot, HG * g)
                if g == G - 1:
                    yield from project_out(ot, [ot.done], w.buf[:, L_WO:L_WO + P], w.buf[:, L_BO:L_BO + P], y, y_at, b)

            def scores_and_next(b, g):
                side = iter(())
                if b + 1 < B:
                    if g == 1:
                        st["side"] = project_in(b + 1)
                    if g in (1, 2):
                        side = st["side"]
                    if g == 3:
                        side = cut_in(b + 1)
                for n, _ in enumerate(scores(b, g)):
                    if n:
                        next(side, None)
                    yield
                if g > 1:
                    for _ in side:
                        yield

            return [((lambda b=b, g=g: scores_and_next(b, g)), (lambda b=b, g=g: attend(b, g)),
                     (lambda b=b, g=g: finish(b, g))) for b in range(B) for g in range(G)]

        def ffn3(l, b):
            st = {}

            def turn():
                h = hn.take()
                done = normalise(tiles(y, b), h.buf, 1e-6, True, *y_at[b], h.busy)
                yield
                yield
                m, st["h"] = turn_batch(h.buf, b, done, scale=vec[:, V_N3 + l:V_N3 + l + 1])
                h.read_by(m)
                yield

            def hidden():
                w = layers[l]
                h = st["hid"] = hid.take()
                for c in range(4):
                    s = wide.take()
                    mm(s.buf[:, 0:S], w.buf[:, L_WG + P * c:L_WG + P * c + P], hT[:, b, :], st["h"], s.busy)
                    m = mm(s.buf[:, S:2 * S], w.buf[:, L_WU + P * c:L_WU + P * c + P], hT[:, b, :], signal=True)
                    g = a_act(h.buf[:, c, :], s.buf[:, 0:S], ACT.Silu, m, h.busy)
                    h.done = v_tt(h.buf[:, c, :], s.buf[:, S:2 * S], h.buf[:, c, :], ALU.mult, g)
                    s.read_by(h.done)
                    yield
                hT_free[b] = [m]

            def down():
                w, h = layers[l], st["hid"]
                done = h.done
                a = acc.take()
                for i in range(NI):
                    for c in range(4):
                        m = mm(a.buf[:, P * i:P * i + P], h.buf[:, c, P * i:P * i + P],
                               w.buf[:, L_WD + P * c:L_WD + P * c + P], done, a.busy, start=c == 0, stop=c == 3,
                               signal=(i, c) == (NI - 1, 3))
                    yield
                h.read_by(m)
                dst = tiles(y, b)
                done = v_tt(dst, a.buf[:, :].rearrange("p (i d) -> p i d", i=NI), dst, ALU.add, m, *y_at[b])
                a.read_by(done)
                y_at[b] = [done]
                if b == B - 1:
                    w.read_by(m)
                    if l + 2 < NL:
                        layers[l + 2] = load_layer(l + 2)
                    elif l + 2 == NL:
                        e3 = layer_w.take()
                        experts3["w"] = e3.buf[:, 0:E8 * D]
                        experts3["mark"] = load("experts3", [(experts3["w"], io["expert_w"])], e3.busy)
                yield
            return turn, hidden, down

        def named(name, items):
            def first(begin=items[0][0]):
                stage(name)
                yield from begin()
            return [(first, *items[0][1:])] + items[1:]

        every = []
        for l in range(NL):
            every += named(f"l3_self{l}", self_items(l))
            every += named(f"l3_cross{l}", cross_unit(4 + l, 8, y, y_at, "l3", False, True, False, 1e-6,
                                                      vec[:, V_N2 + l:V_N2 + l + 1], rms=True))
            every += named(f"l3_ffn{l}", [ffn3(l, b) for b in range(B)])
        pipeline(every)

        stage("l3_moe")

        def moe_first(b, st):
            h = hn.take()
            done = normalise(tiles(y, b), h.buf, 1e-6, True, *y_at[b], h.busy)
            v_tt(h.buf[:, :, :], h.buf[:, :, :], rows[:, R_NF:R_NF + P].unsqueeze(1).broadcast_to([P, NI, D]),
                 ALU.mult, done)
            dst = tiles(x, b)
            xd = v_tt(dst, dst, h.buf[:, :, :], ALU.add, *x_at[b])
            x_at[b] = [xd]
            done = normalise(dst, h.buf, 1e-5, False, xd)
            m, st["h"] = turn_batch(h.buf, b, done)
            h.read_by(m)
            yield
            s = wide.take()
            for i in range(NI):
                m = mm(s.buf[:, E8 * i:E8 * i + E8], hT[:, b, P * i:P * i + P], mats[:, M_ROUT:M_ROUT + E8], st["h"],
                       s.busy, signal=i == NI - 1)
            k = st["k"] = prob.take()
            W = NI * E8
            lg, pv, cand, hot, cf = (k.buf[:, W * n:W * n + W].rearrange("p (i e) -> p i e", e=E8) for n in range(5))
            mx = k.buf[:, 5 * W:5 * W + NI]
            v_tt(lg, s.buf[:, 0:W].rearrange("p (i e) -> p i e", e=E8),
                 rows[:, R_RB:R_RB + E8].unsqueeze(1).broadcast_to([P, NI, E8]), ALU.add, m, k.busy)
            s.read_by(dve.last)
            softmax8(lg, NI, pv, mx)
            first_max(pv, NI, mx, cand, hot)
            st["coef"] = v_tt(cf, hot, mx.unsqueeze(2).broadcast_to([P, NI, E8]), ALU.mult)
            st["cf"] = cf
            yield

        def moe_second(b, st):
            s = wide.take()
            for i in range(NI):
                m = mm(s.buf[0:E8, P * i:P * i + P], st["cf"][:, i, :], ident, st["coef"], s.busy,
                       signal=i == NI - 1, turn=True)
            c = prob.take()
            done = a_copy(c.buf[0:E8, 0:S], s.buf[0:E8, 0:S], m, c.busy)
            s.read_by(done)
            a = acc.take()
            for i in range(NI):
                m = mm(a.buf[:, P * i:P * i + P], c.buf[0:E8, P * i:P * i + P], expert_b[:, :], done, a.busy,
                       signal=i == NI - 1)
            c.read_by(m)
            dst = tiles(x, b)
            done = v_tt(dst, a.buf[:, :].rearrange("p (i d) -> p i d", i=NI), dst, ALU.add, m, *x_at[b])
            a.read_by(done)
            yield
            for i in range(NI):
                t = NI * b + i
                s = wide.take()
                mm(s.buf[:, 0:S], hT[:, b, P * i:P * i + P], experts3["w"][:, 0:S], experts3["mark"], st["h"], s.busy)
                m = mm(s.buf[:, S:2 * S], hT[:, b, P * i:P * i + P], experts3["w"][:, S:2 * S], signal=True)
                for e in range(E8):
                    done = v_stt(x[:, t, :], s.buf[:, D * e:D * e + D], st["cf"][:, i, e:e + 1], x[:, t, :],
                                 ALU.mult, ALU.add, m)
                s.read_by(done)
                yield
            st["k"].read_by(done)
            hT_free[b] = [m]
            out_sem = pr.semaphore(f"out{b}")
            sync.wait(done)
            sync.todo.append(("do16", io["out"][b].rearrange("(i p) d -> p i d", p=P), tiles(x, b), out_sem))
            stores.append(out_sem)
            yield

        stores = []
        sts = [{} for _ in range(B)]
        pipeline([((lambda b=b: moe_first(b, sts[b])), (lambda b=b: moe_second(b, sts[b]))) for b in range(B)])
        for sem in stores:
            sync.todo.append(("wait", sem, 16))

        block = ctx.enter_context(nc.Block())

        @block.sync
        def _(e):
            for entry in sync.todo:
                if entry[0] == "wait":
                    e.wait_ge(entry[1], entry[2])
                else:
                    e.dma_start(entry[1], entry[2]).then_inc(entry[3], 16)

        @block.tensor
        def _(e):
            pe.play(e)

        @block.vector
        def _(e):
            dve.play(e)

        @block.scalar
        def _(e):
            act.play(e)

        @block.gpsimd
        def _(e):
            pool.play(e)


def heads(w, dh):
    out = np.zeros((w.shape[0], 16, HR), w.dtype)
    for part in range(3):
        out[:, :, PART * part:PART * part + dh] = w.reshape(w.shape[0], 16, dh)
    return out.reshape(w.shape[0], 16 * HR)


def constants():
    c = np.zeros((P, CONST_W), np.float32)

    def put(name, v):
        a, w = CONST_COLS[name]
        c[:, a:a + w] = np.asarray(v).reshape(P, w) if np.ndim(v) > 1 else v

    r = np.arange(P)
    put("ident", np.eye(P))
    put("causal", np.where(r[None, :] > r[:, None], NEG, 0.0))
    put("causal_t", np.where(r[:, None] > r[None, :], NEG, 0.0))
    put("cumul", (r[:, None] <= r[None, :]).astype(np.float32))
    inv = (1.0 / np.float32(10000.0) ** (np.arange(0, 8, 2, dtype=np.float32) / np.float32(8))).astype(np.float32)
    ang = (np.arange(S, dtype=np.float32)[:, None] * inv[None, :]).astype(np.float32)
    ang = np.concatenate([ang, ang], 1)
    sign = np.array([-1.0] * 4 + [1.0] * 4, np.float32)
    put("cos", np.cos(ang).reshape(NI, P, 8).transpose(1, 0, 2).reshape(P, -1))
    put("sin", (np.sin(ang) * sign).reshape(NI, P, 8).transpose(1, 0, 2).reshape(P, -1))
    row = r % HR
    put("kscale8", np.where(row < MROW, 8 ** -0.5, 1.0)[:, None])
    put("kscale4", np.where(row < MROW, 4 ** -0.5, 1.0)[:, None])
    low = row // PART == 1
    put("pick", np.stack([low, 1.0 - 2.0 * low], 1))
    put("position", np.arange(S).reshape(NI, P).T)
    put("iota", np.tile(np.arange(SC, dtype=np.float32), (P, 1)))
    put("rev", np.tile(np.arange(E8, 0, -1, dtype=np.float32), (P, 1)))
    put("minus_half", np.full((P, NI), -0.5, np.float32))
    return c


def position_rows():
    slopes = 2.0 ** (-8 + np.arange(16))
    k = np.zeros((HG, HR, G, SK), np.float32)
    for g in range(G):
        for i in range(HG):
            k[i, KROW, g] = -slopes[HG * g + i] * np.arange(SK)
            k[i, QROW, g] = slopes[HG * g + i]
    return k.reshape(P, G, SK)


def mask_words(m):
    out = np.zeros((m.shape[0], 4 * MASK_W), np.uint8)
    out[:, :SC] = m.view(np.uint8)
    return out.view(np.int32)


def layout(i):
    z = np.zeros
    f = np.float32
    unit_w, unit_b, unit_rows = z((8, P, U_BQ), f), z((P, 8, G), f), z((8, U_W - U_BQ), f)

    def unit(n, dh, wq, wk, wv, bq, bk, bv, wo, bo):
        unit_w[n, :, U_WK:U_WK + 512] = heads(wk, dh)
        unit_w[n, :, U_WQ:U_WQ + wq.shape[1]] = wq
        unit_w[n, :, U_WV:U_WV + wv.shape[1]] = wv
        if wo is not None:
            unit_w[n, :wo.shape[0], U_WO:U_WO + P] = wo
        kb = z((1, 16 * HR), f)
        if bq is not None:
            kb = heads(bk[None, :], dh)
            unit_rows[n, 0:bq.size] = bq
            unit_rows[n, P:P + bv.size] = bv
        kb = kb.reshape(G, HG, HR)
        kb[:, :, MROW:MROW + 2] = 1.0
        unit_b[:, n, :] = kb.reshape(G, P).T
        if bo is not None:
            unit_rows[n, 2 * P:] = bo

    unit(0, 8, i["L0_xattn_Wq"].T, i["L0_xattn_Wk"].T, i["L0_xattn_Wv"].T, i["L0_xattn_bq"], i["L0_xattn_bk"],
         i["L0_xattn_bv"], None, None)
    w, wb = i["L1_xattn_Wqkv"], i["L1_xattn_bqkv"]
    for u in range(2):
        c = slice(64 * u, 64 * u + 64)
        unit(1 + u, 4, w[:, :P][:, c], w[:, P:2 * P][:, c], w[:, 2 * P:][:, c], wb[:P][c], wb[P:2 * P][c],
             wb[2 * P:][c], i["L1_xattn_Wo"][c], i["L1_xattn_bo"])
    unit(3, 8, i["L2_xattn_Wq"].T, i["L2_xattn_Wk"].T, i["L2_xattn_Wv"].T, i["L2_xattn_bq"], i["L2_xattn_bk"],
         i["L2_xattn_bv"], i["L2_xattn_Wo"].T, i["L2_xattn_bo"])
    for l in range(NL):
        kv = i["L3_xattn_Wkv_c"][l]
        unit(4 + l, 8, i["L3_xattn_Wq_c"][l].T, kv[:P].T, kv[P:].T, None, None, None, i["L3_xattn_Wo_c"][l].T, None)

    layer_w, layer_rows = z((NL, P, L_BQKV), f), z((NL, L_W - L_BQKV), f)
    for l in range(NL):
        layer_w[l, :, L_QKV:L_QKV + 384] = i["L3_xattn_Wqkv"][l].T
        layer_w[l, :, L_WO:L_WO + P] = i["L3_xattn_Wo"][l].T
        layer_w[l, :, L_WG:L_WG + F0] = i["L3_xattn_Wg"][l].T
        layer_w[l, :, L_WU:L_WU + F0] = i["L3_xattn_Wu"][l].T
        layer_w[l, :, L_WD:L_WD + F0] = i["L3_xattn_Wd"][l].T.reshape(4, P, D).transpose(1, 0, 2).reshape(P, -1)
        layer_rows[l, 0:384] = i["L3_xattn_bqkv"][l]
        layer_rows[l, 384:] = i["L3_xattn_bo"][l]

    vecs = z((P, VEC_W), f)
    for at, name in ((V_N1, "L3_xattn_n1"), (V_N2, "L3_xattn_n2"), (V_N3, "L3_xattn_n3")):
        vecs[:, at:at + NL] = i[name].T
    for at, name in ((V_LNG, "L0_ffn_ln_g"), (V_LNB, "L0_ffn_ln_b"), (V_ATTB, "L0_ffn_attn_b")):
        vecs[:, at] = i[name]
    vecs[:, V_B1:V_B1 + 4 * E8] = i["L0_ffn_b1"].reshape(E8 * 4, P).T
    vecs[:, V_B2:V_B2 + E8] = i["L0_ffn_b2"].T
    rows = np.concatenate([i["L0_ffn_next_b"], i["L2_ffn_weight_scale"], i["L2_ffn_bias"], i["L3_xattn_nf"],
                           i["L3_ffn_router_b"]])
    mats = np.concatenate([i["L0_ffn_attn_w"], i["L0_ffn_next_w"], i["L1_ffn_gate_w"].T, i["L3_ffn_router_w"]], 1)
    ctxT = z((P, B, SK), f)
    ctxT[:, :, :SC] = i["ctx_1024"].transpose(2, 0, 1)
    return {
        "x": i["x"], "ctxT": ctxT, "mask": i["mask_BxSxS2_if1"],
        "attn_mask": mask_words(i["mask_SxS2_bk1"]), "pad_mask": mask_words(i["mask_BxS2_bk0"]),
        "seg": i["itok_BxS_0_255"].reshape(NT, P).T, "unit_w": unit_w, "unit_b": unit_b, "unit_rows": unit_rows,
        "layer_w": layer_w, "layer_rows": layer_rows, "vecs": vecs, "rows": rows, "mats": mats,
        "consts": constants(), "k_extra": position_rows(),
        "w1": i["L0_ffn_w1"].transpose(1, 0, 2),
        "w2": i["L0_ffn_w2"].reshape(E8, 4, P, D).transpose(2, 0, 1, 3),
        "gate1": i["L1_ffn_gate_proj_w"].transpose(2, 0, 1), "up1": i["L1_ffn_up_proj_w"].transpose(2, 0, 1),
        "down1": i["L1_ffn_down_proj_w"].transpose(2, 0, 1).reshape(2, P, E8, D).transpose(1, 2, 0, 3),
        "wq8": np.ascontiguousarray(i["L2_ffn_weight_q"].T).view(np.int32), "expert_w": i["L3_ffn_expert_w"].transpose(1, 0, 2).reshape(P, E8 * D),
        "expert_b": i["L3_ffn_expert_b"],
    }


def kernel(**inputs):
    import concourse.bacc as bacc
    from concourse.bass_utils import run_bass_kernel_spmd as run

    arrays = {f"in_{k}": np.ascontiguousarray(v)
              for k, v in layout({k: np.asarray(v) for k, v in inputs.items()}).items()}
    nc = bacc.Bacc("TRN2", target_bir_lowering=False, num_devices=1)
    io = {k[3:]: nc.dram_tensor(k, v.shape, mybir.dt.from_np(v.dtype), kind="ExternalInput").ap()
          for k, v in arrays.items()}
    io["out"] = nc.dram_tensor("out", (B, S, D), mybir.dt.float32, kind="ExternalOutput").ap()
    build(nc, io)
    return run(nc, [arrays], core_ids=[0]).results[0]["out"]
```

```python
import numpy as np
import concourse.bass as bass
from concourse import mybir
from contextlib import ExitStack
from itertools import zip_longest

P = 128
B, S, D = 4, 512, 128
NI = S // P
NT = B * NI
SC = 77
SK = SC + SC % 2
MASK_W = (SC + 3) // 4
G, HG, HR = 4, 4, 32
PART = 8
MROW, KROW, QROW = 24, 26, 27
VSUM = 8
HIGH = -(1 << 12)
NEG = -float(2 ** 100)
E8 = 8
F0 = 512
F1 = 256
CAP = int(1.25 * B * S / E8)
NL = 4
LOOKBACK = 128
MAGIC = 1.5 * 2 ** 23

CONST_COLS = {}
_at = 0
for _n, _w in (("ident", P), ("causal", P), ("cumul", P), ("cos", NI * 8), ("sin", NI * 8),
               ("kscale8", 1), ("kscale4", 1), ("pick", 2), ("position", NI), ("iota", SC), ("rev", E8), ("minus_half", NI)):
    CONST_COLS[_n] = (_at, _w)
    _at += _w
CONST_W = _at
V_N1, V_N2, V_N3, V_LNG, V_LNB, V_ATTB, V_B1, V_B2 = 0, 4, 8, 12, 13, 14, 15, 47
VEC_W = 55
R_NEXTB, R_WS, R_QB, R_NF, R_RB = 0, P, 2 * P, 3 * P, 4 * P
ROW_W = 4 * P + E8
U_WK, U_WQ, U_WV, U_WO, U_BQ, U_BV, U_BO, U_W = 0, 512, 640, 768, 896, 1024, 1152, 1280
L_QKV, L_WO, L_WG, L_WU, L_WD, L_BQKV, L_BO, L_W = 0, 384, 512, 1024, 1536, 2048, 2432, 2560
M_ATT, M_NEXT, M_GATE, M_ROUT, MAT_W = 0, 128, 256, 264, 272


class Line:

    def __init__(self, prog, name, chained):
        self.prog, self.name, self.chained = prog, name, chained
        self.todo, self.waited, self.last = [], {}, None
        self.part("start")

    def part(self, stage):
        self.sem, self.key = self.prog.semaphore(f"{self.name}_{stage}"), self.prog.nsem
        self.count = 0

    def wait(self, *marks):
        for m in marks:
            if m is None:
                continue
            if isinstance(m, list) or m and isinstance(m[0], (list, tuple)):
                self.wait(*m)
            elif self.waited.get(m[1], 0) < m[2]:
                self.waited[m[1]] = m[2]
                self.todo.append(("wait", m[0], m[2]))

    def do(self, what, *after, signal=True, apart=False):
        self.wait(*after)
        if self.chained and not apart:
            self.wait(self.last)
        if not signal:
            self.todo.append(("do", what, None))
            return None
        self.count += 1
        self.todo.append(("do", what, self.sem))
        self.last = (self.sem, self.key, self.count)
        return self.last

    def play(self, eng):
        for kind, a, n in self.todo:
            if kind == "wait":
                eng.wait_ge(a, n)
            elif n is None:
                a(eng)
            else:
                a(eng).then_inc(n, 1)


class Ring:

    def __init__(self, bufs):
        self.bufs, self.free, self.idle = bufs, [[] for _ in bufs], list(range(len(bufs)))

    def take(self):
        i = self.idle.pop(0)
        return Slot(self, i, self.bufs[i], self.free[i])


class Slot:
    def __init__(self, ring, i, buf, busy):
        self.ring, self.i, self.buf, self.busy = ring, i, buf, busy

    def read_by(self, *marks):
        assert self.i not in self.ring.idle
        self.ring.free[self.i] = list(marks)
        self.ring.idle.append(self.i)


class Prog:
    def __init__(self, nc, ctx):
        self.nc, self.ctx, self.nsem = nc, ctx, 0

    def semaphore(self, name):
        self.nsem += 1
        return self.ctx.enter_context(self.nc.semaphore(name))

    def sbuf(self, name, shape, dt=mybir.dt.float32):
        return self.ctx.enter_context(self.nc.sbuf_tensor(name, shape, dt))

    def psum(self, name, shape, dt=mybir.dt.float32):
        return self.ctx.enter_context(self.nc.psum_tensor(name, shape, dt))


def pipeline(items):
    live = []
    for item in items + [[]]:
        live.append((item, 0))
        while live:
            now = [phases[n]() for phases, n in reversed(live) if phases]
            for _ in zip_longest(*(now[:1] + now[3:] + now[1:3])):
                pass
            live = [(phases, n + 1) for phases, n in live if n + 1 < len(phases)]
            if item:
                break


def beside(*phases):
    def phase():
        for _ in zip_longest(*[p() for p in phases]):
            yield
    return phase


def idle():
    return iter(())


def build(nc, io):
    F32, BF, I32, FR = mybir.dt.float32, mybir.dt.bfloat16, mybir.dt.int32, mybir.dt.float32r
    U8, I8 = mybir.dt.uint8, mybir.dt.int8
    ALU, ACT, AX = mybir.AluOpType, mybir.ActivationFunctionType, mybir.AxisListType
    with ExitStack() as ctx:
        pr = Prog(nc, ctx)
        sb = pr.sbuf
        pe, dve, act, pool = (Line(pr, n, c) for n, c in (("pe", False), ("dve", True), ("act", False), ("pool", True)))
        sync = Line(pr, "sync", False)
        lines = (pe, dve, act, pool)

        def stage(name):
            for line in lines:
                line.part(name)

        A = sb("A", [P, 8192])
        w1 = A[:, 0:4096].rearrange("p (e f) -> p e f", e=E8)
        w2 = A[:, 4096:8192].rearrange("p (e c d) -> p e c d", e=E8, c=4)
        gate1 = A[:, 0:2048].rearrange("p (e h) -> p e h", e=E8)
        up1 = A[:, 2048:4096].rearrange("p (e h) -> p e h", e=E8)
        down1 = A[:, 4096:6144].rearrange("p (e c d) -> p e c d", e=E8, c=2)
        k_tok = A[:, 0:2048].rearrange("p (t h r) -> p t h r", t=NI, h=16)
        v_self = Ring([A[:, 2048 * n:2048 * n + 2048].rearrange("p (t h r) -> p t h r", t=NI, h=16) for n in (1, 2)])
        y = A[:, 6144:8192].rearrange("p (t d) -> p t d", t=NT)
        k_self = Ring([sb(f"k_self{n}", [P, HG, S], FR) for n in range(2)])
        unit_w = Ring([sb(f"unit_w{n}", [P, U_W]) for n in range(2)])
        layer_w = Ring([sb(f"layer_w{n}", [P, L_W]) for n in range(2)])
        x = sb("x", [P, NT, D])
        hT = sb("hT", [P, B, S])
        hn = Ring([sb(f"hn{n}", [P, NI, D]) for n in range(2)])
        kx = sb("kx", [P, HG, G, B * SK], FR)
        vx = sb("vx", [P, B, 16, HR])
        q_g = Ring([sb(f"q_g{n}", [P, S], FR) for n in range(8)])
        prob = Ring([sb(f"prob{n}", [P, 2 * S]) for n in range(3)])
        oT = Ring([sb(f"oT{n}", [P, S]) for n in range(2)])
        o_tok = Ring([sb(f"o_tok{n}", [P, NI, D]) for n in range(2)])
        hid = Ring([sb(f"hid{n}", [P, 4, S]) for n in range(2)])
        bias_q_raw = sb("bias_q", [P, NT * SK // 2])
        bias_k_raw = sb("bias_k", [P, B * S // 2])
        bias_q = bias_q_raw[:, :].bitcast(BF).rearrange("p (t k) -> p t k", t=NT)
        bias_k = bias_k_raw[:, :].bitcast(BF).rearrange("p (b s) -> p b s", b=B)
        k_extra = bias_q_raw[:, 0:G * SK].rearrange("p (g k) -> p g k", g=G)
        qkv = sb("qkv", [P, NI, 3 * D])
        rope_b = sb("rope_b", [P, NI * 2 * D])
        cst = sb("cst", [P, CONST_W])
        ident_b = sb("ident_b", [P, P], BF)
        causal_b = sb("causal_b", [P, P], BF)
        cumul_b = sb("cumul_b", [P, 2 * P], BF)
        vec = sb("vec", [P, VEC_W])
        rows = sb("rows", [P, ROW_W])
        mats = sb("mats", [P, MAT_W])
        ub = sb("ub", [P, 8, G])
        ubs = sb("ubs", [P, 8, G])
        ctxT = sb("ctxT", [P, B, SK])
        expert_b = sb("expert_b", [E8, D])
        wq8_words = sb("wq8", [P, D // 4], I32)
        wq8 = wq8_words[:, :].bitcast(I8)
        wqb = sb("wqb", [P, D], BF)
        moments = Ring([sb(f"moments{n}", [P, NI * 9]) for n in range(3)])
        rstd = Ring([sb(f"rstd{n}", [P, NI]) for n in range(3)])
        recip = sb("recip", [P, NI * HG])
        comb = sb("comb", [P, NT, E8])
        small = sb("small", [P, 16])
        maxima = [sb(f"maxima{n}", [P, NI, HG]) for n in range(2)]

        def const(name):
            a, w = CONST_COLS[name]
            return cst[:, a:a + w]

        ident = const("ident")
        wide = Ring([pr.psum(f"wide{n}", [P, 2 * S]) for n in range(3)])
        acc = Ring([pr.psum(f"acc{n}", [P, S]) for n in range(2)])

        def bank():
            return (acc if acc.idle else wide).take()

        def mm(out, lhsT, rhs, *after, start=True, stop=True, signal=False, turn=False):
            return pe.do(lambda e: e.matmul(out, lhsT, rhs, start=start, stop=stop, is_transpose=turn),
                         *after, signal=signal)

        def v_tt(out, a, b, op, *after, line=dve, apart=False):
            return line.do(lambda e: e.tensor_tensor(out, a, b, op), *after, apart=apart)

        def v_ts(out, a, s1, s2, op0, op1=None, *after, line=dve, apart=False):
            if op1 is None:
                return line.do(lambda e: e.tensor_scalar(out, a, s1, None, op0), *after, apart=apart)
            return line.do(lambda e: e.tensor_scalar(out, a, s1, s2, op0, op1), *after, apart=apart)

        def v_stt(out, a, s, b, op0, op1, *after, apart=False):
            return dve.do(lambda e: e.scalar_tensor_tensor(out=out, in0=a, scalar=s, in1=b, op0=op0, op1=op1),
                          *after, apart=apart)

        def v_red(out, a, op, *after, negate=False, mag=False, apart=False):
            return dve.do(lambda e: e.tensor_reduce(out, a, AX.X, op, negate=negate, apply_absolute_value=mag),
                          *after, apart=apart)

        def v_copy(out, a, *after, line=dve, apart=False):
            return line.do(lambda e: e.tensor_copy(out, a), *after, apart=apart)

        def a_act(out, a, func, *after, bias=0.0, scale=1.0, apart=False):
            return act.do(lambda e: e.activation(out, a, func, bias=bias, scale=scale), *after, apart=apart)

        def a_copy(out, a, *after, scale=1.0, apart=False):
            return a_act(out, a, ACT.Copy, *after, scale=scale, apart=apart)

        def zero(ap, *after, value=0.0, line=pool):
            return line.do(lambda e: e.memset(ap, value), *after)

        def load(name, pairs, *after):
            sem = pr.semaphore(f"load_{name}")
            sync.wait(*after)
            for dst, src in pairs:
                sync.todo.append(("do16", dst, src, sem))
            return (sem, pr.nsem, 16 * len(pairs))

        def spread(src, n, parts=P):
            return src.partition_broadcast(parts) if n else src

        ld_const = load("const", [(cst[:, :], io["consts"])])
        ld_small = load("small", [(ctxT[:, :, :], io["ctxT"]), (ub[:, :, :], io["unit_b"]),
                                  (vec[:, :], io["vecs"]), (mats[:, :], io["mats"]),
                                  (rows[:, :], spread(io["rows"], 1)), (expert_b[:, :], io["expert_b"]),
                                  (wq8_words[:, :], io["wq8"])])

        def load_unit(n, *after):
            s = unit_w.take()
            s.mark = load(f"unit{n}", [(s.buf[:, 0:U_BQ], io["unit_w"][n]),
                                       (s.buf[:, U_BQ:U_W], spread(io["unit_rows"][n], 1))], s.busy, *after)
            return s

        def load_layer(n):
            s = layer_w.take()
            s.mark = load(f"layer{n}", [(s.buf[:, 0:L_BQKV], io["layer_w"][n]),
                                        (s.buf[:, L_BQKV:L_W], spread(io["layer_rows"][n], 1))], s.busy)
            return s

        m_in = hid.bufs[0][:, :, :].rearrange("p c s -> p (c s)")
        mask_raw = m_in[:, 0:NT * SC].bitcast(I32).rearrange("p (t k) -> p t k", t=NT)
        units = {0: load_unit(0)}
        ld_mask = load("mask", [(mask_raw, io["mask"].rearrange("b (i p) k -> p (b i) k", p=P))])
        ld_x = [load(f"x{b}", [(x[:, NI * b:NI * b + NI, :], io["x"][b].rearrange("(i p) d -> p i d", p=P))])
                for b in range(B)]
        units[1] = load_unit(1)
        ld_w0 = load("experts0", [(w1, io["w1"]), (w2, io["w2"])])
        experts3 = {}
        layers = {0: load_layer(0), 1: load_layer(1)}

        zeros = small[:, 0:1]
        blank = zero(zeros)
        made = [zero(vx[:, :, :, :])]
        for i in range(HG):
            for g in range(G):
                v_copy(kx[:, i, g, :], zeros.broadcast_to([P, B * SK]), blank)
        for n in range(2 * HG):
            a_copy(k_self.bufs[n // HG][:, n % HG, :], zeros.broadcast_to([P, S]), blank)
        made_act = act.last
        made = [zero(vx[:, :, :, VSUM:VSUM + 1], value=1.0)]
        for buf in o_tok.bufs:
            made.append(zero(buf[:, :, :]))
        made_pool = made[-1]
        v_copy(ident_b[:, :], ident, ld_const)
        v_copy(causal_b[:, :], const("causal"))
        v_copy(cumul_b[:, 0:P], const("cumul"))
        zero(cumul_b[:, P:2 * P], value=1.0, line=dve)
        v_copy(wqb[:, :], wq8, ld_small)
        for n in range(8):
            made_dve = v_ts(ubs[:, n, :], ub[:, n, :], const("kscale4" if n in (1, 2) else "kscale8"), None,
                            ALU.mult, None)
        for line in (pe, act, pool, dve):
            line.wait(made_act, ld_const, ld_small, made_pool, made_dve)
        x_at = {b: [ld_x[b]] for b in range(B)}
        y_at = {b: [] for b in range(B)}
        hT_free = {b: [] for b in range(B)}

        def tiles(buf, b):
            return buf[:, NI * b:NI * b + NI, :]

        def normalise(src, dst, eps, rms, *after):
            mo = moments.take()
            stats = mo.buf[:, 0:6 * NI].rearrange("p (i c) -> p i c", i=NI)
            mv = mo.buf[:, 6 * NI:8 * NI].rearrange("p (i c) -> p i c", i=NI)
            ve = mo.buf[:, 8 * NI:9 * NI]
            for i in range(NI):
                dve.do(lambda e, i=i: e.bn_stats(stats[:, i, :], src[:, i, :]), *after, *mo.busy, apart=i > 0)
            for i in range(NI):
                dve.do(lambda e, i=i: e.bn_aggr(mv[:, i, :], stats[:, i, :]), apart=i > 0)
            mean, var = mv[:, :, 0], mv[:, :, 1]
            if rms:
                v_tt(ve, mean, mean, ALU.mult)
                ready = v_stt(ve, ve, eps, var, ALU.add, ALU.add)
            else:
                ready = v_ts(ve, var, eps, None, ALU.add)
            r = rstd.take()
            ready = v_tt(r.buf[:, :], ve, const("minus_half"), ALU.pow, ready, r.busy, line=pool)
            yield
            for i in range(NI):
                if rms:
                    done = v_ts(dst[:, i, :], src[:, i, :], r.buf[:, i:i + 1], None, ALU.mult, None, ready,
                                apart=i > 0)
                else:
                    done = v_ts(dst[:, i, :], src[:, i, :], mv[:, i, 0:1], r.buf[:, i:i + 1],
                                ALU.subtract, ALU.mult, ready, apart=i > 0)
            r.read_by(done)
            mo.read_by(done)
            return done

        def turn_batch(src, b, *after, scale=None, shift=None, dst=None, busy=None):
            s = wide.take()
            for i in range(NI):
                m = mm(s.buf[:, P * i:P * i + P], src[:, i, :], ident, *after, s.busy, signal=i == NI - 1, turn=True)
            out = hT[:, b, :] if dst is None else dst
            wait = [m] + (hT_free[b] if busy is None else busy)
            if scale is None:
                done = a_copy(out, s.buf[:, 0:S], wait)
            elif shift is None:
                done = a_copy(out, s.buf[:, 0:S], wait, scale=scale)
            else:
                done = a_act(out, s.buf[:, 0:S], ACT.Identity, wait, bias=shift, scale=scale)
            s.read_by(done)
            return m, done

        mask_free = [[]]

        def turn_masks(name, *after):
            masks[name, "q"] = after
            for b in range(B):
                s = wide.take()
                for i in range(NI):
                    m = mm(s.buf[0:SC, P * i:P * i + P], bias_q[:, NI * b + i, 0:SC], ident_b[:, :], *after, s.busy,
                           signal=i == NI - 1)
                done = a_copy(bias_k[0:SC, b, :], s.buf[0:SC, 0:S], m, mask_free[0])
                s.read_by(done)
            masks[name, "k"] = done

        def project_out(ot, ready, w, bias, stream, at, b):
            s = oT.take()
            m, done = turn_batch(ot.buf, b, *ready, dst=s.buf[:, :], busy=s.busy)
            ot.read_by(m)
            yield
            a = wide.take()
            for i in range(NI):
                m = mm(a.buf[:, P * i:P * i + P], s.buf[:, P * i:P * i + P], w, done, a.busy, signal=i == NI - 1)
            s.read_by(m)
            dst = tiles(stream, b)
            done = v_tt(dst, a.buf[:, 0:S].rearrange("p (i d) -> p i d", i=NI), dst, ALU.add, m, *at[b])
            a.read_by(done)
            if bias is not None:
                done = v_tt(dst, dst, bias.unsqueeze(1).broadcast_to([P, NI, D]), ALU.add, done, line=pool)
            at[b] = [done]
            yield

        def normalise_heads(ta, dh, ot, h0):
            v = ta.buf[:, 0:S].rearrange("p (t i r) -> p t i r", t=NI, i=HG)
            rc = recip[:, :].rearrange("p (t i) -> p t i", t=NI)
            dve.do(lambda e: e.reciprocal(rc, v[:, :, :, VSUM]), ta.mark)
            out = ot.buf[:, :, h0 * dh:(h0 + HG) * dh].rearrange("p t (i r) -> p t i r", i=HG)
            done = v_tt(out, v[:, :, :, 0:dh], rc.unsqueeze(3).broadcast_to([P, NI, HG, dh]), ALU.mult, ot.busy)
            ta.read_by(done)
            return done

        def group_out(a, m, dh, ot, h0, pause=1):
            s = oT.take()
            done = a_copy(s.buf[:, :], a.buf[:, :], m, s.busy)
            a.read_by(done)
            for _ in range(pause):
                yield
            t = wide.take()
            for i in range(NI):
                t.mark = mm(t.buf[:, P * i:P * i + P], s.buf[:, P * i:P * i + P], ident, done, t.busy,
                            signal=i == NI - 1, turn=True)
            s.read_by(t.mark)
            yield
            ot.done = normalise_heads(t, dh, ot, h0)

        def high_part(out, src, *after):
            return dve.do(lambda e: e.tensor_scalar(out.bitcast(I32), src.bitcast(I32), HIGH, None,
                                                    ALU.bitwise_and), *after)

        def queries_in_parts(src, qt, *after):
            high, copy, low = (qt.buf[:, :, :, PART * n:PART * n + src.shape[3]] for n in range(3))
            tail = zero(qt.buf[:, :, :, MROW:HR], qt.busy)
            done = high_part(high, src, *after, qt.busy)
            twin = v_copy(copy, high, done, line=pool)
            return [v_tt(low, src, high, ALU.subtract), twin, tail]

        def token_queries():
            s = hid.take()
            s.buf = s.buf[:, :, :].rearrange("p t (h r) -> p t h r", h=16)
            return s

        def turn_queries(qt, g, q, busy, *after):
            s = bank()
            h = HG * g
            for i in range(NI):
                m = mm(s.buf[:, P * i:P * i + P], qt.buf[:, i, h:h + HG, :].rearrange("p h r -> p (h r)"), ident,
                       *after, s.busy, signal=i == NI - 1, turn=True)
            done = a_copy(q.buf[:, :], s.buf[:, 0:S], m, busy)
            s.read_by(done)
            return m, done

        def maxima_to_queries(qt, g):
            h = HG * g
            v, top = qt.buf[:, :, h:h + HG, :], maxima[g % 2][:, :, :]
            high_part(v[:, :, :, MROW], top)
            return v_tt(v[:, :, :, MROW + 1], top, v[:, :, :, MROW], ALU.subtract)

        kv_free = {b: [] for b in range(B)}
        masks = {}

        def cross_unit(n, dh, src, at, masked, alibi, proj, bias_o, eps, scale_of, first_unit=True, rms=False):
            state = {}
            turned = cross_unit.turned

            def keys_values(b):
                w = units[n]
                s = wide.take()
                for g in range(G):
                    mm(s.buf[:, SK * g:SK * g + SK], w.buf[:, U_WK + P * g:U_WK + P * g + P], ctxT[:, b, :], w.mark,
                       s.busy)
                m = mm(s.buf[0:SC, S:S + P], ctxT[:, b, 0:SC], w.buf[:, U_WV:U_WV + P], signal=True)
                whole, high = (rope_b[:, S * k:S * k + G * SK].rearrange("p (g k) -> p g k", g=G) for k in range(2))
                v_stt(whole, s.buf[:, 0:G * SK].rearrange("p (g k) -> p g k", g=G),
                      const("kscale4" if dh == 4 else "kscale8"),
                      ubs[:, n, :].unsqueeze(2).broadcast_to([P, G, SK]), ALU.mult, ALU.add, m)
                pv = s.buf[0:SC, S:S + P].rearrange("p (h r) -> p h r", r=dh)[:, 0:16, :]
                bv = w.buf[0:SC, U_BV:U_BV + 16 * dh].rearrange("p (h r) -> p h r", h=16)
                s.read_by(v_tt(vx[0:SC, b, :, 0:dh], pv, bv, ALU.add, kv_free[b]))
                yield
                if alibi:
                    v_tt(whole, whole, k_extra, ALU.add, *state["extra"])
                high_part(high, whole)
                v_ts(whole, whole, const("pick")[:, 0:1], None, ALU.mult)
                for i in range(HG):
                    if i % 2 == 0:
                        yield
                    r = slice(HR * i, HR * i + HR)
                    state["kv", b] = v_stt(kx[r, i, :, SK * b:SK * b + SK], high[r], const("pick")[r, 1:2], whole[r],
                                           ALU.mult, ALU.add, apart=i > 0)

            def prepare(b):
                if alibi:
                    state["extra"] = cross_unit.extra
                w = state["w"] = units[n]
                if first_unit:
                    h = hn.take()
                    done = yield from normalise(tiles(src, b), h.buf, eps, rms, *at[b], h.busy)
                yield from keys_values(b)
                if first_unit:
                    m, turned[b] = turn_batch(h.buf, b, done, scale=scale_of)
                    h.read_by(m)
                yield
                s = wide.take()
                for i in range(NI):
                    m = mm(s.buf[:, P * i:P * i + P], hT[:, b, P * i:P * i + P], w.buf[:, U_WQ:U_WQ + P], w.mark,
                           turned[b], s.busy, signal=i == NI - 1)
                hT_free[b] = [m]
                whole = qkv[:, :, 0:D]
                done = v_tt(whole, s.buf[:, 0:S].rearrange("p (i d) -> p i d", i=NI),
                            w.buf[:, U_BQ:U_BQ + D].unsqueeze(1).broadcast_to([P, NI, D]), ALU.add, m)
                s.read_by(done)
                yield
                qt = state["qt", b] = token_queries()
                ready = queries_in_parts(whole.rearrange("p t (h r) -> p t h r", r=dh)[:, :, 0:16, :], qt)
                if alibi:
                    zero(qt.buf[:, :, :, KROW:KROW + 1], value=1.0)
                    ready = [ready, v_copy(qt.buf[:, :, :, QROW], const("position").unsqueeze(2)
                                           .broadcast_to([P, NI, 16]), line=pool)]
                state["cut", b] = ready
                yield

            def full(b, g):
                q = state["q", b][g]
                m, q.full = turn_queries(state["qt", b], g, q, [], state["max", b, g])
                return m

            def scores(b):
                qt = state["qt", b]
                qs = state["q", b] = [q_g.take() for _ in range(G)]

                def turn(g):
                    _, qs[g].turned = turn_queries(qt, g, qs[g], qs[g].busy, *state["cut", b])

                turn(0)
                yield
                turn(1)
                yield
                for g in range(G):
                    for half in range(2):
                        s = wide.take()
                        for tt in range(2):
                            t = 2 * half + tt
                            bank = s.buf[:, S * tt:S * tt + HG * SK].rearrange("p (i k) -> p i k", i=HG)
                            if masked:
                                mm(bank, ident_b[:, :],
                                   bias_q[:, NI * b + t:NI * b + t + 1, :].broadcast_to([P, HG, SK]),
                                   masks[masked, "q"], s.busy, stop=False)
                            m = mm(bank, qs[g].buf[:, P * t:P * t + P], kx[:, :, g, SK * b:SK * b + SK],
                                   qs[g].turned, s.busy, state["kv", b], start=not masked, signal=tt == 1)
                        v = s.buf[:, :].rearrange("p (t c) -> p t c", t=2)[:, :, 0:HG * SK]\
                            .rearrange("p t (i k) -> p t i k", i=HG)[:, :, :, 0:SC]
                        top = v_red(maxima[g % 2][:, 2 * half:2 * half + 2, :], v, ALU.max, m, negate=True, apart=True)
                        s.read_by(top)
                        if half == 1:
                            state["max", b, g] = maxima_to_queries(qt, g)
                            if g > 0:
                                full(b, g - 1)
                        if g == 0:
                            turn(2 + half)
                        yield

            def attend(b):
                ot = o_tok.take()
                pend, out = None, iter(())
                for step in [(g, hp) for g in range(G) for hp in range(HG // 2)] + [None]:
                    nxt = None
                    if step:
                        g, hp = step
                        q = state["q", b][g]
                        if (g, hp) == (1, 0):
                            m = full(b, G - 1)
                            state["qt", b].read_by(m, dve.last)
                        s = wide.take()
                        for ii in range(2):
                            i = 2 * hp + ii
                            bank = s.buf[0:SC, S * ii:S * ii + S]
                            if masked:
                                mm(bank, ident_b[0:SC, 0:SC], bias_k[0:SC, b, :], masks[masked, "k"], s.busy, stop=False)
                            m = mm(bank, kx[:, i, g, SK * b:SK * b + SC], q.buf[:, :], q.full, s.busy,
                                   start=not masked, signal=ii == 1)
                        if hp == HG // 2 - 1:
                            q.read_by(m)
                        pb = prob.take()
                        e = a_act(pb.buf[0:SC, :], s.buf[0:SC, :], ACT.Exp, m, pb.busy)
                        s.read_by(e)
                        nxt = (g, hp, pb, e)
                    next(out, None)
                    if pend:
                        g, hp, pb, e = pend
                        if hp == 0:
                            a = acc.take()
                        for ii in range(2):
                            i = 2 * hp + ii
                            m = mm(a.buf[HR * i:HR * i + HR, :], vx[0:SC, b, HG * g + i, :],
                                   pb.buf[0:SC, S * ii:S * ii + S], e, a.busy, state["kv", b], signal=ii == 1)
                        pb.read_by(m)
                        if hp == 1:
                            for _ in out:
                                pass
                            out = group_out(a, m, dh, ot, HG * g)
                    pend = nxt
                    yield
                state["out", b] = (out, ot)
                kv_free[b] = [m]
                if b == B - 1:
                    mask_free[0] = [m, dve.last]

            def finish(b):
                w = state["w"]
                out, ot = state["out", b]
                yield from out
                for _ in range(2):
                    yield
                if proj:
                    yield from project_out(ot, [ot.done], w.buf[:, U_WO:U_WO + P],
                                           w.buf[:, U_BO:U_BO + P] if bias_o else None, src if rms else x,
                                           at if rms else x_at, b)
                else:
                    dst = tiles(x, b)
                    done = v_tt(dst, dst, ot.buf[:, :, :], ALU.add, ot.done, *x_at[b], line=pool)
                    ot.read_by(done)
                    x_at[b] = [done]
                if b == B - 1:
                    w.read_by(pe.last, pool.last, dve.last)
                    if n in load_after:
                        for k in load_after[n]:
                            units[k] = load_unit(k)
                yield

            return [[(lambda b=b, f=f: f(b)) for f in (prepare, scores, attend, finish)] for b in range(B)]

        load_after = {0: [2], 1: [3], 2: [4], 3: [5], 4: [6], 5: [7]}
        cross_unit.turned = {}

        def named(name, phase):
            def begin():
                stage(name)
                yield from phase()
            return begin

        def staged(name, items):
            return [[named(name, items[0][0])] + items[0][1:]] + items[1:]

        stage("l0_attn")
        cleared = zero(bias_q[:, :, :])
        done = v_ts(bias_q[:, :, 0:SC], mask_raw, 0.0, NEG, ALU.is_equal, ALU.mult, ld_mask, cleared)
        hid.free[0] = [done]
        masks["l0", "q"] = [done]

        def turn_masks0(done=done):
            for _ in range(3):
                yield
            turn_masks("l0", done)
            yield

        every = cross_unit(0, 8, x, x_at, "l0", False, False, False, 1e-5, None) + [[idle]]
        every[1][0] = beside(every[1][0], turn_masks0)

        def ffn0(b):
            st = {}

            def prepare():
                h1, h2 = hn.take(), hn.take()
                done1 = yield from normalise(tiles(x, b), h1.buf, 1e-5, False, *x_at[b], h1.busy)
                done2 = yield from normalise(h1.buf, h2.buf, 1e-5, False, done1, h2.busy)
                for _ in range(3):
                    yield
                t = prob.take()
                x1T, ln = t.buf[:, 0:S], t.buf[:, S:2 * S]
                m, x1_done = turn_batch(h1.buf, b, done1, dst=x1T, busy=t.busy)
                h1.read_by(m, done2)
                yield
                m, ln_done = turn_batch(h2.buf, b, done2, scale=vec[:, V_LNG:V_LNG + 1],
                                        shift=vec[:, V_LNB:V_LNB + 1], dst=ln, busy=t.busy)
                h2.read_by(m)
                yield
                a = wide.take()
                m = mm(a.buf[:, 0:S], mats[:, M_ATT:M_ATT + P], ln, ln_done, a.busy, signal=True)
                st["xa"] = v_stt(hT[:, b, :], a.buf[:, 0:S], vec[:, V_ATTB:V_ATTB + 1], x1T, ALU.add, ALU.add, m,
                                 x1_done, *hT_free[b])
                a.read_by(st["xa"])
                t.read_by(m, st["xa"])
                yield

            def hidden():
                h = st["hid"] = hid.take()
                for i in range(NI):
                    e = (NI * b + i) % E8
                    s = wide.take()
                    for c in range(4):
                        m = mm(s.buf[:, P * c:P * c + P], w1[:, e, P * c:P * c + P], hT[:, b, P * i:P * i + P],
                               ld_w0, st["xa"], s.busy, signal=c == 3)
                    for c in range(4):
                        k = V_B1 + 4 * e + c
                        h.done = a_act(h.buf[:, c, P * i:P * i + P], s.buf[:, P * c:P * c + P], ACT.Gelu, m, h.busy,
                                       bias=vec[:, k:k + 1], apart=True)
                    s.read_by(h.done)
                    yield
                hT_free[b] = [m]

            def down():
                h, y2 = st["hid"], prob.take()
                s = wide.take()
                for i in range(NI):
                    e = (NI * b + i) % E8
                    for c in range(4):
                        m = mm(s.buf[:, P * i:P * i + P], w2[:, e, c, :], h.buf[:, c, P * i:P * i + P], h.done,
                               s.busy, start=c == 0, stop=c == 3, signal=(i, c) == (NI - 1, 3))
                for i in range(NI):
                    e = (NI * b + i) % E8
                    at0 = P * i
                    done = v_ts(y2.buf[:, at0:at0 + P], s.buf[:, at0:at0 + P], vec[:, V_B2 + e:V_B2 + e + 1], None,
                                ALU.add, None, m, y2.busy, apart=i > 0)
                s.read_by(done)
                h.read_by(m)
                if b == B - 1:
                    ld_w1.append(load("experts1", [(gate1, io["gate1"]), (up1, io["up1"]), (down1, io["down1"])], m))
                for _ in range(2):
                    yield
                s = wide.take()
                for i in range(NI):
                    m = mm(s.buf[:, P * i:P * i + P], y2.buf[:, P * i:P * i + P], mats[:, M_NEXT:M_NEXT + P], done,
                           s.busy, signal=i == NI - 1)
                nb = rows[:, R_NEXTB:R_NEXTB + P].unsqueeze(1).broadcast_to([P, NI, D])
                before, after = y2.buf[:, 0:S], y2.buf[:, S:2 * S]
                done = v_tt(before.rearrange("p (i d) -> p i d", i=NI),
                            s.buf[:, 0:S].rearrange("p (i d) -> p i d", i=NI), nb, ALU.add, m)
                s.read_by(done)
                g = a_act(after, before, ACT.Gelu, done)
                dst = tiles(x, b)
                done = v_tt(dst, dst, after.rearrange("p (i d) -> p i d", i=NI), ALU.add, g, *x_at[b], line=pool)
                y2.read_by(done)
                x_at[b] = [done]
                yield

            return [prepare, hidden, down]

        def masks1():
            raw = hid.take()
            words = raw.buf[:, 0, :].bitcast(I32)
            am_w = words[:, 0:NI * MASK_W].rearrange("p (i w) -> p i w", i=NI)
            pm_w = words[:, NI * MASK_W:(NI + B) * MASK_W].rearrange("p (b w) -> p b w", b=B)
            am = raw.buf[:, 0, 0:NI * MASK_W].bitcast(U8).rearrange("p (i k) -> p i k", i=NI)[:, :, 0:SC]
            pm = raw.buf[:, 0, NI * MASK_W:(NI + B) * MASK_W].bitcast(U8)\
                .rearrange("p (b k) -> p b k", b=B)[:, :, 0:SC]
            either = raw.buf[:, 1:4, :].rearrange("p c s -> p (c s)")[:, 0:NT * SC]\
                .rearrange("p (b i k) -> p b i k", b=B, i=NI)
            ld_m1 = load("masks1", [(am_w, io["attn_mask"].rearrange("(i p) k -> p i k", p=P)),
                                    (pm_w, spread(io["pad_mask"], 1))], raw.busy)
            for b in range(B):
                v_tt(either[:, b, :, :], am, pm[:, b:b + 1, :].broadcast_to([P, NI, SC]), ALU.max, ld_m1)
            done = v_ts(bias_q[:, :, 0:SC], either.rearrange("p b i k -> p (b i) k"), 0.0, NEG, ALU.is_gt, ALU.mult,
                        mask_free[0])
            raw.read_by(done)
            for _ in range(3):
                yield
            turn_masks("l1", done)
            yield

        ld_w1 = []
        first0 = staged("l0_ffn", [ffn0(b) for b in range(B)])
        first0[1][0] = beside(first0[1][0], masks1)
        every += first0
        every += staged("l1_attn", cross_unit(1, 4, x, x_at, "l1", False, True, False, 1e-5, None)
                        + cross_unit(2, 4, x, x_at, "l1", False, True, True, 1e-5, None, first_unit=False))

        wk = qkv[:, :, :].rearrange("p t c -> p (t c)")
        taken = [0]

        def piece(n, dt=F32):
            a = taken[0]
            taken[0] += n
            return wk[:, a:a + n]

        def softmax8(lg, n, prob_out, mx, *after):
            v_red(mx, lg, ALU.max, *after)
            v_tt(prob_out, lg, mx.unsqueeze(2).broadcast_to([P, n, E8]), ALU.subtract)
            a_act(prob_out, prob_out, ACT.Exp, dve.last)
            v_red(mx, prob_out, ALU.add, act.last)
            dve.do(lambda e: e.reciprocal(mx, mx))
            return v_tt(prob_out, prob_out, mx.unsqueeze(2).broadcast_to([P, n, E8]), ALU.mult)

        def first_max(pv, n, mx, c, hot):
            v_red(mx, pv, ALU.max)
            v_tt(c, pv, mx.unsqueeze(2).broadcast_to([P, n, E8]), ALU.is_equal)
            v_tt(c, c, const("rev").unsqueeze(1).broadcast_to([P, n, E8]), ALU.mult)
            v_red(small[:, 0:n], c, ALU.max)
            return v_tt(hot, c, small[:, 0:n].unsqueeze(2).broadcast_to([P, n, E8]), ALU.is_equal)

        W8 = NT * E8
        probs = piece(W8).rearrange("p (t e) -> p t e", e=E8)
        cand = piece(W8).rearrange("p (t e) -> p t e", e=E8)
        hot = piece(2 * W8).rearrange("p (k t e) -> p k t e", k=2, e=E8)
        tops = piece(2 * NT).rearrange("p (k t) -> p k t", k=2)
        rank = piece(2 * W8)
        before = piece(2 * W8)
        tot = piece(2 * W8)
        hot_b = piece(W8).bitcast(BF)
        lv = comb[:, :, :]

        def gate(b):
            h = hn.take()
            done = yield from normalise(tiles(x, b), h.buf, 1e-5, False, *x_at[b], h.busy)
            for _ in range(3):
                yield
            m, h1T[b] = turn_batch(h.buf, b, done)
            h.read_by(m)
            yield
            s = wide.take()
            for i in range(NI):
                m = mm(s.buf[:, E8 * i:E8 * i + E8], hT[:, b, P * i:P * i + P], mats[:, M_GATE:M_GATE + E8],
                       h1T[b], s.busy, signal=i == NI - 1)
            s.read_by(v_copy(tiles(lv, b), s.buf[:, 0:NI * E8].rearrange("p (i e) -> p i e", e=E8), m))
            yield

        def choose():
            softmax8(lv, NT, probs, tops[:, 0, :])
            yield
            first_max(probs, NT, tops[:, 0, :], cand, hot[:, 0])
            v_tt(cand, hot[:, 0], probs, ALU.mult)
            v_tt(probs, probs, cand, ALU.subtract)
            v_tt(probs, probs, hot[:, 0], ALU.subtract)
            yield
            first_max(probs, NT, tops[:, 1, :], cand, hot[:, 1])
            v_tt(small[:, 0:NT], tops[:, 0, :], tops[:, 1, :], ALU.add)
            v_ts(small[:, 0:NT], small[:, 0:NT], 1e-9, None, ALU.add)
            dve.do(lambda e: e.reciprocal(small[:, 0:NT], small[:, 0:NT]))
            v_tt(tops, tops, small[:, 0:NT].unsqueeze(1).broadcast_to([P, 2, NT]), ALU.mult)
            chosen.append(v_copy(hot_b, hot.rearrange("p k t e -> p (k t e)")))
            yield

        def admit():
            hf = hot.rearrange("p k t e -> p (k t e)")
            s = wide.take()
            mm(s.buf[:, 0:2 * W8], cumul_b[:, 0:P], hot_b, chosen, s.busy)
            m = mm(s.buf[:, S:S + 2 * W8], cumul_b[:, P:2 * P], hot_b, signal=True)
            v_copy(rank, s.buf[:, 0:2 * W8], m)
            v_copy(tot, s.buf[:, S:S + 2 * W8])
            s.read_by(dve.last)
            yield
            r4, b4, t4 = (v.rearrange("p (k t e) -> p k t e", k=2, e=E8) for v in (rank, before, tot))
            zero(b4[:, :, 0, :], line=dve)
            for t in range(1, NT):
                v_tt(b4[:, :, t, :], b4[:, :, t - 1, :], t4[:, :, t - 1, :], ALU.add)
            yield
            v_tt(rank, rank, before, ALU.add)
            v_ts(rank, rank, float(CAP) + 0.5, None, ALU.is_lt)
            v_tt(rank, rank, hf, ALU.mult)
            for k in range(2):
                v_tt(r4[:, k], r4[:, k], tops[:, k, :].unsqueeze(2).broadcast_to([P, NT, E8]), ALU.mult)
            v_tt(comb[:, :, :], r4[:, 0], r4[:, 1], ALU.add)
            yield

        def ffn1(b, e):
            st = {}

            def hidden():
                h = st["hid"] = hid.take()
                for c in range(2):
                    s = wide.take()
                    mm(s.buf[:, 0:S], gate1[:, e, P * c:P * c + P], hT[:, b, :], *ld_w1, h1T[b], s.busy)
                    m = mm(s.buf[:, S:2 * S], up1[:, e, P * c:P * c + P], hT[:, b, :], signal=True)
                    g = a_act(h.buf[:, c, :], s.buf[:, 0:S], ACT.Silu, m, h.busy)
                    h.done = v_tt(h.buf[:, c, :], s.buf[:, S:2 * S], h.buf[:, c, :], ALU.mult, g)
                    s.read_by(h.done)
                    yield
                hT_free[b] = [m]

            def down():
                h, a = st["hid"], acc.take()
                for i in range(NI):
                    for c in range(2):
                        m = mm(a.buf[:, P * i:P * i + P], h.buf[:, c, P * i:P * i + P], down1[:, e, c, :], h.done,
                               a.busy, start=c == 0, stop=c == 1, signal=(i, c) == (NI - 1, 1))
                    if i == 1:
                        yield
                h.read_by(m)
                st["acc"], st["m"] = a, m
                yield

            def add():
                a = st["acc"]
                for i in range(NI):
                    t = NI * b + i
                    done = v_stt(x[:, t, :], a.buf[:, P * i:P * i + P], comb[:, t, e:e + 1], x[:, t, :], ALU.mult,
                                 ALU.add, st["m"], *x_at[b], apart=i > 0)
                x_at[b] = [done]
                a.read_by(done)
                experts1_read[:] = [st["m"]]
                yield

            return [hidden, down, add]

        def extras():
            cross_unit.extra = [load("extras", [(k_extra, io["k_extra"])], mask_free[0])]
            yield

        h1T, chosen, experts1_read = {}, [], []
        every += staged("l1_ffn", [[(lambda b=b: gate(b))] for b in range(B)])
        items = [ffn1(b, e) for b in range(B) for e in range(E8)]
        items[0][0] = beside(items[0][0], choose)
        items[1][0] = beside(items[1][0], admit, extras)
        every += items

        every += staged("l2_attn", cross_unit(3, 8, x, x_at, "", True, True, True, 1e-5, None))

        def clear():
            zero(A[:, 0:6144], *experts1_read)
            zero(k_tok[:, :, :, MROW:MROW + 2], value=1.0)
            for buf in v_self.bufs:
                cleared = zero(buf[:, :, :, VSUM:VSUM + 1], value=1.0)
            tok_free[0] = [cleared]
            v_self.free[:] = [[cleared], [cleared]]
            yield

        tok_free = [[]]

        def quant_first(b, st):
            h = hn.take()
            yield from normalise(tiles(x, b), h.buf, 1e-5, False, *x_at[b], h.busy)
            xs = prob.take()
            st["xs"] = xs
            sc, inv = xs.buf[:, 0:NI], xs.buf[:, NI:2 * NI]
            v_red(sc, h.buf[:, :, :], ALU.max, xs.busy, mag=True)
            v_ts(sc, sc, 1e-6, 1.0 / 127.0, ALU.max, ALU.mult)
            dve.do(lambda e: e.reciprocal(inv, sc))
            for i in range(NI):
                v_ts(h.buf[:, i, :], h.buf[:, i, :], inv[:, i:i + 1], MAGIC, ALU.mult, ALU.add, apart=i > 0)
            v_ts(h.buf[:, :, :], h.buf[:, :, :], -MAGIC, -128.0, ALU.add, ALU.max)
            done = v_ts(h.buf[:, :, :], h.buf[:, :, :], 127.0, None, ALU.min)
            for _ in range(3):
                yield
            m, st["qd"] = turn_batch(h.buf, b, done, dst=xs.buf[:, S:S + S // 2].bitcast(BF), busy=xs.busy)
            h.read_by(m)
            yield

        def quant_second(b, st):
            a = wide.take()
            qb = st["xs"].buf[:, S:S + S // 2].bitcast(BF)
            for i in range(NI):
                m = mm(a.buf[:, P * i:P * i + P], qb[:, P * i:P * i + P], wqb[:, :], st["qd"], a.busy,
                       signal=i == NI - 1)
            h = hid.take()
            hv = h.buf[:, 0, :].rearrange("p (i d) -> p i d", i=NI)
            for i in range(NI):
                v_stt(hv[:, i, :], a.buf[:, P * i:P * i + P], st["xs"].buf[:, i:i + 1], rows[:, R_WS:R_WS + P],
                      ALU.mult, ALU.mult, m, h.busy)
            a.read_by(dve.last)
            st["xs"].read_by(m, dve.last)
            done = v_tt(hv, hv, rows[:, R_QB:R_QB + P].unsqueeze(1).broadcast_to([P, NI, D]), ALU.add)
            dst = tiles(x, b)
            done = v_tt(dst, dst, hv, ALU.add, done, *x_at[b], line=pool)
            h.read_by(done)
            x_at[b] = [done]
            yield

        def masks3():
            raw = hid.take()
            seg_i = raw.buf[:, 3, 0:NT].bitcast(I32)
            seg = raw.buf[:, 3, NT:2 * NT]
            seg_lo = raw.buf[:, 3, 2 * NT:3 * NT]
            flat = raw.buf[:, 0:3, :].rearrange("p c s -> p (c s)")
            ld_seg = load("segments", [(seg_i, io["seg"])], raw.busy)
            late = flat[:, 0:NT * SC].rearrange("p (t k) -> p t k", t=NT)
            iota = const("iota").unsqueeze(1).broadcast_to([P, NT, SC])
            empty = zero(bias_q[:, :, :], mask_free[0])
            v_copy(seg, seg_i, ld_seg)
            v_ts(seg_lo, seg, -float(LOOKBACK), None, ALU.add)
            v_tt(late, iota, seg.unsqueeze(2).broadcast_to([P, NT, SC]), ALU.is_gt)
            yield
            v_tt(bias_q[:, :, 0:SC], iota, seg_lo.unsqueeze(2).broadcast_to([P, NT, SC]), ALU.is_le, mask_free[0],
                 empty)
            yield
            v_tt(late, late, bias_q[:, :, 0:SC], ALU.max)
            yield
            done = v_ts(bias_q[:, :, 0:SC], late, NEG, None, ALU.mult)
            raw.read_by(done)
            for _ in range(3):
                yield
            turn_masks("l3", done)
            yield

        def inner(b):
            y_at[b] = [(yield from normalise(tiles(x, b), tiles(y, b), 1e-5, False, *x_at[b], *experts1_read))]
            yield

        sts = [{} for _ in range(B)]
        items = staged("l2_ffn", [[(lambda b=b: quant_first(b, sts[b])), (lambda b=b: quant_second(b, sts[b])),
                                   (lambda b=b: inner(b))] for b in range(B)])
        items[0][0] = beside(items[0][0], clear)
        every += items

        def self_items(l):
            st = {}

            def project_in(b):
                w = st["w"] = layers[l]
                h = hn.take()
                done = yield from normalise(tiles(y, b), h.buf, 1e-6, True, *y_at[b], h.busy)
                for _ in range(2):
                    yield
                m, hd = turn_batch(h.buf, b, done, scale=vec[:, V_N1 + l:V_N1 + l + 1])
                h.read_by(m)
                yield
                vs = st["v", b] = v_self.take()
                for half in range(2):
                    s = wide.take()
                    for tt in range(2):
                        i = 2 * half + tt
                        m = mm(s.buf[:, S * tt:S * tt + 3 * D], hT[:, b, P * i:P * i + P],
                               w.buf[:, L_QKV:L_QKV + 3 * D], w.mark, hd, s.busy, signal=tt == 1)
                    v = s.buf[:, :].rearrange("p (t c) -> p t c", t=2)
                    bias = w.buf[:, L_BQKV:L_BQKV + 3 * D].unsqueeze(1).broadcast_to([P, 2, 3 * D])
                    v_tt(qkv[:, 2 * half:2 * half + 2, 0:2 * D], v[:, :, 0:2 * D], bias[:, :, 0:2 * D], ALU.add, m)
                    for tt in range(2):
                        vs.mark = v_tt(vs.buf[:, 2 * half + tt, :, 0:8],
                                       v[:, tt, 2 * D:3 * D].rearrange("p (h r) -> p h r", h=16),
                                       w.buf[:, L_BQKV + 2 * D:L_BQKV + 3 * D].rearrange("p (h r) -> p h r", h=16),
                                       ALU.add, vs.busy, apart=True)
                    s.read_by(vs.mark)
                    yield
                hT_free[b] = [m]

            def causal(v, n, *after):
                return pool.do(lambda e: e.affine_select(out=v, in_=v, compare_op=ALU.is_ge, fill=0.0, base=0,
                                                         pattern=[[0, n], [1, P]], channel_multiplier=-1),
                               *after, apart=True)

            rot = rope_b[:, :].rearrange("p (t h r) -> p t h r", t=NI, r=8)

            def rotate(b):
                qk = qkv[:, :, 0:2 * D].rearrange("p t (h r) -> p t h r", r=8)
                cs = const("cos").rearrange("p (t r) -> p t r", t=NI)
                sn = const("sin").rearrange("p (t r) -> p t r", t=NI)
                shape = [P, NI, 32, 4]
                v_tt(rot[:, :, :, 0:4], qk[:, :, :, 4:8], sn[:, :, 0:4].unsqueeze(2).broadcast_to(shape), ALU.mult)
                yield
                v_tt(rot[:, :, :, 4:8], qk[:, :, :, 0:4], sn[:, :, 4:8].unsqueeze(2).broadcast_to(shape), ALU.mult,
                     apart=True)
                yield
                v_tt(qk, qk, cs.unsqueeze(2).broadcast_to([P, NI, 32, 8]), ALU.mult)
                yield
                v_tt(rot, rot, qk, ALU.add)
                yield

            def cut_in(b):
                q, k = rot[:, :, 0:16, :], rot[:, :, 16:32, :]
                qt = st["qt", b] = token_queries()
                ready = queries_in_parts(q, qt)
                yield
                high, low, copy = (k_tok[:, :, :, PART * n:PART * n + PART] for n in range(3))
                done = high_part(high, k, tok_free[0])
                twin = v_copy(copy, high, done, line=pool)
                done = v_tt(low, k, high, ALU.subtract)
                st["qk"] = ready + [twin, done]
                yield

            def prepare(b, g):
                side = iter(())
                if g == 0:
                    side = cut_in(b)
                elif g == 2 and b + 1 < B:
                    side = project_in(b + 1)
                elif g == 3 and b + 1 < B:
                    side = rotate(b + 1)
                for _ in range(6):
                    next(side, None)
                    yield
                q, kk = q_g.take(), k_self.take()
                st[b, g] = (q, kk)
                _, turned = turn_queries(st["qt", b], g, q, q.busy, *st["qk"])
                s = wide.take()
                for i in range(NI):
                    m = mm(s.buf[:, P * i:P * i + P],
                           k_tok[:, i, HG * g:HG * g + HG, :].rearrange("p h r -> p (h r)"), ident,
                           st["qk"], s.busy, signal=i == NI - 1, turn=True)
                if g == G - 1:
                    tok_free[0] = [m]
                q.turned = [turned]
                for i in range(HG):
                    r = slice(HR * i, HR * i + HR)
                    if i > 0:
                        q.turned.append(a_copy(kk.buf[r, i, :], s.buf[r, 0:S], m, kk.busy, apart=True))
                    else:
                        q.turned.append(v_copy(kk.buf[r, i, :], s.buf[r, 0:S], m, kk.busy, apart=True))
                s.read_by(*q.turned)
                yield

            def scores(b, g):
                qt = st["qt", b]
                q, kk = st[b, g]
                for t in range(NI):
                    n = P * (t + 1)
                    per = HG if t < 2 else 2
                    for h0 in range(0, HG, per):
                        s = wide.take()
                        pitch = n if t < 2 else S
                        for i in range(h0, h0 + per):
                            at0 = pitch * (i - h0)
                            mm(s.buf[:, at0:at0 + n], q.buf[:, P * t:P * t + P],
                               kk.buf[:, i, 0:n], *q.turned, s.busy, stop=False)
                            m = mm(s.buf[:, at0 + n - P:at0 + n], ident_b[:, :], causal_b[:, :], start=False,
                                   signal=i == h0 + per - 1)
                        v = s.buf[:, 0:pitch * per].rearrange("p (i k) -> p i k", i=per)[:, :, 0:n]
                        top = v_red(maxima[g % 2][:, t, h0:h0 + per], v, ALU.max, m, negate=True, apart=True)
                        s.read_by(top)
                        if (t, h0 + per) == (NI - 1, HG):
                            top = maxima_to_queries(qt, g)
                        yield
                yield
                m, q.full = turn_queries(qt, g, q, [], top)
                if g == G - 1:
                    qt.read_by(m)
                yield

            def attend(b, g):
                q, kk = st[b, g]
                a = acc.take()
                if g == 0:
                    st["o", b] = o_tok.take()
                ot = st["o", b]
                steps = [(j, h0, HG if j > 1 else 2) for j in range(NI) for h0 in range(0, HG, HG if j > 1 else 2)]
                pend = None
                for step in steps + [None]:
                    nxt = None
                    if step:
                        j, h0, per = step
                        n = S - P * j
                        pitch = n if j > 1 else S
                        s = wide.take()
                        for i in range(h0, h0 + per):
                            at0 = pitch * (i - h0)
                            m = mm(s.buf[:, at0:at0 + n], kk.buf[:, i, P * j:P * j + P],
                                   q.buf[:, P * j:S], q.full, s.busy, signal=i == h0 + per - 1)
                        pb = prob.take()
                        sv = s.buf[:, 0:pitch * per].rearrange("p (i k) -> p i k", i=per)[:, :, 0:n]
                        pv = pb.buf[:, 0:n * per].rearrange("p (i k) -> p i k", i=per)
                        e = a_act(pv, sv, ACT.Exp, m, pb.busy, scale=8 ** -0.5)
                        s.read_by(e)
                        e = [e, causal(pv[:, :, 0:P], per, e)]
                        nxt = (j, h0, per, n, pb, pv, e)
                        if step == steps[-1]:
                            q.read_by(m)
                            kk.read_by(m)
                        yield
                    if pend:
                        j, h0, per, n, pb, pv, e = pend
                        for i in range(h0, h0 + per):
                            m = mm(a.buf[HR * i:HR * i + HR, P * j:S], st["v", b].buf[:, j, HG * g + i, :],
                                   pv[:, i - h0, :], e, a.busy, st["v", b].mark, start=j == 0, stop=j == NI - 1,
                                   signal=i == h0 + per - 1)
                        pb.read_by(m)
                    pend = nxt
                if g == G - 1:
                    st["v", b].read_by(m)
                st["out", b, g] = (a, m, ot)

            def finish(b, g):
                a, m, ot = st["out", b, g]
                w = st["w"]
                yield from group_out(a, m, 8, ot, HG * g, pause=1 if g == G - 1 else 6)
                if g == G - 1:
                    for _ in range(2):
                        yield
                    yield from project_out(ot, [ot.done], w.buf[:, L_WO:L_WO + P], w.buf[:, L_BO:L_BO + P], y, y_at, b)

            items = [[(lambda b=b, g=g, f=f: f(b, g)) for f in (prepare, scores, attend, finish)]
                     for b in range(B) for g in range(G)]
            return (lambda: project_in(0)), [(lambda: rotate(0))], items

        def ffn3(l, b):
            st = {}

            def turn():
                h = hn.take()
                done = yield from normalise(tiles(y, b), h.buf, 1e-6, True, *y_at[b], h.busy)
                for _ in range(2):
                    yield
                m, st["h"] = turn_batch(h.buf, b, done, scale=vec[:, V_N3 + l:V_N3 + l + 1])
                h.read_by(m)
                yield

            def hidden():
                w = layers[l]
                h = st["hid"] = hid.take()
                for c in range(4):
                    s = wide.take()
                    mm(s.buf[:, 0:S], w.buf[:, L_WG + P * c:L_WG + P * c + P], hT[:, b, :], st["h"], s.busy)
                    m = mm(s.buf[:, S:2 * S], w.buf[:, L_WU + P * c:L_WU + P * c + P], hT[:, b, :], signal=True)
                    g = a_act(h.buf[:, c, :], s.buf[:, 0:S], ACT.Silu, m, h.busy)
                    h.done = v_tt(h.buf[:, c, :], s.buf[:, S:2 * S], h.buf[:, c, :], ALU.mult, g)
                    s.read_by(h.done)
                    yield
                hT_free[b] = [m]

            def down():
                w, h = layers[l], st["hid"]
                done = h.done
                a = acc.take()
                for i in range(NI):
                    for c in range(4):
                        m = mm(a.buf[:, P * i:P * i + P], h.buf[:, c, P * i:P * i + P],
                               w.buf[:, L_WD + P * c:L_WD + P * c + P], done, a.busy, start=c == 0, stop=c == 3,
                               signal=(i, c) == (NI - 1, 3))
                    yield
                h.read_by(m)
                dst = tiles(y, b)
                done = v_tt(dst, a.buf[:, :].rearrange("p (i d) -> p i d", i=NI), dst, ALU.add, m, *y_at[b])
                a.read_by(done)
                y_at[b] = [done]
                if b == B - 1:
                    w.read_by(m)
                    if l + 2 < NL:
                        layers[l + 2] = load_layer(l + 2)
                    elif l + 2 == NL:
                        e3 = layer_w.take()
                        experts3["w"] = e3.buf[:, 0:E8 * D]
                        experts3["mark"] = load("experts3", [(experts3["w"], io["expert_w"])], e3.busy)
                yield
            return [turn, hidden, down]

        for l in range(NL):
            project, rotate_item, items = self_items(l)
            every[-1] = [beside(every[-1][0], project)] + every[-1][1:]
            if l == 0:
                items[1][0] = beside(items[1][0], masks3)
            every += staged(f"l3_self{l}", [rotate_item] + items)
            every += staged(f"l3_cross{l}", cross_unit(4 + l, 8, y, y_at, "l3", False, True, False, 1e-6,
                                                       vec[:, V_N2 + l:V_N2 + l + 1], rms=True))
            every += [[idle]] + staged(f"l3_ffn{l}", [ffn3(l, b) for b in range(B)])

        def moe_first(b, st):
            h = hn.take()
            done = yield from normalise(tiles(y, b), h.buf, 1e-6, True, *y_at[b], h.busy)
            done = v_tt(h.buf[:, :, :], h.buf[:, :, :],
                        rows[:, R_NF:R_NF + P].unsqueeze(1).broadcast_to([P, NI, D]), ALU.mult, done, line=pool)
            dst = tiles(x, b)
            x_at[b] = [v_tt(dst, dst, h.buf[:, :, :], ALU.add, *x_at[b], line=pool)]
            st["hn"] = h
            yield

        def moe_turn(b, st):
            h = st["hn"]
            done = yield from normalise(tiles(x, b), h.buf, 1e-5, False, *x_at[b])
            yield
            m, st["h"] = turn_batch(h.buf, b, done)
            h.read_by(m)
            yield

        def moe_choose(b, st):
            s = bank()
            for i in range(NI):
                m = mm(s.buf[:, E8 * i:E8 * i + E8], hT[:, b, P * i:P * i + P], mats[:, M_ROUT:M_ROUT + E8], st["h"],
                       s.busy, signal=i == NI - 1)
            k = st["k"] = prob.take()
            W = NI * E8
            lg, pv, cand, hot, cf = (k.buf[:, W * n:W * n + W].rearrange("p (i e) -> p i e", e=E8) for n in range(5))
            mx = k.buf[:, 5 * W:5 * W + NI]
            s.read_by(v_tt(lg, s.buf[:, 0:W].rearrange("p (i e) -> p i e", e=E8),
                           rows[:, R_RB:R_RB + E8].unsqueeze(1).broadcast_to([P, NI, E8]), ALU.add, m, k.busy))
            yield
            softmax8(lg, NI, pv, mx)
            yield
            first_max(pv, NI, mx, cand, hot)
            coef = v_tt(cf, hot, mx.unsqueeze(2).broadcast_to([P, NI, E8]), ALU.mult)
            st["cf"] = cf
            yield
            yield
            s = bank()
            for i in range(NI):
                m = mm(s.buf[0:E8, P * i:P * i + P], cf[:, i, :], ident, coef, s.busy, signal=i == NI - 1, turn=True)
            st["cT"] = k.buf[0:E8, S:2 * S]
            st["cT_done"] = a_copy(st["cT"], s.buf[0:E8, 0:S], m)
            s.read_by(st["cT_done"])
            yield

        def moe_second(b, st):
            a = bank()
            for i in range(NI):
                m = mm(a.buf[:, P * i:P * i + P], st["cT"][:, P * i:P * i + P], expert_b[:, :], st["cT_done"], a.busy,
                       signal=i == NI - 1)
            dst = tiles(x, b)
            done = v_tt(dst, a.buf[:, 0:S].rearrange("p (i d) -> p i d", i=NI), dst, ALU.add, m, *x_at[b])
            a.read_by(done)
            yield
            for pair in range(NI // 2):
                sums = [[2 * pair + k, wide.take(), done] for k in range(2)]
                marks = []
                for half in range(2):
                    for i, s, _ in sums:
                        m = mm(s.buf[:, S * half:S * half + S], hT[:, b, P * i:P * i + P],
                               experts3["w"][:, S * half:S * half + S], experts3["mark"], st["h"], s.busy,
                               signal=True)
                    marks.append(m)
                for e in range(E8):
                    for last in sums:
                        i, s, before = last
                        xt = x[:, NI * b + i, :]
                        last[2] = done = v_stt(xt, s.buf[:, D * e:D * e + D], st["cf"][:, i, e:e + 1], xt, ALU.mult,
                                               ALU.add, marks[D * e // S], before, apart=True)
                for _, s, last in sums:
                    s.read_by(last)
                yield
            st["k"].read_by(done)
            hT_free[b] = [m]
            out_sem = pr.semaphore(f"out{b}")
            sync.wait(done)
            sync.todo.append(("do16", io["out"][b].rearrange("(i p) d -> p i d", p=P), tiles(x, b), out_sem))
            stores.append(out_sem)
            yield

        stores = []
        sts = [{} for _ in range(B)]
        every += staged("l3_moe", [[(lambda b=b, f=f: f(b, sts[b])) for f in (moe_first, moe_turn, moe_choose, moe_second)]
                                   for b in range(B)])
        pipeline(every)
        for sem in stores:
            sync.todo.append(("wait", sem, 16))

        block = ctx.enter_context(nc.Block())

        @block.sync
        def _(e):
            for entry in sync.todo:
                if entry[0] == "wait":
                    e.wait_ge(entry[1], entry[2])
                else:
                    e.dma_start(entry[1], entry[2]).then_inc(entry[3], 16)

        @block.tensor
        def _(e):
            pe.play(e)

        @block.vector
        def _(e):
            dve.play(e)

        @block.scalar
        def _(e):
            act.play(e)

        @block.gpsimd
        def _(e):
            pool.play(e)


def heads(w, dh):
    out = np.zeros((w.shape[0], 16, HR), w.dtype)
    for part in range(3):
        out[:, :, PART * part:PART * part + dh] = w.reshape(w.shape[0], 16, dh)
    return out.reshape(w.shape[0], 16 * HR)


def constants():
    c = np.zeros((P, CONST_W), np.float32)

    def put(name, v):
        a, w = CONST_COLS[name]
        c[:, a:a + w] = np.asarray(v).reshape(P, w) if np.ndim(v) > 1 else v

    r = np.arange(P)
    put("ident", np.eye(P))
    put("causal", np.where(r[None, :] > r[:, None], NEG, 0.0))
    put("cumul", (r[:, None] <= r[None, :]).astype(np.float32))
    inv = (1.0 / np.float32(10000.0) ** (np.arange(0, 8, 2, dtype=np.float32) / np.float32(8))).astype(np.float32)
    ang = (np.arange(S, dtype=np.float32)[:, None] * inv[None, :]).astype(np.float32)
    ang = np.concatenate([ang, ang], 1)
    sign = np.array([-1.0] * 4 + [1.0] * 4, np.float32)
    put("cos", np.cos(ang).reshape(NI, P, 8).transpose(1, 0, 2).reshape(P, -1))
    put("sin", (np.sin(ang) * sign).reshape(NI, P, 8).transpose(1, 0, 2).reshape(P, -1))
    row = r % HR
    put("kscale8", np.where(row < MROW, 8 ** -0.5, 1.0)[:, None])
    put("kscale4", np.where(row < MROW, 4 ** -0.5, 1.0)[:, None])
    low = row // PART == 1
    put("pick", np.stack([low, 1.0 - 2.0 * low], 1))
    put("position", np.arange(S).reshape(NI, P).T)
    put("iota", np.tile(np.arange(SC, dtype=np.float32), (P, 1)))
    put("rev", np.tile(np.arange(E8, 0, -1, dtype=np.float32), (P, 1)))
    put("minus_half", np.full((P, NI), -0.5, np.float32))
    return c


def position_rows():
    slopes = 2.0 ** (-8 + np.arange(16))
    k = np.zeros((HG, HR, G, SK), np.float32)
    for g in range(G):
        for i in range(HG):
            k[i, KROW, g] = -slopes[HG * g + i] * np.arange(SK)
            k[i, QROW, g] = slopes[HG * g + i]
    return k.reshape(P, G, SK)


def mask_words(m):
    out = np.zeros((m.shape[0], 4 * MASK_W), np.uint8)
    out[:, :SC] = m.view(np.uint8)
    return out.view(np.int32)


def layout(i):
    z = np.zeros
    f = np.float32
    unit_w, unit_b, unit_rows = z((8, P, U_BQ), f), z((P, 8, G), f), z((8, U_W - U_BQ), f)

    def unit(n, dh, wq, wk, wv, bq, bk, bv, wo, bo):
        unit_w[n, :, U_WK:U_WK + 512] = heads(wk, dh)
        unit_w[n, :, U_WQ:U_WQ + wq.shape[1]] = wq
        unit_w[n, :, U_WV:U_WV + wv.shape[1]] = wv
        if wo is not None:
            unit_w[n, :wo.shape[0], U_WO:U_WO + P] = wo
        kb = z((1, 16 * HR), f)
        if bq is not None:
            kb = heads(bk[None, :], dh)
            unit_rows[n, 0:bq.size] = bq
            unit_rows[n, P:P + bv.size] = bv
        kb = kb.reshape(G, HG, HR)
        kb[:, :, MROW:MROW + 2] = 1.0
        unit_b[:, n, :] = kb.reshape(G, P).T
        if bo is not None:
            unit_rows[n, 2 * P:] = bo

    unit(0, 8, i["L0_xattn_Wq"].T, i["L0_xattn_Wk"].T, i["L0_xattn_Wv"].T, i["L0_xattn_bq"], i["L0_xattn_bk"],
         i["L0_xattn_bv"], None, None)
    w, wb = i["L1_xattn_Wqkv"], i["L1_xattn_bqkv"]
    for u in range(2):
        c = slice(64 * u, 64 * u + 64)
        unit(1 + u, 4, w[:, :P][:, c], w[:, P:2 * P][:, c], w[:, 2 * P:][:, c], wb[:P][c], wb[P:2 * P][c],
             wb[2 * P:][c], i["L1_xattn_Wo"][c], i["L1_xattn_bo"])
    unit(3, 8, i["L2_xattn_Wq"].T, i["L2_xattn_Wk"].T, i["L2_xattn_Wv"].T, i["L2_xattn_bq"], i["L2_xattn_bk"],
         i["L2_xattn_bv"], i["L2_xattn_Wo"].T, i["L2_xattn_bo"])
    for l in range(NL):
        kv = i["L3_xattn_Wkv_c"][l]
        unit(4 + l, 8, i["L3_xattn_Wq_c"][l].T, kv[:P].T, kv[P:].T, None, None, None, i["L3_xattn_Wo_c"][l].T, None)

    layer_w, layer_rows = z((NL, P, L_BQKV), f), z((NL, L_W - L_BQKV), f)
    for l in range(NL):
        layer_w[l, :, L_QKV:L_QKV + 384] = i["L3_xattn_Wqkv"][l].T
        layer_w[l, :, L_WO:L_WO + P] = i["L3_xattn_Wo"][l].T
        layer_w[l, :, L_WG:L_WG + F0] = i["L3_xattn_Wg"][l].T
        layer_w[l, :, L_WU:L_WU + F0] = i["L3_xattn_Wu"][l].T
        layer_w[l, :, L_WD:L_WD + F0] = i["L3_xattn_Wd"][l].T.reshape(4, P, D).transpose(1, 0, 2).reshape(P, -1)
        layer_rows[l, 0:384] = i["L3_xattn_bqkv"][l]
        layer_rows[l, 384:] = i["L3_xattn_bo"][l]

    vecs = z((P, VEC_W), f)
    for at, name in ((V_N1, "L3_xattn_n1"), (V_N2, "L3_xattn_n2"), (V_N3, "L3_xattn_n3")):
        vecs[:, at:at + NL] = i[name].T
    for at, name in ((V_LNG, "L0_ffn_ln_g"), (V_LNB, "L0_ffn_ln_b"), (V_ATTB, "L0_ffn_attn_b")):
        vecs[:, at] = i[name]
    vecs[:, V_B1:V_B1 + 4 * E8] = i["L0_ffn_b1"].reshape(E8 * 4, P).T
    vecs[:, V_B2:V_B2 + E8] = i["L0_ffn_b2"].T
    rows = np.concatenate([i["L0_ffn_next_b"], i["L2_ffn_weight_scale"], i["L2_ffn_bias"], i["L3_xattn_nf"],
                           i["L3_ffn_router_b"]])
    mats = np.concatenate([i["L0_ffn_attn_w"], i["L0_ffn_next_w"], i["L1_ffn_gate_w"].T, i["L3_ffn_router_w"]], 1)
    ctxT = z((P, B, SK), f)
    ctxT[:, :, :SC] = i["ctx_1024"].transpose(2, 0, 1)
    return {
        "x": i["x"], "ctxT": ctxT, "mask": i["mask_BxSxS2_if1"],
        "attn_mask": mask_words(i["mask_SxS2_bk1"]), "pad_mask": mask_words(i["mask_BxS2_bk0"]),
        "seg": i["itok_BxS_0_255"].reshape(NT, P).T, "unit_w": unit_w, "unit_b": unit_b, "unit_rows": unit_rows,
        "layer_w": layer_w, "layer_rows": layer_rows, "vecs": vecs, "rows": rows, "mats": mats,
        "consts": constants(), "k_extra": position_rows(),
        "w1": i["L0_ffn_w1"].transpose(1, 0, 2),
        "w2": i["L0_ffn_w2"].reshape(E8, 4, P, D).transpose(2, 0, 1, 3),
        "gate1": i["L1_ffn_gate_proj_w"].transpose(2, 0, 1), "up1": i["L1_ffn_up_proj_w"].transpose(2, 0, 1),
        "down1": i["L1_ffn_down_proj_w"].transpose(2, 0, 1).reshape(2, P, E8, D).transpose(1, 2, 0, 3),
        "wq8": np.ascontiguousarray(i["L2_ffn_weight_q"].T).view(np.int32), "expert_w": i["L3_ffn_expert_w"].transpose(1, 0, 2).reshape(P, E8 * D),
        "expert_b": i["L3_ffn_expert_b"],
    }


def kernel(**inputs):
    import concourse.bacc as bacc
    from concourse.bass_utils import run_bass_kernel_spmd as run

    arrays = {f"in_{k}": np.ascontiguousarray(v)
              for k, v in layout({k: np.asarray(v) for k, v in inputs.items()}).items()}
    nc = bacc.Bacc("TRN2", target_bir_lowering=False, num_devices=1)
    io = {k[3:]: nc.dram_tensor(k, v.shape, mybir.dt.from_np(v.dtype), kind="ExternalInput").ap()
          for k, v in arrays.items()}
    io["out"] = nc.dram_tensor("out", (B, S, D), mybir.dt.float32, kind="ExternalOutput").ap()
    build(nc, io)
    return run(nc, [arrays], core_ids=[0]).results[0]["out"]
```
